# Optimizing a Trainium2 kernel written in Bass

```python
import numpy as np
import jax
import jax.numpy as jnp

def _softmax(x, axis=-1):
    return jax.nn.softmax(x, axis=axis)

def _gelu(x):
    return jax.nn.gelu(x, approximate=True)

def _silu(x):
    return jax.nn.silu(x)

def _sigmoid(x):
    return jax.nn.sigmoid(x)

def _layernorm(x, axis=-1, eps=1e-05):
    m = jnp.mean(x, axis=axis, keepdims=True)
    v = jnp.var(x, axis=axis, keepdims=True)
    return (x - m) / jnp.sqrt(v + eps)

def _scatter_add(tgt, idx, src, axis=0):
    return tgt.at[idx].add(src)

def _segment_sum(src, seg, n):
    return jax.ops.segment_sum(src, seg, n)
kernel_name = 'mk_cond_seq_d2_seqx_r4_d025d2'

def setup_inputs(seed: int=0):
    np.random.seed(seed)
    _w = jnp.asarray

    def _rec_inputs():
        import jax
        import jax.numpy as jnp
        _rk = jax.random.key(seed)
        x = -0.0005207 + 1.001 * jax.random.normal(jax.random.fold_in(_rk, 1), (32, 256, 256), jnp.float32)
        _lenS = 256 - jax.random.randint(jax.random.fold_in(_rk, 7), (32,), 0, max(1, 256 // 4) + 1, jnp.int32)
        _lenS2 = 256 - jax.random.randint(jax.random.fold_in(_rk, 8), (32,), 0, max(1, 256 // 4) + 1, jnp.int32)
        itok_B_34_63 = jax.random.randint(jax.random.fold_in(_rk, 12), (32,), 34, 64, jnp.int32)
        fside_Bx16xSxS_0 = -1.47943e-05 + 1.00017 * jax.random.normal(jax.random.fold_in(_rk, 13), (32, 16, 256, 256), jnp.float32)
        condB_safetyscore = -0.927215 + 0.920279 * jax.random.normal(jax.random.fold_in(_rk, 14), (32,), jnp.float32)
        _validS = jnp.arange(256)[None, :] < _lenS[:, None]
        _validS2 = jnp.arange(256)[None, :] < _lenS2[:, None]
        _causal = jnp.tril(jnp.ones((256, 256), dtype=bool))
        mask_Bx1xSxS_bk0 = jnp.logical_not(jnp.broadcast_to(_validS[:, None, None, :], (32, 1, 256, 256)))
        return (x, itok_B_34_63, fside_Bx16xSxS_0, condB_safetyscore, mask_Bx1xSxS_bk0)
    x, itok_B_34_63, fside_Bx16xSxS_0, condB_safetyscore, mask_Bx1xSxS_bk0 = _rec_inputs()

    def _L0_cond_setup():
        import jax, jax.numpy as jnp
        import numpy as np
        import math
        D_MODEL = 256
        N_HEAD = 16
        HEAD_DIM = D_MODEL // N_HEAD
        D_FF = 1024
        NUM_STEPS = 100.0
        RESCALE = 4000.0
        EPS = 1e-05

        def _sin_emb(t):
            half = D_MODEL // 2
            x = t.astype(jnp.float32) / NUM_STEPS * RESCALE
            freqs = jnp.exp(jnp.arange(half, dtype=jnp.float32) * (-math.log(10000.0) / (half - 1)))
            e = x[:, None] * freqs[None, :]
            return jnp.concatenate([jnp.sin(e), jnp.cos(e)], axis=-1)

        def _ln(x):
            m = jnp.mean(x, axis=-1, keepdims=True)
            v = jnp.var(x, axis=-1, keepdims=True)
            return (x - m) / jnp.sqrt(v + EPS)

        def _gelu2(x):
            return x * jax.nn.sigmoid(1.702 * x)
        key = jax.random.key(seed)
        ks = jax.random.split(key, 24)
        B, S, D, F = (4, 128, D_MODEL, D_FF)
        std = 0.02
        inp = {'src': jax.random.normal(ks[0], (B, S, D), dtype=jnp.float32), 'src_mask': jax.random.randint(ks[1], (B, 1, S, S), 0, 2).astype(bool), 'timestep': jax.random.randint(ks[2], (B,), 0, 100, dtype=jnp.int32), 'attention_bias': jax.random.normal(ks[3], (B, N_HEAD, S, S), dtype=jnp.float32), 'W_ada': jax.random.normal(ks[4], (D, 2 * D), dtype=jnp.float32) * std, 'b_ada': jnp.zeros((2 * D,), dtype=jnp.float32), 'Wq': jax.random.normal(ks[5], (D, D), dtype=jnp.float32) * std, 'bq': jnp.zeros((D,), dtype=jnp.float32), 'Wk': jax.random.normal(ks[6], (D, D), dtype=jnp.float32) * std, 'bk': jnp.zeros((D,), dtype=jnp.float32), 'Wv': jax.random.normal(ks[7], (D, D), dtype=jnp.float32) * std, 'bv': jnp.zeros((D,), dtype=jnp.float32), 'Wo': jax.random.normal(ks[8], (D, D), dtype=jnp.float32) * std, 'bo': jnp.zeros((D,), dtype=jnp.float32), 'W1': jax.random.normal(ks[9], (D, F), dtype=jnp.float32) * std, 'b1': jnp.zeros((F,), dtype=jnp.float32), 'W2': jax.random.normal(ks[10], (F, D), dtype=jnp.float32) * std, 'b2': jnp.zeros((D,), dtype=jnp.float32), 'g2': jnp.ones((D,), dtype=jnp.float32), 'beta2': jnp.zeros((D,), dtype=jnp.float32)}
        return inp
    _L0_cond_all = _L0_cond_setup()
    _L0_cond_in = {k: v for k, v in _L0_cond_all.items() if k in ('W_ada', 'b_ada', 'Wq', 'bq', 'Wk', 'bk', 'Wv', 'bv', 'Wo', 'bo', 'W1', 'b1', 'W2', 'b2', 'g2', 'beta2')}
    del _L0_cond_all

    def _L1_cond_setup():
        import jax, jax.numpy as jnp
        import numpy as np
        TEMPERATURE = 1.0
        ACT_THRESHOLD = 0.1
        MAX_ACT = 1.0
        SAFETY_KNOB = 1.0
        EPS = 1e-08

        def gram_schmidt(X):
            r = X.shape[1]
            Q = X
            for i in range(r):
                q = Q[:, i]
                q = q / (jnp.linalg.norm(q) + EPS)
                Q = Q.at[:, i].set(q)
                coeffs = q @ Q[:, i + 1:]
                Q = Q.at[:, i + 1:].add(-jnp.outer(q, coeffs))
            return Q
        key = jax.random.key(seed)
        ks = jax.random.split(key, 8)
        B, S, D, R = (8, 1024, 256, 32)
        init_std = 0.02
        return {'hidden_states': jax.random.normal(ks[0], (B, S, D), jnp.float32), 'safety_score': jax.random.normal(ks[1], (B,), jnp.float32), 'U': jax.random.normal(ks[2], (D, R), jnp.float32) * init_std, 'V': jax.random.normal(ks[3], (D, R), jnp.float32) * init_std, 'safety_bias': jnp.zeros((D,), jnp.float32), 'gate_w1': jax.random.normal(ks[4], (D // 4, D), jnp.float32) * (1.0 / np.sqrt(D)), 'gate_b1': jnp.zeros((D // 4,), jnp.float32), 'gate_w2': jax.random.normal(ks[5], (1, D // 4), jnp.float32) * (1.0 / np.sqrt(D // 4)), 'gate_b2': jnp.zeros((1,), jnp.float32), 'resp_w': jax.random.normal(ks[6], (D, R), jnp.float32) * (1.0 / np.sqrt(R)), 'resp_b': jnp.zeros((D,), jnp.float32)}
    _L1_cond_all = _L1_cond_setup()
    _L1_cond_in = {k: v for k, v in _L1_cond_all.items() if k in ('U', 'V', 'safety_bias', 'gate_w1', 'gate_b1', 'gate_w2', 'gate_b2', 'resp_w', 'resp_b')}
    del _L1_cond_all
    return {'x': x, 'itok_B_34_63': itok_B_34_63, 'fside_Bx16xSxS_0': fside_Bx16xSxS_0, 'condB_safetyscore': condB_safetyscore, 'mask_Bx1xSxS_bk0': mask_Bx1xSxS_bk0, 'L0_cond_W_ada': _L0_cond_in['W_ada'], 'L0_cond_b_ada': _L0_cond_in['b_ada'], 'L0_cond_Wq': _L0_cond_in['Wq'], 'L0_cond_bq': _L0_cond_in['bq'], 'L0_cond_Wk': _L0_cond_in['Wk'], 'L0_cond_bk': _L0_cond_in['bk'], 'L0_cond_Wv': _L0_cond_in['Wv'], 'L0_cond_bv': _L0_cond_in['bv'], 'L0_cond_Wo': _L0_cond_in['Wo'], 'L0_cond_bo': _L0_cond_in['bo'], 'L0_cond_W1': _L0_cond_in['W1'], 'L0_cond_b1': _L0_cond_in['b1'], 'L0_cond_W2': _L0_cond_in['W2'], 'L0_cond_b2': _L0_cond_in['b2'], 'L0_cond_g2': _L0_cond_in['g2'], 'L0_cond_beta2': _L0_cond_in['beta2'], 'L1_cond_U': _L1_cond_in['U'], 'L1_cond_V': _L1_cond_in['V'], 'L1_cond_safety_bias': _L1_cond_in['safety_bias'], 'L1_cond_gate_w1': _L1_cond_in['gate_w1'], 'L1_cond_gate_b1': _L1_cond_in['gate_b1'], 'L1_cond_gate_w2': _L1_cond_in['gate_w2'], 'L1_cond_gate_b2': _L1_cond_in['gate_b2'], 'L1_cond_resp_w': _L1_cond_in['resp_w'], 'L1_cond_resp_b': _L1_cond_in['resp_b']}

def reference(x, itok_B_34_63, fside_Bx16xSxS_0, condB_safetyscore, mask_Bx1xSxS_bk0, L0_cond_W_ada, L0_cond_b_ada, L0_cond_Wq, L0_cond_bq, L0_cond_Wk, L0_cond_bk, L0_cond_Wv, L0_cond_bv, L0_cond_Wo, L0_cond_bo, L0_cond_W1, L0_cond_b1, L0_cond_W2, L0_cond_b2, L0_cond_g2, L0_cond_beta2, L1_cond_U, L1_cond_V, L1_cond_safety_bias, L1_cond_gate_w1, L1_cond_gate_b1, L1_cond_gate_w2, L1_cond_gate_b2, L1_cond_resp_w, L1_cond_resp_b):
    import jax
    import jax.numpy as jnp

    def _L0_cond_ref(src, src_mask, timestep, attention_bias, W_ada, b_ada, Wq, bq, Wk, bk, Wv, bv, Wo, bo, W1, b1, W2, b2, g2, beta2):
        import jax, jax.numpy as jnp
        import numpy as np
        import math
        D_MODEL = 256
        N_HEAD = 16
        HEAD_DIM = D_MODEL // N_HEAD
        D_FF = 1024
        NUM_STEPS = 100.0
        RESCALE = 4000.0
        EPS = 1e-05

        def _sin_emb(t):
            half = D_MODEL // 2
            x = t.astype(jnp.float32) / NUM_STEPS * RESCALE
            freqs = jnp.exp(jnp.arange(half, dtype=jnp.float32) * (-math.log(10000.0) / (half - 1)))
            e = x[:, None] * freqs[None, :]
            return jnp.concatenate([jnp.sin(e), jnp.cos(e)], axis=-1)

        def _ln(x):
            m = jnp.mean(x, axis=-1, keepdims=True)
            v = jnp.var(x, axis=-1, keepdims=True)
            return (x - m) / jnp.sqrt(v + EPS)

        def _gelu2(x):
            return x * jax.nn.sigmoid(1.702 * x)
        B, S, D = src.shape
        emb = jax.nn.silu(_sin_emb(timestep)) @ W_ada + b_ada
        scale, shift = jnp.split(emb[:, None, :], 2, axis=-1)
        x = _ln(src) * (1.0 + scale) + shift
        q = (x @ Wq + bq).reshape(B, S, N_HEAD, HEAD_DIM).transpose(0, 2, 1, 3)
        k = (x @ Wk + bk).reshape(B, S, N_HEAD, HEAD_DIM).transpose(0, 2, 1, 3)
        v = (x @ Wv + bv).reshape(B, S, N_HEAD, HEAD_DIM).transpose(0, 2, 1, 3)
        scores = jnp.einsum('bhqd,bhkd->bhqk', q / math.sqrt(HEAD_DIM), k)
        scores = scores + attention_bias
        scores = jnp.where(src_mask, -jnp.inf, scores.astype(jnp.float32))
        probs = jax.nn.softmax(scores, axis=-1).astype(v.dtype)
        ctx = jnp.einsum('bhqk,bhkd->bhqd', probs, v)
        ctx = ctx.transpose(0, 2, 1, 3).reshape(B, S, D)
        x = x + (ctx @ Wo + bo)
        h = _ln(x) * g2 + beta2
        ff = _gelu2(h @ W1 + b1) @ W2 + b2
        return x + ff

    def _L1_cond_ref(hidden_states, safety_score, U, V, safety_bias, gate_w1, gate_b1, gate_w2, gate_b2, resp_w, resp_b):
        import jax, jax.numpy as jnp
        import numpy as np
        TEMPERATURE = 1.0
        ACT_THRESHOLD = 0.1
        MAX_ACT = 1.0
        SAFETY_KNOB = 1.0
        EPS = 1e-08

        def gram_schmidt(X):
            r = X.shape[1]
            Q = X
            for i in range(r):
                q = Q[:, i]
                q = q / (jnp.linalg.norm(q) + EPS)
                Q = Q.at[:, i].set(q)
                coeffs = q @ Q[:, i + 1:]
                Q = Q.at[:, i + 1:].add(-jnp.outer(q, coeffs))
            return Q
        R = resp_w.shape[1]
        U_o = gram_schmidt(U)
        V_o = gram_schmidt(V)
        basis = U_o @ V_o.T
        pooled = hidden_states.mean(axis=1)
        h1 = jax.nn.relu(pooled @ gate_w1.T + gate_b1)
        base_act = jax.nn.sigmoid(h1 @ gate_w2.T + gate_b2)
        mod = jax.nn.sigmoid(safety_score[:, None] / TEMPERATURE)
        knob = jnp.clip(jnp.asarray(SAFETY_KNOB, hidden_states.dtype), ACT_THRESHOLD, MAX_ACT)
        strength = (base_act * mod * knob)[:, None, :]
        proj = hidden_states @ basis
        feats = proj @ basis.T[:, :R]
        response = feats @ resp_w.T + resp_b + safety_bias
        return hidden_states + strength * response
    x = _L0_cond_ref(x, mask_Bx1xSxS_bk0, itok_B_34_63, fside_Bx16xSxS_0, L0_cond_W_ada, L0_cond_b_ada, L0_cond_Wq, L0_cond_bq, L0_cond_Wk, L0_cond_bk, L0_cond_Wv, L0_cond_bv, L0_cond_Wo, L0_cond_bo, L0_cond_W1, L0_cond_b1, L0_cond_W2, L0_cond_b2, L0_cond_g2, L0_cond_beta2)
    x = _L1_cond_ref(x, condB_safetyscore, L1_cond_U, L1_cond_V, L1_cond_safety_bias, L1_cond_gate_w1, L1_cond_gate_b1, L1_cond_gate_w2, L1_cond_gate_b2, L1_cond_resp_w, L1_cond_resp_b)
    return x

_drawn_inputs = setup_inputs


def setup_inputs(seed=0):
    import zlib

    import numpy as np

    out = dict(_drawn_inputs(seed))
    spreads = {'L0_cond_b_ada': (0.0, 0.1),
     'L0_cond_bq': (0.0, 0.8),
     'L0_cond_bk': (0.0, 0.8),
     'L0_cond_bv': (0.0, 0.27),
     'L0_cond_bo': (0.0, 0.1),
     'L0_cond_b1': (0.0, 0.1),
     'L0_cond_b2': (0.0, 0.1),
     'L0_cond_g2': (1.0, 0.6),
     'L0_cond_beta2': (0.0, 0.788),
     'L1_cond_safety_bias': (0.0, 0.471),
     'L1_cond_gate_b1': (0.0, 0.8),
     'L1_cond_resp_b': (0.0, 0.421)}
    factors = {'fside_Bx16xSxS_0': 6.691,
     'L0_cond_Wq': 8.0,
     'L0_cond_Wk': 8.0,
     'L0_cond_Wv': 2.895,
     'L1_cond_V': 8.0,
     'L1_cond_gate_w1': 8.0,
     'L1_cond_gate_w2': 8.0}
    for name, (base, spread) in spreads.items():
        noise = np.random.default_rng([zlib.crc32(name.encode()), seed]).standard_normal(out[name].shape)
        drawn = base * np.exp(spread * noise) if base else spread * noise
        out[name] = jnp.asarray(drawn.astype(out[name].dtype))
    for name, factor in factors.items():
        out[name] = (out[name] * factor).astype(out[name].dtype)
    return out
```

```python
from contextlib import ExitStack

import numpy as np

import concourse.bass as bass
from concourse import mybir

F32 = mybir.dt.float32
BF16 = mybir.dt.bfloat16
I32 = mybir.dt.int32
U8 = mybir.dt.uint8
ALU = mybir.AluOpType
ACT = mybir.ActivationFunctionType

P = 128
B, S, D = 32, 256, 256
H, HD = 16, 16
F = 1024
R = 32
GW = 64
QT = S // P
DC = D // P
FC = F // P
HG = 4
NG = H // HG
CH = 8
RING = 4
VW = 32
LN_EPS = 1e-5
GS_EPS = 1e-8
SPLIT = [(0, 0), (0, 1), (0, 2), (1, 0), (1, 1), (2, 0)]
NS = len(SPLIT)
KQ = NS * HD
GELU_A = 1.702
TWO_PI = 2.0 * np.pi
C1 = 6.28125
C2 = float(np.float32(np.round((TWO_PI - C1) * 2.0**21) / 2.0**21))
C3 = float(np.float32(TWO_PI - C1 - C2))
MASKED = -1.0e30
ROW_MAX_NEG = 1.0e29
MAGIC = 1.5 * 2.0**23
PI_IN = 3.1415925


class Batch:

    def __init__(self, off, i=None):
        self.par = off % 2
        self.half = off // 2 if i is None else i + off // 2
        self.n = off if i is None else 2 * i + off
        self.off, self.i = off, i

    def plus(self, k):
        return Batch(self.off + k, self.i)


def behind(b, n, h, k):
    if h >= k:
        return (b, h - k) if n is None or n < B else None
    return (b.plus(-1), h - k + H) if n is None or n >= 1 else None


def run_batches(eng, first, loop_from, loop_to, last, body):
    for b in range(first, loop_from):
        body(Batch(b), b)
    with eng.Fori(0, (loop_to - loop_from) // 2) as i:
        for off in range(2):
            body(Batch(loop_from + off, i), None)
    for b in range(loop_to, last):
        body(Batch(b), b)


def attention_block_kernel(nc, x, itok, fside, score, mask, W_ada, b_ada, Wq, bq, Wk, bk, Wv, bv, Wo, bo,
                           W1, b1, W2, b2, g2, beta2, U, V, safety_bias, gate_w1T, gate_b1, gate_w2T, gate_b2,
                           resp_wT, resp_b, freqs, out):
    with ExitStack() as ctx:
        def sb(name, shape, dt=F32):
            return ctx.enter_context(nc.sbuf_tensor(name, shape, dt))

        def sem(name):
            return ctx.enter_context(nc.semaphore(name))

        parts_d = nc.dram_tensor("parts_d", (2, 2, 3 * DC, P, S), BF16, kind="Internal").ap()
        x2_d = nc.dram_tensor("x2_d", (B, S, D), F32, kind="Internal").ap()

        wq = sb("wq", [P, DC, D]); wk = sb("wk", [P, DC, D]); wv = sb("wv", [P, DC, D]); wo = sb("wo", [P, DC, D])
        w1 = sb("w1", [P, DC, F]); w2 = sb("w2", [P, FC, D]); wada = sb("wada", [P, 2, 2 * D])
        bqk = sb("bqk", [P, 2, DC]); bada = sb("bada", [P, 2 * DC]); b1c = sb("b1c", [P, FC]); b1t = sb("b1t", [P, FC])
        g2c = sb("g2c", [P, DC]); be2c = sb("be2c", [P, DC])
        bvb = sb("bvb", [P, D]); bob = sb("bob", [P, D]); b2b = sb("b2b", [P, D]); cb = sb("cb", [P, D]); cb2 = sb("cb2", [P, D])
        ident = sb("ident", [P, P]); later = sb("later", [P, R, R]); expo = sb("expo", [P, 2, 2])
        frq = sb("frq", [P, 1]); tti = sb("tti", [P, B], I32); ttf = sb("ttf", [P, B]); ang = sb("ang", [P, B])
        turns = sb("turns", [P, 2, B]); red = sb("red", [P, 2, B]); red2 = sb("red2", [P, 2, B])
        sc = sb("sc", [P, 2, B]); sct = sb("sct", [P, 2, B]); emb = sb("emb", [P, 2, B])
        adaS = sb("adaS", [P, DC, B]); adaB = sb("adaB", [P, DC, B])
        scr = sb("scr", [P, B]); modh = sb("modh", [P, B]); modt = sb("modt", [P, B])
        gw1 = sb("gw1", [P, DC, GW]); gb1 = sb("gb1", [GW, 1]); gw2 = sb("gw2", [GW, 1]); gb2 = sb("gb2", [P, 1]); gb2h = sb("gb2h", [P, 1])
        uv = sb("uv", [P, 2, DC, R]); ucol = sb("ucol", [P, 2, DC]); gsb = sb("gsb", [P, 2, R]); gii = sb("gii", [P, 2])
        nrm = sb("nrm", [P, 2]); nrme = sb("nrme", [P, 2]); rnrm = sb("rnrm", [P, 2]); qneg = sb("qneg", [P, 2, DC]); coef = sb("coef", [P, 2, R])
        respT = sb("respT", [R, D]); gram = sb("gram", [R, R]); t1 = sb("t1", [R, D]); t2 = sb("t2", [R, D]); uoT = sb("uoT", [R, D]); resp_m = sb("resp_m", [P, DC, D])

        ring = sb("ring", [P, RING, QT, CH, S])
        pT = sb("pT", [P, 2 * HG, QT, S])
        stack = sb("stack", [KQ, 2, 2, H, S], BF16)
        parts = sb("parts", [P, 2, 3, DC, S], BF16)
        xt = sb("xt", [P, 2, QT, D]); st6 = sb("st6", [P, QT, 6]); mv = sb("mv", [P, QT, 2])
        vpe = sb("vpe", [P, QT]); rstd = sb("rstd", [P, QT]); mneg = sb("mneg", [P, QT]); nmr = sb("nmr", [P, QT])
        xn = sb("xn", [P, QT, D]); xT = sb("xT", [P, DC, S]); xres = sb("xres", [P, 2, QT, D])
        vt = sb("vt", [P, 2, QT, H, VW])
        mk = sb("mk", [P, 2, QT, S], U8); maskv = sb("maskv", [P, QT, S])
        nmax = sb("nmax", [P, 2, H, QT])
        pv_sb = sb("pv_sb", [P, NG, S]); rec = sb("rec", [P, QT, H]); ctxn = sb("ctxn", [P, QT, D]); ctxT = sb("ctxT", [P, DC, S]); x2s = sb("x2s", [P, 2, QT, D])

        big = ring[:].rearrange("p r q c s -> p (r q c s)")
        place = [0]

        def carve(*shape):
            n = int(np.prod(shape))
            a = big[:, place[0]:place[0] + n]
            place[0] += n
            if len(shape) == 2:
                return a.rearrange("p (a b) -> p a b", a=shape[0])
            return a.rearrange("p (a b c) -> p a b c", a=shape[0], b=shape[1])

        y2 = carve(2, QT, D)
        yb = carve(2, QT, D)
        yn = carve(QT, D)
        hT = carve(2, DC, S)
        th = carve(4, 2, S)
        up = carve(4, 2, S)
        gT = carve(2, FC, S)
        hid = carve(2, QT, D)
        hidT = carve(DC, S)
        rsp = carve(QT, D)
        fin = carve(2, QT, D)
        pooled = sb("pooled", [P, DC]); h1 = sb("h1", [GW, 1]); gth = sb("gth", [P, 1]); strg = sb("strg", [P, 2])
        st6b = sb("st6b", [P, QT, 6]); mvb = sb("mvb", [P, 2, QT, 2]); vpeb = sb("vpeb", [P, QT]); rstdb = sb("rstdb", [P, QT]); mnegb = sb("mnegb", [P, QT]); nmrb = sb("nmrb", [P, QT])

        bank = [ctx.enter_context(nc.psum_tensor(f"bank{i}", [P, 512], F32)) for i in range(8)]

        def tiles2(i):
            return bank[i][:].rearrange("p (a s) -> p a s", a=2)

        qk_ps = [tiles2(0), tiles2(1)]
        tp_ps = [tiles2(2), tiles2(3)]
        pv_ps = bank[4][:, 0:S]
        gs_ps = bank[7][:, 0:2 * R]
        prep_a, prep_b, tail_ps = tiles2(5), tiles2(6), tiles2(7)

        s_load = sem("s_load"); s_const = sem("s_const"); s_dve0 = sem("s_dve0"); s_red = sem("s_red"); s_sin = sem("s_sin"); s_emb = sem("s_emb")
        s_act0 = sem("s_act0"); s_adaps = sem("s_adaps"); s_setup = sem("s_setup")
        s_gcol = sem("s_gcol"); s_gram = sem("s_gram"); s_gii = sem("s_gii"); s_gnrm = sem("s_gnrm"); s_gp = sem("s_gp"); s_gself = sem("s_gself")
        s_rm = sem("s_rm"); s_rmc = sem("s_rmc")
        s_x = [sem("s_x0"), sem("s_x1")]; s_mk = [sem("s_mk0"), sem("s_mk1")]; s_bias = [sem(f"s_bias{i}") for i in range(RING)]
        s_wq_d = sem("s_partq_out"); s_wk_d = sem("s_partk_out"); s_stq = [sem("s_stackq0"), sem("s_stackq1")]; s_stk = [sem("s_stackk0"), sem("s_stackk1")]
        s_x2st = [sem("s_x2st0"), sem("s_x2st1")]
        s_maskv = sem("s_maskv"); s_masked = sem("s_masked"); s_pool = sem("s_pool"); s_rstd = sem("s_rstd")
        s_stats6 = sem("s_stats6"); s_stats = sem("s_stats"); s_reduced = sem("s_reduced"); s_ptd = sem("s_ptd"); s_xT = sem("s_xT")
        s_r1 = sem("s_r1"); s_p3 = sem("s_p3"); s_v = sem("s_v"); s_xres = sem("s_xres"); s_rec = sem("s_rec"); s_ctxn = sem("s_ctxn"); s_x2 = sem("s_x2")
        s_xn = sem("s_xn"); s_exp = sem("s_exp"); s_pta = sem("s_pta"); s_p1 = sem("s_p1"); s_p2 = sem("s_p2"); s_pvc = sem("s_pvc"); s_ctxT = sem("s_ctxT")
        s_qk = sem("s_qk"); s_tp = sem("s_tp"); s_pv = sem("s_pv"); s_xtp = sem("s_xtp"); s_qp = sem("s_qp"); s_kp = sem("s_kp"); s_vp = sem("s_vp"); s_xb = sem("s_xb")
        s_cn = sem("s_cn"); s_cT = sem("s_cT"); s_o = sem("s_o")
        s_y = [sem("s_y0"), sem("s_y1")]; s_out = [sem("s_out0"), sem("s_out1")]
        s2_six = sem("s2_six"); s2_stats = sem("s2_stats"); s2_pool = sem("s2_pool"); s2_rstd = sem("s2_rstd"); s2_yb = sem("s2_yb"); s2_yn = sem("s2_yn")
        s2_yt = sem("s2_yt"); s2_hT = sem("s2_hT"); s2_up = sem("s2_up"); s2_th = sem("s2_th"); s2_u = sem("s2_u"); s2_g = sem("s2_g"); s2_dn = sem("s2_dn")
        s2_hid = sem("s2_hid"); s2_hidp = sem("s2_hidp"); s2_hidT = sem("s2_hidT"); s2_r = sem("s2_r"); s2_h1p = sem("s2_h1p"); s2_h1 = sem("s2_h1"); s2_zp = sem("s2_zp")
        s2_z = sem("s2_z"); s2_str = sem("s2_str"); s2_rs = sem("s2_rs"); s2_fin = sem("s2_fin")

        loads = [
            (xt[:, 0], x[0].rearrange("(t p) d -> p t d", p=P), s_x[0]), (xt[:, 1], x[1].rearrange("(t p) d -> p t d", p=P), s_x[1]),
            (frq[:], freqs.rearrange("(p a) -> p a", a=1)), (tti[:], itok.partition_broadcast(P)),
            (wada[:], W_ada.rearrange("(c p) n -> p c n", p=P)), (bada[:], b_ada),
            (uv[:, 0], U.rearrange("(c p) r -> p c r", p=P)), (uv[:, 1], V.rearrange("(c p) r -> p c r", p=P)),
            (wq[:], Wq.rearrange("(c p) n -> p c n", p=P)), (wk[:], Wk.rearrange("(c p) n -> p c n", p=P)),
            (wv[:], Wv.rearrange("(c p) n -> p c n", p=P)), (wo[:], Wo.rearrange("(c p) n -> p c n", p=P)),
            (bqk[:, 0], bq), (bqk[:, 1], bk), (bvb[:], bv.partition_broadcast(P)), (bob[:], bo.partition_broadcast(P)),
            (w1[:], W1.rearrange("(c p) n -> p c n", p=P)), (w2[:], W2.rearrange("(c p) n -> p c n", p=P)),
            (b1c[:], b1), (g2c[:], g2), (be2c[:], beta2), (b2b[:], b2.partition_broadcast(P)),
            (cb[:], resp_b.partition_broadcast(P)), (cb2[:], safety_bias.partition_broadcast(P)),
            (scr[:], score.partition_broadcast(P)), (gw1[:], gate_w1T.rearrange("(c p) n -> p c n", p=P)),
            (gb1[:], gate_b1.rearrange("(p a) -> p a", a=1)), (gw2[:], gate_w2T), (gb2[:], gate_b2.partition_broadcast(P)),
            (respT[:], resp_wT),
        ]
        n_loads = sum(1 for a in loads if len(a) == 2)

        def x_view(b):
            return x[bass.ds(b.n, 1)].rearrange("a (t p) d -> p (a t) d", p=P)

        def bias_chunk(b, c, qt):
            return fside[bass.ds(b.n, 1), c * CH:(c + 1) * CH, qt * P:(qt + 1) * P, :].rearrange("a h p k -> p (a h) k")

        def free_pT(eng, b, h):
            g = h // HG
            if b.i is not None or NG * b.off + g >= 2:
                eng.wait_ge(s_pv, NG * b.n + g - 1)

        block = ctx.enter_context(nc.Block())

        @block.sync
        def _(sp):
            for dst, src, *own in loads:
                sp.dma_start(dst, src).then_inc(own[0] if own else s_load, 16)

            def load_mask(b):
                sp.dma_start(mk[:, b.par], mask[bass.ds(b.n, 1)].rearrange("a c (t p) k -> p (a c t) k", p=P)).then_inc(s_mk[b.par], 16)

            def load_bias(b, c):
                slot = 2 * b.par + c
                for qt in range(QT):
                    sp.dma_start(ring[:, slot, qt], bias_chunk(b, c, qt)).then_inc(s_bias[slot], 16)

            def restack(b):
                for t, (s_out_d, s_in) in enumerate(((s_wq_d, s_stq), (s_wk_d, s_stk))):
                    sp.wait_ge(s_p3, 2 * b.n + t + 1)
                    sp.dma_start(parts_d[b.par, t].rearrange("a p s -> p a s"),
                                 parts[:, t].rearrange("p a c s -> p (a c) s")).then_inc(s_out_d, 16)
                for t, (s_out_d, s_in) in enumerate(((s_wq_d, s_stq), (s_wk_d, s_stk))):
                    sp.wait_ge(s_out_d, 16 * b.n + 16)
                    for i, pair in enumerate(SPLIT):
                        src = parts_d[b.par, t, DC * pair[t]:DC * pair[t] + DC].rearrange("c (j d) s -> d (c j) s", d=HD)
                        sp.dma_start(stack[HD * i:HD * i + HD, b.par, t], src).then_inc(s_in[b.par], 16)

            load_mask(Batch(0))
            load_mask(Batch(1))
            load_bias(Batch(0), 0)
            load_bias(Batch(0), 1)
            restack(Batch(0))
            load_bias(Batch(1), 0)

            def store_x2(b):
                sp.wait_ge(s_x2, b.n + 1)
                sp.dma_start(x2_d[bass.ds(b.n, 1)].rearrange("a (t p) d -> p (a t) d", p=P), x2s[:, b.par]).then_inc(s_x2st[b.par], 16)

            def body(b, n):
                if n is None or n + 2 < B:
                    sp.wait_ge(s_xn, b.n + 1)
                    sp.dma_start(xt[:, b.par], x_view(b.plus(2))).then_inc(s_x[b.par], 16)
                if n is None or n + 1 < B:
                    if n is None or n >= 1:
                        sp.wait_ge(s_tp, H * b.n)
                    load_bias(b.plus(1), 1)
                if n is None or n + 2 < B:
                    sp.wait_ge(s_maskv, b.n + 1)
                    load_mask(b.plus(2))
                if n is None or n + 1 < B:
                    restack(b.plus(1))
                if n is None or n + 2 < B:
                    sp.wait_ge(s_tp, H * b.n + CH)
                    load_bias(b.plus(2), 0)
                if n is None or n >= 1:
                    store_x2(b.plus(-1))

            run_batches(sp, 0, 3, B - 3, B, body)
            store_x2(Batch(B - 1))

            def load_y(b):
                sp.wait_ge(s_x2st[b.par], 16 * b.half + 16)
                sp.dma_start(y2[:, b.par], x2_d[bass.ds(b.n, 1)].rearrange("a (t p) d -> p (a t) d", p=P)).then_inc(s_y[b.par], 16)

            def store_out(b):
                sp.wait_ge(s2_fin, b.n + 1)
                sp.dma_start(out[bass.ds(b.n, 1)].rearrange("a (t p) d -> p (a t) d", p=P), fin[:, b.par]).then_inc(s_out[b.par], 16)

            sp.wait_ge(s_tp, H * B)
            load_y(Batch(0))
            load_y(Batch(1))

            def body2(b, n):
                if n is None or n + 2 < B:
                    sp.wait_ge(s2_yn, b.n + 1)
                    sp.wait_ge(s2_yb, b.n + 1)
                    load_y(b.plus(2))
                if n is None or n >= 1:
                    store_out(b.plus(-1))

            run_batches(sp, 0, 3, B - 3, B, body2)
            store_out(Batch(B - 1))
            for par in range(2):
                sp.wait_ge(s_out[par], 16 * B // 2)

        @block.gpsimd
        def _(pool):
            nc.gpsimd.memset(ident[:], 0.0)
            nc.gpsimd.memset(later[:], 1.0)
            nc.gpsimd.memset(expo[:, 0], -0.5)
            nc.gpsimd.memset(expo[:, 1], 0.5).then_inc(s_gp, 1)
            pool.wait_ge(s_gp, 1)
            nc.gpsimd.affine_select(out=ident[:], in_=ident[:], compare_op=ALU.not_equal, fill=1.0, base=0,
                                    pattern=[[-1, P]], channel_multiplier=1)
            nc.gpsimd.affine_select(out=later[:], in_=later[:], compare_op=ALU.is_gt, fill=0.0, base=0,
                                    pattern=[[-1, R], [1, R]], channel_multiplier=0).then_inc(s_const, 1)
            pool.wait_ge(s_const, 1)

            def gs_norm(i):
                pool.wait_ge(s_gii, i + 1)
                nc.gpsimd.tensor_tensor(nrm[:], gii[:], expo[:, 1], ALU.pow).then_inc(s_gp, 1)
                pool.wait_ge(s_gp, i + 2)
                pool.nop(nofuse=True)
                nc.gpsimd.tensor_scalar(nrme[:], nrm[:], GS_EPS, 1.0, ALU.add, ALU.mult).then_inc(s_gnrm, 1)

            def inv_std(b):
                pool.wait_ge(s_stats, b.n + 1)
                pool.nop(nofuse=True)
                nc.gpsimd.tensor_scalar(vpe[:], mv[:, :, 1], LN_EPS, 1.0, ALU.add, ALU.mult)
                nc.gpsimd.tensor_scalar(mneg[:], mv[:, :, 0], -1.0, 1.0, ALU.mult, ALU.mult).then_inc(s_pool, 1)
                pool.wait_ge(s_pool, 2 * b.n + 1)
                if b.i is not None or b.off >= 1:
                    pool.wait_ge(s_xn, b.n)
                nc.gpsimd.tensor_tensor(rstd[:], vpe[:], expo[:, 0], ALU.pow).then_inc(s_pool, 1)
                pool.wait_ge(s_pool, 2 * b.n + 2)
                nc.gpsimd.tensor_tensor(nmr[:], mneg[:], rstd[:], ALU.mult).then_inc(s_rstd, 1)

            def mask_values(b):
                pool.wait_ge(s_mk[b.par], 16 * b.half + 16)
                if b.i is not None or b.off >= 1:
                    pool.wait_ge(s_masked, 2 * NG * b.n)
                pool.nop(nofuse=True)
                nc.gpsimd.tensor_scalar(maskv[:], mk[:, b.par], MASKED, 1.0, ALU.mult, ALU.mult).then_inc(s_maskv, 1)
                pool.wait_ge(s_maskv, b.n + 1)

            def add_mask(b, g):
                slot, h0 = 2 * b.par + g // 2, (g % 2) * HG
                if g % 2 == 0:
                    pool.wait_ge(s_bias[slot], 32 * b.half + 32)
                for qt in range(QT):
                    v = ring[:, slot, qt, h0:h0 + HG]
                    m = maskv[:, qt:qt + 1].to_broadcast([P, HG, S])
                    nc.gpsimd.tensor_tensor(v, v, m, ALU.add).then_inc(s_masked, 1)

            inv_std(Batch(0))
            inv_std(Batch(1))

            def body(b, n):
                mask_values(b)
                add_mask(b, 0)
                add_mask(b, 1)
                if n is None or n + 2 < B:
                    inv_std(b.plus(2))
                add_mask(b, 2)
                gs_norm(b.n)
                add_mask(b, 3)

            run_batches(pool, 0, 3, B - 3, B, body)

            def inv_std2(b):
                pool.wait_ge(s2_stats, b.n + 1)
                if b.i is not None or b.off >= 1:
                    pool.wait_ge(s2_rstd, b.n)
                pool.nop(nofuse=True)
                nc.gpsimd.tensor_scalar(vpeb[:], mvb[:, b.par, :, 1], LN_EPS, 1.0, ALU.add, ALU.mult)
                nc.gpsimd.tensor_scalar(mnegb[:], mvb[:, b.par, :, 0], -1.0, 1.0, ALU.mult, ALU.mult).then_inc(s2_pool, 1)
                pool.wait_ge(s2_pool, 2 * b.n + 1)
                if b.i is not None or b.off >= 1:
                    pool.wait_ge(s2_yn, b.n)
                nc.gpsimd.tensor_tensor(rstdb[:], vpeb[:], expo[:, 0], ALU.pow).then_inc(s2_pool, 1)
                pool.wait_ge(s2_pool, 2 * b.n + 2)
                nc.gpsimd.tensor_tensor(nmrb[:], mnegb[:], rstdb[:], ALU.mult).then_inc(s2_rstd, 1)
                if b.i is not None or b.off >= 2:
                    pool.wait_ge(s2_hid, b.n - 1)
                nc.gpsimd.tensor_tensor(yb[:, b.par], y2[:, b.par], b2b[:].unsqueeze(1).to_broadcast([P, QT, D]), ALU.add).then_inc(s2_yb, 1)

            run_batches(pool, 0, 4, B, B, lambda b, n: inv_std2(b))

        @block.vector
        def _(dve):
            chain = [0]

            def link(ins):
                chain[0] += 1
                ins.then_inc(s_dve0, 1)
                dve.wait_ge(s_dve0, chain[0])

            nc.vector.memset(vt[:, :, :, :, HD:VW], 0.0)
            link(nc.vector.memset(strg[:], 0.0))
            nc.vector.memset(vt[:, :, :, :, HD:HD + 1], 1.0)

            def stats(b):
                dve.wait_ge(s_x[b.par], 16 * b.half + 16)
                if b.i is not None or b.off >= 1:
                    dve.wait_ge(s_rstd, b.n)
                for t in range(QT):
                    ins = nc.vector.bn_stats(st6[:, t], xt[:, b.par, t])
                ins.then_inc(s_stats6, 1)
                dve.wait_ge(s_stats6, b.n + 1)
                dve.nop(nofuse=True)
                for t in range(QT):
                    ins = nc.vector.bn_aggr(mv[:, t], st6[:, t])
                ins.then_inc(s_stats, 1)

            stats(Batch(0))
            dve.wait_ge(s_const, 1)
            dve.wait_ge(s_load, 16 * n_loads)
            nc.vector.tensor_scalar(wq[:], wq[:], HD ** -0.5, None, ALU.mult)
            nc.vector.tensor_scalar(bqk[:, 0], bqk[:, 0], HD ** -0.5, None, ALU.mult)
            nc.vector.tensor_scalar(w2[:], w2[:], 0.5, None, ALU.mult)
            nc.vector.tensor_scalar(b1t[:], b1c[:], 0.5 * GELU_A, None, ALU.mult)
            nc.vector.tensor_scalar(gb2h[:], gb2[:], 0.5, None, ALU.mult)
            nc.vector.tensor_tensor(cb[:], cb[:], cb2[:], ALU.add)
            link(nc.vector.tensor_copy(ttf[:], tti[:]))
            link(nc.vector.tensor_scalar(ang[:], ttf[:], 40.0, frq[:, 0:1], ALU.mult, ALU.mult))
            nc.vector.tensor_scalar(turns[:, 0], ang[:], 1.0 / TWO_PI, None, ALU.mult)
            link(nc.vector.tensor_scalar(turns[:, 1], ang[:], 1.0 / TWO_PI, 0.25, ALU.mult, ALU.add))
            link(nc.vector.tensor_scalar(turns[:], turns[:], MAGIC, None, ALU.add))
            link(nc.vector.tensor_scalar(turns[:], turns[:], -MAGIC, None, ALU.add))
            link(nc.vector.scalar_tensor_tensor(red[:], turns[:], -C1, ang[:].unsqueeze(1).to_broadcast([P, 2, B]), ALU.mult, ALU.add))
            link(nc.vector.scalar_tensor_tensor(red2[:], turns[:], -C2, red[:], ALU.mult, ALU.add))
            link(nc.vector.scalar_tensor_tensor(red[:], turns[:], -C3, red2[:], ALU.mult, ALU.add))
            link(nc.vector.tensor_scalar(red[:, 1], red[:, 1], float(np.pi / 2), None, ALU.add))
            nc.vector.tensor_scalar(red[:], red[:], PI_IN, -PI_IN, ALU.min, ALU.max).then_inc(s_red, 1)
            dve.wait_ge(s_sin, 1)
            link(nc.vector.scalar_tensor_tensor(emb[:], sct[:], 1.0, sc[:], ALU.add, ALU.mult))
            nc.vector.tensor_scalar(emb[:], emb[:], 0.5, None, ALU.mult).then_inc(s_emb, 1)
            nc.vector.tensor_scalar(modh[:], modt[:], 0.25, 0.25, ALU.mult, ALU.add)
            dve.wait_ge(s_adaps, 1)
            for c in range(DC):
                nc.vector.tensor_scalar(adaS[:, c], bank[7][:, c * B:(c + 1) * B], bada[:, c:c + 1], 1.0, ALU.add, ALU.add)
            for c in range(DC):
                link(nc.vector.tensor_scalar(adaB[:, c], bank[7][:, (DC + c) * B:(DC + c + 1) * B], bada[:, DC + c:DC + c + 1], None, ALU.add))

            link(nc.vector.memset(gii[:], 0.0))
            nc.vector.memset(pooled[:], 0.0).then_inc(s_setup, 1)

            def column(i):
                return uv[:, :, :, bass.ds(i, 1)].rearrange("p a c r -> p a (c r)")

            def gs_column(i, first):
                if not first:
                    dve.wait_ge(s_gself, 5 * i)
                nc.vector.tensor_copy(ucol[:], column(i)).then_inc(s_gcol, 1)

            def gs_products(i):
                dve.wait_ge(s_gram, i + 1)
                nc.vector.tensor_copy(gsb[:], gs_ps.rearrange("p (a r) -> p a r", a=2)).then_inc(s_gself, 1)
                dve.wait_ge(s_gself, 5 * i + 1)
                nc.vector.tensor_copy(gii[:], gsb[:, :, bass.ds(i, 1)].rearrange("p a r -> p (a r)")).then_inc(s_gii, 1)

            def gs_update(i):
                dve.wait_ge(s_gnrm, i + 1)
                nc.vector.reciprocal(rnrm[:], nrme[:]).then_inc(s_gself, 1)
                dve.wait_ge(s_gself, 5 * i + 2)
                for a in range(2):
                    nc.vector.scalar_tensor_tensor(coef[:, a], gsb[:, a], rnrm[:, a:a + 1],
                                                   later[:, bass.ds(i, 1)].rearrange("p a r -> p (a r)"), ALU.mult, ALU.mult)
                    ins = nc.vector.tensor_scalar(qneg[:, a], ucol[:, a], rnrm[:, a:a + 1], -1.0, ALU.mult, ALU.mult)
                ins.then_inc(s_gself, 1)
                dve.wait_ge(s_gself, 5 * i + 3)
                for a in range(2):
                    for c in range(DC):
                        ins = nc.vector.scalar_tensor_tensor(uv[:, a, c], coef[:, a], qneg[:, a, c:c + 1], uv[:, a, c], ALU.mult, ALU.add)
                ins.then_inc(s_gself, 1)
                dve.wait_ge(s_gself, 5 * i + 4)
                nc.vector.tensor_scalar(column(i), qneg[:], -1.0, None, ALU.mult).then_inc(s_gself, 1)

            def response_matrix():
                dve.wait_ge(s_rm, 1)
                nc.vector.tensor_copy(gram[:], bank[0][0:R, 0:R])
                nc.vector.tensor_copy(t1[:], bank[1][0:R, 0:D])
                nc.vector.tensor_copy(uoT[:], bank[2][0:R, 0:D]).then_inc(s_rmc, 1)
                dve.wait_ge(s_rm, 2)
                nc.vector.tensor_copy(t2[:], bank[3][0:R, 0:D]).then_inc(s_rmc, 1)
                dve.wait_ge(s_rm, 3)
                nc.vector.tensor_copy(resp_m[:], tiles2(7)).then_inc(s_rmc, 1)

            stats(Batch(1))

            def reduce_head(b, h):
                slot = 2 * b.par + h // CH
                dve.wait_ge(s_qk, H * b.n + h + 1)
                for qt in range(QT):
                    v = ring[:, slot, qt, h % CH]
                    if h % HG == 0:
                        dve.wait_ge(s_masked, 2 * NG * b.n + 2 * (h // HG) + qt + 1)
                    dve.nop(nofuse=True)
                    nc.vector.tensor_tensor_reduce(out=v, in0=qk_ps[h % 2][:, qt], in1=v, scale=-1.0, scalar=ROW_MAX_NEG,
                                                   op0=ALU.add, op1=ALU.min, accum_out=nmax[:, b.par, h, qt:qt + 1]).then_inc(s_reduced, 1)

            def copy_pT(b, h):
                dve.wait_ge(s_tp, H * b.n + h + 1)
                free_pT(dve, b, h)
                nc.vector.tensor_copy(pT[:, h % (2 * HG)], tp_ps[h % 2]).then_inc(s_ptd, 1)

            def xT_out(b):
                dve.wait_ge(s_xtp, b.n + 1)
                for c in range(DC):
                    ins = nc.vector.tensor_scalar(xT[:, c], prep_a[:, c], adaS[:, c, bass.ds(b.n, 1)], adaB[:, c, bass.ds(b.n, 1)], ALU.mult, ALU.add)
                ins.then_inc(s_xT, 1)

            def rest1(b, t):
                ps = prep_b if t == 0 else prep_a
                dve.wait_ge(s_p1, 2 * b.n + t + 1)
                for c in range(DC):
                    ins = nc.vector.scalar_tensor_tensor(ps[:, c], ps[:, c], bqk[:, t, c:c + 1], parts[:, t, 0, c], ALU.add, ALU.subtract)
                ins.then_inc(s_r1, 1)

            def rest2(b, t):
                ps = prep_b if t == 0 else prep_a
                dve.wait_ge(s_p2, 2 * b.n + t + 1)
                nc.vector.tensor_tensor(parts[:, t, 2], ps, parts[:, t, 1], ALU.subtract).then_inc(s_p3, 1)

            def v_out(b):
                dve.wait_ge(s_vp, b.n + 1)
                for t in range(QT):
                    ins = nc.vector.tensor_tensor(vt[:, b.par, t, :, 0:HD], prep_b[:, t].rearrange("p (h d) -> p h d", d=HD),
                                                  bvb[:].rearrange("p (h d) -> p h d", d=HD), ALU.add)
                ins.then_inc(s_v, 1)

            def xres_out(b):
                dve.wait_ge(s_xb, b.n + 1)
                if b.i is not None or b.off >= 2:
                    dve.wait_ge(s_x2, b.n - 1)
                nc.vector.tensor_tensor(xres[:, b.par], prep_a, bob[:].unsqueeze(1).to_broadcast([P, QT, D]), ALU.add).then_inc(s_xres, 1)

            def normalise_ctx(b, qt):
                dve.wait_ge(s_cn, 2 * b.n + qt + 1)
                heads = bank[7][:].rearrange("p (h w) -> p h w", w=VW)
                nc.vector.reciprocal(rec[:, qt].unsqueeze(2), heads[:, :, HD:HD + 1]).then_inc(s_rec, 1)
                dve.wait_ge(s_rec, 2 * b.n + qt + 1)
                nc.vector.tensor_tensor(ctxn[:, qt].rearrange("p (h d) -> p h d", d=HD), heads[:, :, 0:HD],
                                        rec[:, qt].unsqueeze(2).to_broadcast([P, H, HD]), ALU.mult).then_inc(s_ctxn, 1)

            def x2_out(b):
                dve.wait_ge(s_o, b.n + 1)
                if b.i is not None or b.off >= 2:
                    dve.wait_ge(s_x2st[b.par], 16 * b.half)
                dve.wait_ge(s_xres, b.n + 1)
                nc.vector.tensor_tensor(x2s[:, b.par], tail_ps, xres[:, b.par], ALU.add).then_inc(s_x2, 1)

            def prep_all(b):
                xT_out(b)
                rest1(b, 0)
                rest2(b, 0)
                rest1(b, 1)
                rest2(b, 1)
                v_out(b)
                xres_out(b)

            prep_all(Batch(0))

            def body(b, n):
                main = n is None or n < B
                prep = n is None or n + 1 < B
                tail = n is None or n >= 1
                for h in range(H):
                    if main:
                        reduce_head(b, h)
                    at = behind(b, n, h, 3)
                    if at and at[1] % 2 == 1:
                        copy_pT(*at)
                    if prep:
                        if h == 1:
                            xT_out(b.plus(1))
                        if h == 4:
                            rest1(b.plus(1), 0)
                        if h == 5:
                            rest1(b.plus(1), 1)
                        if h == 6:
                            rest2(b.plus(1), 0)
                        if h == 7:
                            rest2(b.plus(1), 1)
                        if h == 9:
                            v_out(b.plus(1))
                    if h == 3 and (n is None or n + 2 < B):
                        stats(b.plus(2))
                    if main:
                        if h == 0:
                            gs_column(b.n, n == 0)
                        if h == 3:
                            gs_products(b.n)
                        if h == 14:
                            gs_update(b.n)
                    if tail:
                        if h == 7:
                            normalise_ctx(b.plus(-1), 0)
                        if h == 9:
                            normalise_ctx(b.plus(-1), 1)
                        if h == 12:
                            x2_out(b.plus(-1))
                    if prep and h == 13:
                        xres_out(b.plus(1))

            run_batches(dve, 0, 3, B - 3, B + 1, body)
            last = Batch(B - 1)
            response_matrix()

            def stats2(b):
                dve.wait_ge(s_y[b.par], 16 * b.half + 16)
                if b.i is not None or b.off >= 1:
                    dve.wait_ge(s2_stats, b.n)
                for t in range(QT):
                    ins = nc.vector.bn_stats(st6b[:, t], y2[:, b.par, t])
                ins.then_inc(s2_six, 1)
                dve.wait_ge(s2_six, b.n + 1)
                if b.i is not None or b.off >= 2:
                    dve.wait_ge(s2_rstd, b.n - 1)
                dve.nop(nofuse=True)
                dve.nop(nofuse=True)
                for t in range(QT):
                    ins = nc.vector.bn_aggr(mvb[:, b.par, t], st6b[:, t])
                ins.then_inc(s2_stats, 1)

            def gate_pair(b, j):
                dve.wait_ge(s2_up, 4 * b.n + j + 1)
                dve.wait_ge(s2_th, 4 * b.n + j + 1)
                if b.i is not None or b.off >= 1:
                    dve.wait_ge(s2_g, 4 * (b.n - 1) + j + 1)
                for f in range(2):
                    ins = nc.vector.tensor_scalar(up[:, j, f], tiles2(j)[:, f], b1c[:, 2 * j + f:2 * j + f + 1], None, ALU.add)
                ins.then_inc(s2_u, 1)
                dve.wait_ge(s2_u, 4 * b.n + j + 1)
                nc.vector.scalar_tensor_tensor(gT[:, b.par, 2 * j:2 * j + 2], th[:, j], 1.0, up[:, j], ALU.add, ALU.mult).then_inc(s2_g, 1)

            def hid_out(b):
                dve.wait_ge(s2_dn, b.n + 1)
                dve.wait_ge(s2_yb, b.n + 1)
                if b.i is not None or b.off >= 2:
                    dve.wait_ge(s2_fin, b.n - 1)
                nc.vector.tensor_tensor(hid[:, b.par], tiles2(4), yb[:, b.par], ALU.add).then_inc(s2_hid, 1)

            def strength(b):
                dve.wait_ge(s2_z, b.n + 1)
                if b.i is not None or b.off >= 1:
                    dve.wait_ge(s2_fin, b.n)
                nc.vector.tensor_scalar(strg[:, b.par:b.par + 1], gth[:], 1.0, modh[:, bass.ds(b.n, 1)], ALU.add, ALU.mult).then_inc(s2_str, 1)

            def fin_out(b):
                dve.wait_ge(s2_r, b.n + 1)
                dve.wait_ge(s2_hid, b.n + 1)
                if b.i is not None or b.off >= 1:
                    dve.wait_ge(s2_fin, b.n)
                nc.vector.tensor_tensor(rsp[:], tiles2(7), cb[:].unsqueeze(1).to_broadcast([P, QT, D]), ALU.add).then_inc(s2_rs, 1)
                dve.wait_ge(s2_rs, b.n + 1)
                dve.wait_ge(s2_str, b.n + 1)
                if b.i is not None or b.off >= 2:
                    dve.wait_ge(s_out[b.par], 16 * b.half)
                nc.vector.scalar_tensor_tensor(fin[:, b.par], rsp[:], strg[:, b.par:b.par + 1], hid[:, b.par], ALU.mult, ALU.add).then_inc(s2_fin, 1)

            dve.wait_ge(s_tp, H * B)
            stats2(Batch(0))
            stats2(Batch(1))

            def body2(b, n):
                tail = n is None or n >= 1
                for j in range(4):
                    gate_pair(b, j)
                    if j == 1 and (n is None or n + 2 < B):
                        stats2(b.plus(2))
                if tail:
                    strength(b.plus(-1))
                    fin_out(b.plus(-1))
                hid_out(b)

            run_batches(dve, 0, 3, B - 3, B, body2)
            strength(last)
            fin_out(last)

        @block.scalar
        def _(act):
            act.wait_ge(s_red, 1)
            nc.scalar.activation(sc[:], red[:], ACT.Sin).then_inc(s_act0, 1)
            act.wait_ge(s_act0, 1)
            nc.scalar.activation(modt[:], scr[:], ACT.Tanh, scale=0.5)
            nc.scalar.activation(sct[:], sc[:], ACT.Tanh, scale=0.5).then_inc(s_sin, 1)

            def xn_out(b):
                act.wait_ge(s_rstd, b.n + 1)
                act.wait_ge(s_x[b.par], 16 * b.half + 16)
                if b.i is not None or b.off >= 1:
                    act.wait_ge(s_xtp, b.n)
                for t in range(QT):
                    ins = nc.scalar.activation(xn[:, t], xt[:, b.par, t], ACT.Identity, bias=nmr[:, t:t + 1], scale=rstd[:, t:t + 1])
                ins.then_inc(s_xn, 1)

            def exp_head(b, h):
                slot = 2 * b.par + h // CH
                for qt in range(QT):
                    v = ring[:, slot, qt, h % CH]
                    act.wait_ge(s_reduced, 2 * H * b.n + 2 * h + qt + 1)
                    nc.scalar.activation(v, v, ACT.Exp, bias=nmax[:, b.par, h, qt:qt + 1], scale=-1.0).then_inc(s_exp, 1)

            def copy_pT(b, h):
                act.wait_ge(s_tp, H * b.n + h + 1)
                free_pT(act, b, h)
                nc.scalar.activation(pT[:, h % (2 * HG)], tp_ps[h % 2], ACT.Copy).then_inc(s_pta, 1)

            def part1(b, t):
                ps = prep_b if t == 0 else prep_a
                act.wait_ge(s_qp if t == 0 else s_kp, b.n + 1)
                if b.i is not None or b.off >= 1:
                    act.wait_ge(s_wq_d if t == 0 else s_wk_d, 16 * b.n)
                for c in range(DC):
                    ins = nc.scalar.activation(parts[:, t, 0, c], ps[:, c], ACT.Identity, bias=bqk[:, t, c:c + 1])
                ins.then_inc(s_p1, 1)

            def part2(b, t):
                ps = prep_b if t == 0 else prep_a
                act.wait_ge(s_r1, 2 * b.n + t + 1)
                nc.scalar.activation(parts[:, t, 1], ps, ACT.Copy).then_inc(s_p2, 1)

            def pv_out(b, g):
                act.wait_ge(s_pv, NG * b.n + g + 1)
                if g == 0 and (b.i is not None or b.off >= 1):
                    act.wait_ge(s_cn, 2 * b.n)
                nc.scalar.activation(pv_sb[:, g], pv_ps, ACT.Copy).then_inc(s_pvc, 1)

            def ctxT_out(b):
                act.wait_ge(s_cT, b.n + 1)
                nc.scalar.activation(ctxT[:], tail_ps, ACT.Copy).then_inc(s_ctxT, 1)

            def prep_parts(b):
                for t in range(2):
                    part1(b, t)
                    part2(b, t)

            act.wait_ge(s_setup, 1)
            xn_out(Batch(0))
            prep_parts(Batch(0))
            xn_out(Batch(1))

            def body(b, n):
                prep = n is None or n + 1 < B
                tail = n is None or n >= 1
                for h in range(H):
                    at = behind(b, n, h, 1)
                    if at:
                        exp_head(*at)
                    at = behind(b, n, h, 3)
                    if at and at[1] % 2 == 0:
                        copy_pT(*at)
                    at = behind(b, n, h, 8)
                    if at and at[1] % HG == 0:
                        pv_out(at[0], at[1] // HG)
                    if prep:
                        if h == 3:
                            part1(b.plus(1), 0)
                        if h == 4:
                            part1(b.plus(1), 1)
                        if h == 5:
                            part2(b.plus(1), 0)
                        if h == 6:
                            part2(b.plus(1), 1)
                    if tail and h == 10:
                        ctxT_out(b.plus(-1))
                    if h == 14 and (n is None or n + 2 < B):
                        xn_out(b.plus(2))

            run_batches(act, 0, 3, B - 3, B + 1, body)
            last = Batch(B - 1)

            def yn_out(b):
                act.wait_ge(s2_rstd, b.n + 1)
                act.wait_ge(s_y[b.par], 16 * b.half + 16)
                if b.i is not None or b.off >= 1:
                    act.wait_ge(s2_yt, b.n)
                for t in range(QT):
                    ins = nc.scalar.activation(yn[:, t], y2[:, b.par, t], ACT.Identity, bias=nmrb[:, t:t + 1], scale=rstdb[:, t:t + 1])
                ins.then_inc(s2_yn, 1)

            def hT_out(b):
                act.wait_ge(s2_yt, b.n + 1)
                if b.i is not None or b.off >= 2:
                    act.wait_ge(s2_up, 4 * (b.n - 1))
                for c in range(DC):
                    ins = nc.scalar.activation(hT[:, b.par, c], tiles2(5)[:, c], ACT.Identity, bias=be2c[:, c:c + 1], scale=g2c[:, c:c + 1])
                ins.then_inc(s2_hT, 1)

            def tanh_pair(b, j):
                act.wait_ge(s2_up, 4 * b.n + j + 1)
                if b.i is not None or b.off >= 1:
                    act.wait_ge(s2_g, 4 * (b.n - 1) + j + 1)
                for f in range(2):
                    ins = nc.scalar.activation(th[:, j, f], tiles2(j)[:, f], ACT.Tanh, bias=b1t[:, 2 * j + f:2 * j + f + 1], scale=0.5 * GELU_A)
                ins.then_inc(s2_th, 1)

            def hidT_out(b):
                act.wait_ge(s2_hidp, b.n + 1)
                if b.i is not None or b.off >= 1:
                    act.wait_ge(s2_r, b.n)
                    act.wait_ge(s2_h1p, b.n)
                for c in range(DC):
                    ins = nc.scalar.activation(hidT[:, c], tiles2(6)[:, c], ACT.Copy, accum_out=pooled[:, c:c + 1])
                ins.then_inc(s2_hidT, 1)

            def gate1(b):
                act.wait_ge(s2_h1p, b.n + 1)
                nc.scalar.activation(h1[:], bank[6][0:GW, 0:1], ACT.Relu, bias=gb1[:], scale=1.0 / S).then_inc(s2_h1, 1)

            def gate2(b):
                act.wait_ge(s2_zp, b.n + 1)
                if b.i is not None or b.off >= 1:
                    act.wait_ge(s2_str, b.n)
                nc.scalar.activation(gth[:], bank[6][:, 8:9], ACT.Tanh, bias=gb2h[:], scale=0.5).then_inc(s2_z, 1)

            yn_out(Batch(0))
            hT_out(Batch(0))
            yn_out(Batch(1))

            def body2(b, n):
                tail = n is None or n >= 1
                tanh_pair(b, 0)
                tanh_pair(b, 1)
                if n is None or n + 1 < B:
                    hT_out(b.plus(1))
                tanh_pair(b, 2)
                if tail:
                    hidT_out(b.plus(-1))
                tanh_pair(b, 3)
                if tail:
                    gate1(b.plus(-1))
                    gate2(b.plus(-1))
                if n is None or n + 2 < B:
                    yn_out(b.plus(2))

            run_batches(act, 0, 3, B - 3, B, body2)
            hidT_out(last)
            gate1(last)
            gate2(last)

        @block.tensor
        def _(pe):
            mm = nc.tensor.matmul
            pe.wait_ge(s_emb, 1)
            for n in range(2 * DC):
                for c in range(2):
                    ins = mm(bank[7][:, n * B:(n + 1) * B], wada[:, c, n * P:(n + 1) * P], emb[:, c], start=(c == 0), stop=(c == 1))
            ins.then_inc(s_adaps, 1)

            def gs_gram(i, i_prev, i_prev2):
                pe.wait_ge(s_gcol, i + 1)
                if i_prev:
                    pe.wait_ge(s_gself, 5 * i)
                if i_prev2:
                    pe.wait_ge(s_x2, i - 1)
                for a in range(2):
                    for c in range(DC):
                        ins = mm(gs_ps[:, a * R:(a + 1) * R], ucol[:, a, c:c + 1].to_broadcast([P, P]), uv[:, a, c], start=(c == 0), stop=(c == DC - 1))
                ins.then_inc(s_gram, 1)

            def response_matrix():
                pe.wait_ge(s_gself, 5 * R)
                for c in range(DC):
                    mm(bank[0][0:R, 0:R], uv[:, 1, c], uv[:, 1, c], start=(c == 0), stop=(c == DC - 1))
                mm(bank[1][0:R, 0:D], uv[0:R, 0, 0], respT[:], start=True, stop=True)
                for c in range(DC):
                    ins = nc.tensor.transpose(bank[2][0:R, c * P:(c + 1) * P], uv[:, 0, c], ident[:])
                ins.then_inc(s_rm, 1)
                pe.wait_ge(s_rmc, 1)
                mm(bank[3][0:R, 0:D], gram[:], t1[:], start=True, stop=True).then_inc(s_rm, 1)
                pe.wait_ge(s_rmc, 2)
                for c in range(DC):
                    ins = mm(bank[7][:, c * D:(c + 1) * D], uoT[:, c * P:(c + 1) * P], t2[:], start=True, stop=True)
                ins.then_inc(s_rm, 1)
                pe.wait_ge(s_rmc, 3)
            pe.wait_ge(s_setup, 1)

            def scores(b, h):
                if b.i is not None or H * b.off + h >= 2:
                    pe.wait_ge(s_reduced, 2 * (H * b.n + h - 1))
                if h == 0:
                    pe.wait_ge(s_stq[b.par], 16 * NS * (b.half + 1))
                    pe.wait_ge(s_stk[b.par], 16 * NS * (b.half + 1))
                for qt in range(QT):
                    ins = mm(qk_ps[h % 2][:, qt], stack[:, b.par, 0, h, qt * P:(qt + 1) * P], stack[:, b.par, 1, h, :], start=True, stop=True)
                ins.then_inc(s_qk, 1)

            def transposes(b, h):
                slot = 2 * b.par + h // CH
                if b.i is not None or H * b.off + h >= 2:
                    pe.wait_ge(s_pta if h % 2 == 0 else s_ptd, (H // 2) * b.n + h // 2)
                for qt in range(QT):
                    pe.wait_ge(s_exp, 2 * H * b.n + 2 * h + qt + 1)
                    for kt in range(QT):
                        ins = nc.tensor.transpose(tp_ps[h % 2][:, kt, qt * P:(qt + 1) * P], ring[:, slot, qt, h % CH, kt * P:(kt + 1) * P], ident[:])
                ins.then_inc(s_tp, 1)

            def pv(b, g):
                pe.wait_ge(s_pta, (H // 2) * b.n + 2 * g + 2)
                pe.wait_ge(s_ptd, (H // 2) * b.n + 2 * g + 2)
                if g == 0:
                    pe.wait_ge(s_v, b.n + 1)
                if b.i is not None or NG * b.off + g >= 1:
                    pe.wait_ge(s_pvc, NG * b.n + g)
                for kt in range(QT):
                    for j in range(HG):
                        h = HG * g + j
                        ins = mm(pv_ps[VW * j:VW * (j + 1), :], vt[:, b.par, kt, h], pT[:, h % (2 * HG), kt], start=(kt == 0), stop=(kt == QT - 1))
                ins.then_inc(s_pv, 1)

            def x_transpose(b):
                pe.wait_ge(s_xn, b.n + 1)
                if b.i is not None or b.off >= 1:
                    pe.wait_ge(s_xres, b.n)
                for c in range(DC):
                    for t in range(QT):
                        ins = nc.tensor.transpose(prep_a[:, c, t * P:(t + 1) * P], xn[:, t, c * P:(c + 1) * P], ident[:])
                ins.then_inc(s_xtp, 1)

            def project_qk(b, t):
                w, ps = (wq, prep_b) if t == 0 else (wk, prep_a)
                pe.wait_ge(s_xT, b.n + 1)
                if t == 0 and (b.i is not None or b.off >= 1):
                    pe.wait_ge(s_v, b.n)
                for n in range(DC):
                    for c in range(DC):
                        ins = mm(ps[:, n], w[:, c, n * P:(n + 1) * P], xT[:, c], start=(c == 0), stop=(c == DC - 1))
                ins.then_inc(s_qp if t == 0 else s_kp, 1)

            def project_v(b):
                pe.wait_ge(s_p3, 2 * b.n + 1)
                for t in range(QT):
                    for c in range(DC):
                        ins = mm(prep_b[:, t], xT[:, c, t * P:(t + 1) * P], wv[:, c], start=(c == 0), stop=(c == DC - 1))
                ins.then_inc(s_vp, 1)

            def x_back(b):
                pe.wait_ge(s_p3, 2 * b.n + 2)
                for t in range(QT):
                    for c in range(DC):
                        ins = nc.tensor.transpose(prep_a[:, t, c * P:(c + 1) * P], xT[:, c, t * P:(t + 1) * P], ident[:])
                ins.then_inc(s_xb, 1)

            def ctx_natural(b, qt):
                pe.wait_ge(s_pvc, NG * b.n + NG)
                if qt == 0:
                    if b.i is not None or b.off >= 1:
                        pe.wait_ge(s_x2, b.n)
                    if b.i is not None or b.off + 1 < B:
                        pe.wait_ge(s_gii, b.n + 2)
                else:
                    pe.wait_ge(s_ctxn, 2 * b.n + 1)
                for g in range(NG):
                    ins = nc.tensor.transpose(bank[7][:, g * P:(g + 1) * P], pv_sb[:, g, qt * P:(qt + 1) * P], ident[:])
                ins.then_inc(s_cn, 1)

            def ctx_transpose(b):
                pe.wait_ge(s_ctxn, 2 * b.n + 2)
                for c in range(DC):
                    for t in range(QT):
                        ins = nc.tensor.transpose(tail_ps[:, c, t * P:(t + 1) * P], ctxn[:, t, c * P:(c + 1) * P], ident[:])
                ins.then_inc(s_cT, 1)

            def project_o(b):
                pe.wait_ge(s_ctxT, b.n + 1)
                for t in range(QT):
                    for c in range(DC):
                        ins = mm(tail_ps[:, t], ctxT[:, c, t * P:(t + 1) * P], wo[:, c], start=(c == 0), stop=(c == DC - 1))
                ins.then_inc(s_o, 1)

            first = Batch(0)
            x_transpose(first)
            project_qk(first, 0)
            project_qk(first, 1)
            project_v(first)
            x_back(first)
            scores(first, 0)

            def body(b, n):
                main = n is None or n < B
                prep = n is None or n + 1 < B
                tail = n is None or n >= 1
                for h in range(H):
                    if main and h + 1 < H:
                        scores(b, h + 1)
                    elif prep:
                        scores(b.plus(1), 0)
                    at = behind(b, n, h, 2)
                    if at:
                        transposes(*at)
                    at = behind(b, n, h, 7)
                    if at and at[1] % HG == 0:
                        pv(at[0], at[1] // HG)
                    if prep:
                        if h == 0:
                            x_transpose(b.plus(1))
                        if h == 2:
                            project_qk(b.plus(1), 0)
                        if h == 3:
                            project_qk(b.plus(1), 1)
                        if h == 8:
                            project_v(b.plus(1))
                        if h == 10:
                            x_back(b.plus(1))
                    if main and h == 1:
                        gs_gram(b.n, n is None or n >= 1, n is None or n >= 2)
                    if tail:
                        if h == 6:
                            ctx_natural(b.plus(-1), 0)
                        if h == 8:
                            ctx_natural(b.plus(-1), 1)
                        if h == 9:
                            ctx_transpose(b.plus(-1))
                        if h == 11:
                            project_o(b.plus(-1))

            run_batches(pe, 0, 3, B - 3, B + 1, body)
            last = Batch(B - 1)

            pe.wait_ge(s_x2, B)
            response_matrix()

            def y_transpose(b):
                pe.wait_ge(s2_yn, b.n + 1)
                if b.i is not None or b.off >= 1:
                    pe.wait_ge(s2_hT, b.n)
                for c in range(DC):
                    for t in range(QT):
                        ins = nc.tensor.transpose(tiles2(5)[:, c, t * P:(t + 1) * P], yn[:, t, c * P:(c + 1) * P], ident[:])
                ins.then_inc(s2_yt, 1)

            def up_pair(b, j):
                if j == 0:
                    pe.wait_ge(s2_hT, b.n + 1)
                if b.i is not None or b.off >= 1:
                    pe.wait_ge(s2_u, 4 * (b.n - 1) + j + 1)
                for f in range(2):
                    n = 2 * j + f
                    for c in range(DC):
                        ins = mm(tiles2(j)[:, f], w1[:, c, n * P:(n + 1) * P], hT[:, b.par, c], start=(c == 0), stop=(c == DC - 1))
                ins.then_inc(s2_up, 1)

            def down(b):
                if b.i is not None or b.off >= 1:
                    pe.wait_ge(s2_hid, b.n)
                for t in range(QT):
                    for f in range(FC):
                        if t == 0 and f % 2 == 0:
                            pe.wait_ge(s2_g, 4 * b.n + f // 2 + 1)
                        ins = mm(tiles2(4)[:, t], gT[:, b.par, f, t * P:(t + 1) * P], w2[:, f], start=(f == 0), stop=(f == FC - 1))
                ins.then_inc(s2_dn, 1)

            def hid_transpose(b):
                pe.wait_ge(s2_hid, b.n + 1)
                if b.i is not None or b.off >= 1:
                    pe.wait_ge(s2_z, b.n)
                for c in range(DC):
                    for t in range(QT):
                        ins = nc.tensor.transpose(tiles2(6)[:, c, t * P:(t + 1) * P], hid[:, b.par, t, c * P:(c + 1) * P], ident[:])
                ins.then_inc(s2_hidp, 1)

            def gate_h1(b):
                pe.wait_ge(s2_hidT, b.n + 1)
                for c in range(DC):
                    ins = mm(bank[6][0:GW, 0:1], gw1[:, c], pooled[:, c:c + 1], start=(c == 0), stop=(c == DC - 1))
                ins.then_inc(s2_h1p, 1)

            def gate_z(b):
                pe.wait_ge(s2_h1, b.n + 1)
                mm(bank[6][:, 8:9], h1[:].to_broadcast([GW, P]), gw2[:], start=True, stop=True).then_inc(s2_zp, 1)

            def response(b):
                pe.wait_ge(s2_hidT, b.n + 1)
                if b.i is not None or b.off >= 1:
                    pe.wait_ge(s2_rs, b.n)
                for t in range(QT):
                    for c in range(DC):
                        ins = mm(tiles2(7)[:, t], hidT[:, c, t * P:(t + 1) * P], resp_m[:, c], start=(c == 0), stop=(c == DC - 1))
                ins.then_inc(s2_r, 1)

            y_transpose(first)

            def body2(b, n):
                tail = n is None or n >= 1
                up_pair(b, 0)
                if n is None or n + 1 < B:
                    y_transpose(b.plus(1))
                up_pair(b, 1)
                if tail:
                    hid_transpose(b.plus(-1))
                up_pair(b, 2)
                up_pair(b, 3)
                if tail:
                    gate_h1(b.plus(-1))
                    response(b.plus(-1))
                    gate_z(b.plus(-1))
                down(b)

            run_batches(pe, 0, 3, B - 3, B, body2)
            hid_transpose(last)
            gate_h1(last)
            response(last)
            gate_z(last)


_NAMES = ['W_ada', 'b_ada', 'Wq', 'bq', 'Wk', 'bk', 'Wv', 'bv', 'Wo', 'bo', 'W1', 'b1', 'W2', 'b2', 'g2', 'beta2']


def kernel(**inputs):
    import concourse.bacc as _bacc
    from concourse.bass_utils import run_bass_kernel_spmd as _run

    a = {k: np.asarray(v) for k, v in inputs.items()}
    feeds = {
        "x": a["x"], "itok": a["itok_B_34_63"], "fside": a["fside_Bx16xSxS_0"], "score": a["condB_safetyscore"],
        "mask": a["mask_Bx1xSxS_bk0"],
    }
    feeds.update({n: a["L0_cond_" + n] for n in _NAMES})
    feeds.update({n: feeds[n].reshape(-1, P).T for n in ('b_ada', 'bq', 'bk', 'b1', 'g2', 'beta2')})
    feeds.update({
        "U": a["L1_cond_U"], "V": a["L1_cond_V"], "safety_bias": a["L1_cond_safety_bias"],
        "gate_w1T": a["L1_cond_gate_w1"].T, "gate_b1": a["L1_cond_gate_b1"], "gate_w2T": a["L1_cond_gate_w2"].T,
        "gate_b2": a["L1_cond_gate_b2"], "resp_wT": a["L1_cond_resp_w"].T, "resp_b": a["L1_cond_resp_b"],
        "freqs": np.exp(np.arange(D // 2, dtype=np.float32) * np.float32(-np.log(10000.0) / (D // 2 - 1))).astype(np.float32),
    })
    nc = _bacc.Bacc("TRN2", target_bir_lowering=False, num_devices=1)
    arrays, aps = {}, {}
    for name, v in feeds.items():
        v = np.ascontiguousarray(v)
        arrays["in_" + name] = v
        aps[name] = nc.dram_tensor("in_" + name, v.shape, mybir.dt.from_np(v.dtype), kind="ExternalInput").ap()
    aps["out"] = nc.dram_tensor("out_0", (B, S, D), F32, kind="ExternalOutput").ap()
    attention_block_kernel(nc, **aps)
    r = _run(nc, [arrays], core_ids=[0])
    return r.results[0]["out_0"]
```

```python
from contextlib import ExitStack

import numpy as np

import concourse.bass as bass
from concourse import mybir

F32 = mybir.dt.float32
F32R = mybir.dt.float32r
BF16 = mybir.dt.bfloat16
I32 = mybir.dt.int32
U8 = mybir.dt.uint8
ALU = mybir.AluOpType
ACT = mybir.ActivationFunctionType

P = 128
B, S, D = 32, 256, 256
H, HD = 16, 16
F = 1024
R = 32
GW = 64
QT = S // P
DC = D // P
FC = F // P
HG = 4
NG = H // HG
CH = 8
RING = 4
VW = 32
LN_EPS = 1e-5
GS_EPS = 1e-8
RUNS = [[(0, 3, 0, 0), (3, 2, 1, 0), (5, 1, 2, 0)], [(0, 3, 0, 1), (3, 2, 0, 1), (5, 1, 0, 0)]]
SPLIT = [(0, 0), (0, 1), (0, 2), (1, 0), (1, 1), (2, 0)]
NS = len(SPLIT)
KQ = NS * HD
GELU_A = 1.702
TWO_PI = 2.0 * np.pi
C1 = 6.28125
C2 = float(np.float32(np.round((TWO_PI - C1) * 2.0**21) / 2.0**21))
C3 = float(np.float32(TWO_PI - C1 - C2))
MASKED = -1.0e30
ROW_MAX_NEG = 1.0e29
MAGIC = 1.5 * 2.0**23
PI_IN = 3.1415925


HI_LO = [(0, 0), (0, 1), (1, 0)]
U_ACT = [0, 2]


def u_done(owner_has, b, j):
    return 2 * b.n + sum(1 for k in range(j + 1) if (k in U_ACT) == owner_has)


def f32(a):
    return a.bitcast(F32)


class Batch:

    def __init__(self, off, i=None):
        self.par = off % 2
        self.half = off // 2 if i is None else i + off // 2
        self.n = off if i is None else 2 * i + off
        self.off, self.i = off, i

    def plus(self, k):
        return Batch(self.off + k, self.i)


ACT_HEADS = [h for h in range(H) if h % 2 == 0 or h == H - 1 or h == 7]
DVE_HEADS = [h for h in range(H) if h not in ACT_HEADS]


def copied(heads, b, h):
    return len(heads) * b.n + sum(1 for k in heads if k <= h)


def behind(b, n, h, k):
    if h >= k:
        return (b, h - k) if n is None or n < B else None
    return (b.plus(-1), h - k + H) if n is None or n >= 1 else None


def run_batches(eng, first, loop_from, loop_to, last, body):
    for b in range(first, loop_from):
        body(Batch(b), b)
    with eng.Fori(0, (loop_to - loop_from) // 2) as i:
        for off in range(2):
            body(Batch(loop_from + off, i), None)
    for b in range(loop_to, last):
        body(Batch(b), b)


def attention_block_kernel(nc, x, itok, fside, score, mask, W_ada, b_ada, Wq, bq, Wk, bk, Wv, bv, Wo, bo,
                           W1, b1, W2, b2, g2, beta2, U, V, safety_bias, gate_w1T, gate_b1, gate_w2T, gate_b2,
                           resp_wT, resp_b, freqs, out):
    with ExitStack() as ctx:
        def sb(name, shape, dt=F32):
            return ctx.enter_context(nc.sbuf_tensor(name, shape, dt))

        def sem(name):
            return ctx.enter_context(nc.semaphore(name))

        parts_d = nc.dram_tensor("parts_d", (2, 2, 3, P, DC * S), BF16, kind="Internal").ap()
        x2_d = nc.dram_tensor("x2_d", (B, S, D), F32, kind="Internal").ap()

        wq = sb("wq", [P, DC, D]); wk = sb("wk", [P, DC, D]); wv = sb("wv", [P, DC, D]); wo = sb("wo", [P, DC, D])
        w1 = sb("w1", [P, DC, F]); w2 = sb("w2", [P, FC, D]); wada = sb("wada", [P, 2, 2 * D])
        bqk = sb("bqk", [P, 2, DC]); bada = sb("bada", [P, 2 * DC]); b1c = sb("b1c", [P, FC]); b1t = sb("b1t", [P, FC])
        g2c = sb("g2c", [P, DC]); be2c = sb("be2c", [P, DC])
        bvb = sb("bvb", [P, D]); bob = sb("bob", [P, D]); b2b = sb("b2b", [P, D]); cb = sb("cb", [P, D]); cb2 = sb("cb2", [P, D])
        ident = sb("ident", [P, P]); later = sb("later", [P, R, R]); expo = sb("expo", [P, 2, 2])
        frq = sb("frq", [P, 1]); tti = sb("tti", [P, B], I32); ttf = sb("ttf", [P, B]); ang = sb("ang", [P, B])
        turns = sb("turns", [P, 2, B]); red = sb("red", [P, 2, B]); red2 = sb("red2", [P, 2, B])
        sc = sb("sc", [P, 2, B]); sct = sb("sct", [P, 2, B]); emb = sb("emb", [P, 2, B])
        adaS = sb("adaS", [P, DC, B]); adaB = sb("adaB", [P, DC, B])
        scr = sb("scr", [P, B]); modh = sb("modh", [P, B]); modt = sb("modt", [P, B])
        gw1 = sb("gw1", [P, DC, GW]); gb1 = sb("gb1", [GW, 1]); gw2 = sb("gw2", [GW, 1]); gb2 = sb("gb2", [P, 1]); gb2h = sb("gb2h", [P, 1])
        uv = sb("uv", [P, 2, DC, R]); ucol = sb("ucol", [P, 2, DC]); gsb = sb("gsb", [P, 2, R]); gii = sb("gii", [P, 2])
        nrm = sb("nrm", [P, 2]); nrme = sb("nrme", [P, 2]); rnrm = sb("rnrm", [P, 2]); qneg = sb("qneg", [P, 2, DC]); coef = sb("coef", [P, 2, R])
        respT = sb("respT", [R, D]); gram = sb("gram", [R, R]); t1 = sb("t1", [R, D]); t2 = sb("t2", [R, D]); uoT = sb("uoT", [R, D]); resp_m = sb("resp_m", [P, DC, D])

        ring = sb("ring", [P, RING, QT, CH, S])
        ring_at = nc.sbuf_base - 4 * RING * QT * CH * S
        pT = sb("pT", [P, 2 * HG, QT, S])
        stack_all = sb("stack", [P, 2, 2, H, S], BF16)
        stack = stack_all[0:KQ]
        parts = sb("parts", [P, 2, 3, DC, S], BF16)
        xt = sb("xt", [P, 2, QT, D]); st6 = sb("st6", [P, QT, 6]); mv = sb("mv", [P, QT, 2])
        vpe = sb("vpe", [P, QT]); rstd = sb("rstd", [P, QT]); mneg = sb("mneg", [P, QT]); nmr = sb("nmr", [P, QT])
        xn = sb("xn", [P, QT, D]); xT = sb("xT", [P, DC, S]); xres = sb("xres", [P, 2, QT, D])
        vt = sb("vt", [P, 2, QT, H, VW])
        vt_at = nc.sbuf_base - 4 * 2 * QT * H * VW
        mk = sb("mk", [P, 2, QT, S], U8); maskv = sb("maskv", [P, QT, S])
        nmax = sb("nmax", [P, 2, H, QT])
        pv_sb = sb("pv_sb", [P, NG, S]); rec = sb("rec", [P, QT, H]); ctxn = sb("ctxn", [P, QT, D]); ctxT = sb("ctxT", [P, DC, S]); x2s = sb("x2s", [P, 2, QT, D])

        def lay(name, shape, at):
            return nc.alloc_sbuf_tensor_at(name, shape, F32R, offset=at)[:]

        w1s = [lay("w1_high", [P, DC, F], ring_at), lay("w1_rest", [P, DC, F], ring_at + 4 * DC * F)]
        w2s_at = ring_at + 4 * 2 * DC * F
        w2s = [lay("w2_high", [P, FC, D], w2s_at), lay("w2_rest", [P, FC, D], w2s_at + 4 * FC * D)]
        gTs_at = w2s_at + 4 * 2 * FC * D
        gTs = [lay("gT_high", [P, 2, FC, S], gTs_at), lay("gT_rest", [P, 2, FC, S], gTs_at + 4 * 2 * FC * S)]
        hTs = [lay("hT_high", [P, 2, DC, S], vt_at), lay("hT_rest", [P, 2, DC, S], vt_at + 4 * 2 * DC * S)]
        regions = [stack_all[:].rearrange("p a t h s -> p (a t h s)").bitcast(F32), pT[:].rearrange("p h t s -> p (h t s)")]
        place = [0, 0]

        def carve(*shape):
            n = int(np.prod(shape))
            i = 0 if place[0] + n <= regions[0].shape[1] else 1
            a = regions[i][:, place[i]:place[i] + n]
            place[i] += n
            if len(shape) == 2:
                return a.rearrange("p (a b) -> p a b", a=shape[0])
            return a.rearrange("p (a b c) -> p a b c", a=shape[0], b=shape[1])

        y2 = carve(2, QT, D)
        yb = carve(2, QT, D)
        yn = carve(QT, D)
        hT = carve(DC, S)
        th = carve(4, 2, S)
        up = carve(4, 2, S)
        gT = carve(FC, S)
        hid = carve(2, QT, D)
        hidT = carve(DC, S)
        rsp = carve(QT, D)
        fin = carve(2, QT, D)
        pooled = sb("pooled", [P, DC]); h1 = sb("h1", [GW, 1]); gth = sb("gth", [P, 1]); strg = sb("strg", [P, 2])
        st6b = sb("st6b", [P, QT, 6]); mvb = sb("mvb", [P, 2, QT, 2]); vpeb = sb("vpeb", [P, QT]); rstdb = sb("rstdb", [P, QT]); mnegb = sb("mnegb", [P, QT]); nmrb = sb("nmrb", [P, QT])

        bank = [ctx.enter_context(nc.psum_tensor(f"bank{i}", [P, 512], F32)) for i in range(8)]

        def tiles2(i):
            return bank[i][:].rearrange("p (a s) -> p a s", a=2)

        qk_ps = [tiles2(0), tiles2(1)]
        tp_ps = [tiles2(2), tiles2(3)]
        pv_ps = bank[4][:, 0:S]
        gs_ps = bank[7][:, 0:2 * R]
        prep_a, prep_b, tail_ps = tiles2(5), tiles2(6), tiles2(7)

        s_load = sem("s_load"); s_const = sem("s_const"); s_dve0 = sem("s_dve0"); s_red = sem("s_red"); s_sin = sem("s_sin"); s_emb = sem("s_emb")
        s_act0 = sem("s_act0"); s_adaps = sem("s_adaps"); s_setup = sem("s_setup")
        s_gcol = sem("s_gcol"); s_gram = sem("s_gram"); s_gii = sem("s_gii"); s_gnrm = sem("s_gnrm"); s_gp = sem("s_gp"); s_gself = sem("s_gself")
        s_rm = sem("s_rm"); s_rmc = sem("s_rmc")
        s_x = [sem("s_x0"), sem("s_x1")]; s_mk = [sem("s_mk0"), sem("s_mk1")]; s_bias = [sem(f"s_bias{i}") for i in range(RING)]
        s_wq_d = sem("s_partq_out"); s_wk_d = sem("s_partk_out"); s_stq = [sem("s_stackq0"), sem("s_stackq1")]; s_stk = [sem("s_stackk0"), sem("s_stackk1")]
        s_x2st = [sem("s_x2st0"), sem("s_x2st1")]
        s_maskv = sem("s_maskv"); s_masked = sem("s_masked"); s_pool = sem("s_pool"); s_rstd = sem("s_rstd")
        s_stats6 = sem("s_stats6"); s_stats = sem("s_stats"); s_reduced = sem("s_reduced"); s_ptd = sem("s_ptd"); s_xT = sem("s_xT")
        s_r1 = sem("s_r1"); s_p3 = sem("s_p3"); s_v = sem("s_v"); s_xres = sem("s_xres"); s_rec = sem("s_rec"); s_ctxn = sem("s_ctxn"); s_x2 = sem("s_x2")
        s_xn = sem("s_xn"); s_exp = sem("s_exp"); s_pta = sem("s_pta"); s_p1 = sem("s_p1"); s_p2 = sem("s_p2"); s_pvc = sem("s_pvc"); s_ctxT = sem("s_ctxT")
        s_qk = sem("s_qk"); s_tp = sem("s_tp"); s_pv = sem("s_pv"); s_xtp = sem("s_xtp"); s_qp = sem("s_qp"); s_kp = sem("s_kp"); s_vp = sem("s_vp"); s_xb = sem("s_xb")
        s_cn = sem("s_cn"); s_cT = sem("s_cT"); s_o = sem("s_o")
        s_y = [sem("s_y0"), sem("s_y1")]; s_out = [sem("s_out0"), sem("s_out1")]
        s2_six = sem("s2_six"); s2_stats = sem("s2_stats"); s2_pool = sem("s2_pool"); s2_rstd = sem("s2_rstd"); s2_yb = sem("s2_yb"); s2_yn = sem("s2_yn")
        s2_yt = sem("s2_yt"); s2_hT = sem("s2_hT"); s2_up = sem("s2_up"); s2_th = sem("s2_th"); s2_u = sem("s2_u"); s2_ua = sem("s2_ua"); s2_w = sem("s2_w"); s2_wl = sem("s2_wl"); s2_hf = sem("s2_hf"); s2_hl = sem("s2_hl"); s2_gh = sem("s2_gh"); s2_gl = sem("s2_gl"); s2_g = sem("s2_g"); s2_dn = sem("s2_dn")
        s2_hid = sem("s2_hid"); s2_hidp = sem("s2_hidp"); s2_hidT = sem("s2_hidT"); s2_r = sem("s2_r"); s2_h1p = sem("s2_h1p"); s2_h1 = sem("s2_h1"); s2_zp = sem("s2_zp")
        s2_z = sem("s2_z"); s2_str = sem("s2_str"); s2_rs = sem("s2_rs"); s2_fin = sem("s2_fin")

        loads = [
            (xt[:, 0], x[0].rearrange("(t p) d -> p t d", p=P), s_x[0]), (xt[:, 1], x[1].rearrange("(t p) d -> p t d", p=P), s_x[1]),
            (frq[:], freqs.rearrange("(p a) -> p a", a=1)), (tti[:], itok.partition_broadcast(P)),
            (wada[:], W_ada.rearrange("(c p) n -> p c n", p=P)), (bada[:], b_ada),
            (uv[:, 0], U.rearrange("(c p) r -> p c r", p=P)), (uv[:, 1], V.rearrange("(c p) r -> p c r", p=P)),
            (wq[:], Wq.rearrange("(c p) n -> p c n", p=P)), (wk[:], Wk.rearrange("(c p) n -> p c n", p=P)),
            (wv[:], Wv.rearrange("(c p) n -> p c n", p=P)), (wo[:], Wo.rearrange("(c p) n -> p c n", p=P)),
            (bqk[:, 0], bq), (bqk[:, 1], bk), (bvb[:], bv.partition_broadcast(P)), (bob[:], bo.partition_broadcast(P)),
            (w1[:], W1.rearrange("(c p) n -> p c n", p=P)), (w2[:], W2.rearrange("(c p) n -> p c n", p=P)),
            (b1c[:], b1), (g2c[:], g2), (be2c[:], beta2), (b2b[:], b2.partition_broadcast(P)),
            (cb[:], resp_b.partition_broadcast(P)), (cb2[:], safety_bias.partition_broadcast(P)),
            (scr[:], score.partition_broadcast(P)), (gw1[:], gate_w1T.rearrange("(c p) n -> p c n", p=P)),
            (gb1[:], gate_b1.rearrange("(p a) -> p a", a=1)), (gw2[:], gate_w2T), (gb2[:], gate_b2.partition_broadcast(P)),
            (respT[:], resp_wT),
        ]
        n_loads = sum(1 for a in loads if len(a) == 2)

        def x_view(b):
            return x[bass.ds(b.n, 1)].rearrange("a (t p) d -> p (a t) d", p=P)

        def bias_chunk(b, c, qt):
            return fside[bass.ds(b.n, 1), c * CH:(c + 1) * CH, qt * P:(qt + 1) * P, :].rearrange("a h p k -> p (a h) k")

        def free_pT(eng, b, h):
            g = h // HG
            if b.i is not None or NG * b.off + g >= 2:
                eng.wait_ge(s_pv, NG * b.n + g - 1)

        block = ctx.enter_context(nc.Block())

        @block.sync
        def _(sp):
            for dst, src, *own in loads:
                sp.dma_start(dst, src).then_inc(own[0] if own else s_load, 16)

            def load_mask(b):
                sp.dma_start(mk[:, b.par], mask[bass.ds(b.n, 1)].rearrange("a c (t p) k -> p (a c t) k", p=P)).then_inc(s_mk[b.par], 16)

            def load_bias(b, c):
                slot = 2 * b.par + c
                for qt in range(QT):
                    sp.dma_start(ring[:, slot, qt], bias_chunk(b, c, qt)).then_inc(s_bias[slot], 16)

            def restack(b):
                for t, (s_written, s_back) in enumerate(((s_wq_d, s_stq), (s_wk_d, s_stk))):
                    sp.wait_ge(s_p3, 2 * b.n + t + 1)
                    sp.dma_start(parts_d[b.par, t].rearrange("a p n -> p a n"),
                                 parts[:, t].rearrange("p a c s -> p a (c s)")).then_inc(s_written, 16)
                    sp.wait_ge(s_written, 16 * b.n + 16)
                    for row, n, part, step in RUNS[t]:
                        src = parts_d[b.par, t].rearrange("a (d j) n -> a d (j n)", d=HD)
                        src = src[part:part + n] if step else src[part:part + 1].to_broadcast([n, HD, H * S])
                        sp.dma_start(stack[HD * row:HD * (row + n), b.par, t].rearrange("p h s -> p (h s)"), src).then_inc(s_back[b.par], 16)

            def load_x(b):
                sp.wait_ge(s_xn, b.n - 1)
                sp.dma_start(xt[:, b.par], x_view(b)).then_inc(s_x[b.par], 16)

            load_mask(Batch(0))
            load_mask(Batch(1))
            load_bias(Batch(0), 0)
            load_bias(Batch(0), 1)
            restack(Batch(0))
            load_bias(Batch(1), 0)
            load_x(Batch(2))

            def store_x2(b):
                sp.wait_ge(s_x2, b.n + 1)
                sp.dma_start(x2_d[bass.ds(b.n, 1)].rearrange("a (t p) d -> p (a t) d", p=P), x2s[:, b.par]).then_inc(s_x2st[b.par], 16)

            def body(b, n):
                if n is None or n + 3 < B:
                    load_x(b.plus(3))
                if n is None or n + 1 < B:
                    if n is None or n >= 1:
                        sp.wait_ge(s_tp, H * b.n)
                    load_bias(b.plus(1), 1)
                if n is None or n + 2 < B:
                    sp.wait_ge(s_maskv, b.n + 1)
                    sp.nop(nofuse=True)
                    load_mask(b.plus(2))
                if n is None or n + 1 < B:
                    restack(b.plus(1))
                if n is None or n + 2 < B:
                    sp.wait_ge(s_tp, H * b.n + CH)
                    load_bias(b.plus(2), 0)
                if n is None or n >= 1:
                    store_x2(b.plus(-1))

            run_batches(sp, 0, 3, B - 3, B, body)
            store_x2(Batch(B - 1))

            def load_y(b):
                sp.wait_ge(s_x2st[b.par], 16 * b.half + 16)
                sp.dma_start(y2[:, b.par], x2_d[bass.ds(b.n, 1)].rearrange("a (t p) d -> p (a t) d", p=P)).then_inc(s_y[b.par], 16)

            def store_out(b):
                sp.wait_ge(s2_fin, b.n + 1)
                sp.dma_start(out[bass.ds(b.n, 1)].rearrange("a (t p) d -> p (a t) d", p=P), fin[:, b.par]).then_inc(s_out[b.par], 16)

            sp.wait_ge(s_qk, H * B)
            sp.wait_ge(s_pv, NG * B)
            load_y(Batch(0))
            load_y(Batch(1))

            def body2(b, n):
                if n is None or n + 2 < B:
                    sp.wait_ge(s2_yn, b.n + 1)
                    sp.wait_ge(s2_yb, b.n + 1)
                    load_y(b.plus(2))
                if n is None or n >= 2:
                    store_out(b.plus(-2))

            run_batches(sp, 0, 3, B - 3, B + 2, body2)
            for par in range(2):
                sp.wait_ge(s_out[par], 16 * B // 2)

        @block.gpsimd
        def _(pool):
            nc.gpsimd.memset(ident[:], 0.0)
            nc.gpsimd.memset(later[:], 1.0)
            nc.gpsimd.memset(expo[:, 0], -0.5)
            nc.gpsimd.memset(expo[:, 1], 0.5).then_inc(s_gp, 1)
            pool.wait_ge(s_gp, 1)
            nc.gpsimd.affine_select(out=ident[:], in_=ident[:], compare_op=ALU.not_equal, fill=1.0, base=0,
                                    pattern=[[-1, P]], channel_multiplier=1)
            nc.gpsimd.affine_select(out=later[:], in_=later[:], compare_op=ALU.is_gt, fill=0.0, base=0,
                                    pattern=[[-1, R], [1, R]], channel_multiplier=0).then_inc(s_const, 1)
            pool.wait_ge(s_const, 1)

            def gs_norm(i):
                pool.wait_ge(s_gii, i + 1)
                nc.gpsimd.tensor_tensor(nrm[:], gii[:], expo[:, 1], ALU.pow).then_inc(s_gp, 1)
                pool.wait_ge(s_gp, i + 2)
                pool.nop(nofuse=True)
                nc.gpsimd.tensor_scalar(nrme[:], nrm[:], GS_EPS, 1.0, ALU.add, ALU.mult).then_inc(s_gnrm, 1)

            def inv_std(b):
                pool.wait_ge(s_stats, b.n + 1)
                pool.nop(nofuse=True)
                nc.gpsimd.tensor_scalar(vpe[:], mv[:, :, 1], LN_EPS, 1.0, ALU.add, ALU.mult)
                nc.gpsimd.tensor_scalar(mneg[:], mv[:, :, 0], -1.0, 1.0, ALU.mult, ALU.mult).then_inc(s_pool, 1)
                pool.wait_ge(s_pool, 2 * b.n + 1)
                if b.i is not None or b.off >= 1:
                    pool.wait_ge(s_xn, b.n)
                nc.gpsimd.tensor_tensor(rstd[:], vpe[:], expo[:, 0], ALU.pow).then_inc(s_pool, 1)
                pool.wait_ge(s_pool, 2 * b.n + 2)
                nc.gpsimd.tensor_tensor(nmr[:], mneg[:], rstd[:], ALU.mult).then_inc(s_rstd, 1)

            def mask_values(b):
                pool.wait_ge(s_mk[b.par], 16 * b.half + 16)
                if b.i is not None or b.off >= 1:
                    pool.wait_ge(s_masked, 2 * NG * b.n)
                pool.nop(nofuse=True)
                nc.gpsimd.tensor_scalar(maskv[:], mk[:, b.par], MASKED, 1.0, ALU.mult, ALU.mult).then_inc(s_maskv, 1)
                pool.wait_ge(s_maskv, b.n + 1)

            def add_mask(b, g):
                slot, h0 = 2 * b.par + g // 2, (g % 2) * HG
                if g % 2 == 0:
                    pool.wait_ge(s_bias[slot], 32 * b.half + 32)
                for qt in range(QT):
                    v = ring[:, slot, qt, h0:h0 + HG]
                    m = maskv[:, qt:qt + 1].to_broadcast([P, HG, S])
                    nc.gpsimd.tensor_tensor(v, v, m, ALU.add).then_inc(s_masked, 1)

            inv_std(Batch(0))
            inv_std(Batch(1))

            def body(b, n):
                mask_values(b)
                add_mask(b, 0)
                add_mask(b, 1)
                if n is None or n + 2 < B:
                    inv_std(b.plus(2))
                add_mask(b, 2)
                gs_norm(b.n)
                add_mask(b, 3)

            run_batches(pool, 0, 3, B - 3, B, body)

            def inv_std2(b):
                pool.wait_ge(s2_stats, b.n + 1)
                if b.i is not None or b.off >= 1:
                    pool.wait_ge(s2_rstd, b.n)
                pool.nop(nofuse=True)
                nc.gpsimd.tensor_scalar(vpeb[:], mvb[:, b.par, :, 1], LN_EPS, 1.0, ALU.add, ALU.mult)
                nc.gpsimd.tensor_scalar(mnegb[:], mvb[:, b.par, :, 0], -1.0, 1.0, ALU.mult, ALU.mult).then_inc(s2_pool, 1)
                pool.wait_ge(s2_pool, 2 * b.n + 1)
                if b.i is not None or b.off >= 1:
                    pool.wait_ge(s2_yn, b.n)
                nc.gpsimd.tensor_tensor(rstdb[:], vpeb[:], expo[:, 0], ALU.pow).then_inc(s2_pool, 1)
                pool.wait_ge(s2_pool, 2 * b.n + 2)
                nc.gpsimd.tensor_tensor(nmrb[:], mnegb[:], rstdb[:], ALU.mult).then_inc(s2_rstd, 1)
                if b.i is not None or b.off >= 2:
                    pool.wait_ge(s2_hid, b.n - 1)
                nc.gpsimd.tensor_tensor(yb[:, b.par], y2[:, b.par], b2b[:].unsqueeze(1).to_broadcast([P, QT, D]), ALU.add).then_inc(s2_yb, 1)

            run_batches(pool, 0, 4, B, B, lambda b, n: inv_std2(b))

        @block.vector
        def _(dve):
            chain = [0]

            def link(ins):
                chain[0] += 1
                ins.then_inc(s_dve0, 1)
                dve.wait_ge(s_dve0, chain[0])

            nc.vector.memset(vt[:, :, :, :, HD:VW], 0.0)
            link(nc.vector.memset(strg[:], 0.0))
            nc.vector.memset(vt[:, :, :, :, HD:HD + 1], 1.0)

            def stats(b):
                dve.wait_ge(s_x[b.par], 16 * b.half + 16)
                if b.i is not None or b.off >= 1:
                    dve.wait_ge(s_rstd, b.n)
                for t in range(QT):
                    ins = nc.vector.bn_stats(st6[:, t], xt[:, b.par, t])
                ins.then_inc(s_stats6, 1)

            def stats_end(b):
                dve.wait_ge(s_stats6, b.n + 1)
                dve.nop(nofuse=True)
                for t in range(QT):
                    ins = nc.vector.bn_aggr(mv[:, t], st6[:, t])
                ins.then_inc(s_stats, 1)

            stats(Batch(0))
            stats_end(Batch(0))
            dve.wait_ge(s_const, 1)
            dve.wait_ge(s_load, 16 * n_loads)
            nc.vector.tensor_scalar(wq[:], wq[:], HD ** -0.5, None, ALU.mult)
            nc.vector.tensor_scalar(bqk[:, 0], bqk[:, 0], HD ** -0.5, None, ALU.mult)
            nc.vector.tensor_scalar(w2[:], w2[:], 0.5, None, ALU.mult)
            nc.vector.tensor_scalar(b1t[:], b1c[:], 0.5 * GELU_A, None, ALU.mult)
            nc.vector.tensor_scalar(gb2h[:], gb2[:], 0.5, None, ALU.mult)
            nc.vector.tensor_tensor(cb[:], cb[:], cb2[:], ALU.add)
            link(nc.vector.tensor_copy(ttf[:], tti[:]))
            link(nc.vector.tensor_scalar(ang[:], ttf[:], 40.0, frq[:, 0:1], ALU.mult, ALU.mult))
            nc.vector.tensor_scalar(turns[:, 0], ang[:], 1.0 / TWO_PI, None, ALU.mult)
            link(nc.vector.tensor_scalar(turns[:, 1], ang[:], 1.0 / TWO_PI, 0.25, ALU.mult, ALU.add))
            link(nc.vector.tensor_scalar(turns[:], turns[:], MAGIC, None, ALU.add))
            link(nc.vector.tensor_scalar(turns[:], turns[:], -MAGIC, None, ALU.add))
            link(nc.vector.scalar_tensor_tensor(red[:], turns[:], -C1, ang[:].unsqueeze(1).to_broadcast([P, 2, B]), ALU.mult, ALU.add))
            link(nc.vector.scalar_tensor_tensor(red2[:], turns[:], -C2, red[:], ALU.mult, ALU.add))
            link(nc.vector.scalar_tensor_tensor(red[:], turns[:], -C3, red2[:], ALU.mult, ALU.add))
            link(nc.vector.tensor_scalar(red[:, 1], red[:, 1], float(np.pi / 2), None, ALU.add))
            nc.vector.tensor_scalar(red[:], red[:], PI_IN, -PI_IN, ALU.min, ALU.max).then_inc(s_red, 1)
            dve.wait_ge(s_sin, 1)
            link(nc.vector.scalar_tensor_tensor(emb[:], sct[:], 1.0, sc[:], ALU.add, ALU.mult))
            nc.vector.tensor_scalar(emb[:], emb[:], 0.5, None, ALU.mult).then_inc(s_emb, 1)
            nc.vector.tensor_scalar(modh[:], modt[:], 0.25, 0.25, ALU.mult, ALU.add)
            dve.wait_ge(s_adaps, 1)
            for c in range(DC):
                nc.vector.tensor_scalar(adaS[:, c], bank[7][:, c * B:(c + 1) * B], bada[:, c:c + 1], 1.0, ALU.add, ALU.add)
            for c in range(DC):
                link(nc.vector.tensor_scalar(adaB[:, c], bank[7][:, (DC + c) * B:(DC + c + 1) * B], bada[:, DC + c:DC + c + 1], None, ALU.add))

            link(nc.vector.memset(gii[:], 0.0))
            nc.vector.memset(pooled[:], 0.0).then_inc(s_setup, 1)

            def column(i):
                return uv[:, :, :, bass.ds(i, 1)].rearrange("p a c r -> p a (c r)")

            def gs_column(i, first):
                if not first:
                    dve.wait_ge(s_gself, 4 * i)
                nc.vector.tensor_copy(ucol[:], column(i)).then_inc(s_gcol, 1)

            def gs_products(i):
                dve.wait_ge(s_gram, i + 1)
                nc.vector.tensor_copy(gii[:], gs_ps.rearrange("p (a r) -> p a r", a=2)[:, :, bass.ds(i, 1)].rearrange("p a r -> p (a r)"))
                nc.vector.tensor_copy(gsb[:], gs_ps.rearrange("p (a r) -> p a r", a=2)).then_inc(s_gii, 1)

            def gs_reciprocal(i):
                dve.wait_ge(s_gnrm, i + 1)
                nc.vector.reciprocal(rnrm[:], nrme[:]).then_inc(s_gself, 1)

            def gs_coefficients(i):
                dve.wait_ge(s_gii, i + 1)
                dve.wait_ge(s_gself, 4 * i + 1)
                for a in range(2):
                    nc.vector.scalar_tensor_tensor(coef[:, a], gsb[:, a], rnrm[:, a:a + 1],
                                                   later[:, bass.ds(i, 1)].rearrange("p a r -> p (a r)"), ALU.mult, ALU.mult)
                    ins = nc.vector.tensor_scalar(qneg[:, a], ucol[:, a], rnrm[:, a:a + 1], -1.0, ALU.mult, ALU.mult)
                ins.then_inc(s_gself, 1)

            def gs_update(i):
                dve.wait_ge(s_gself, 4 * i + 2)
                for a in range(2):
                    for c in range(DC):
                        ins = nc.vector.scalar_tensor_tensor(uv[:, a, c], coef[:, a], qneg[:, a, c:c + 1], uv[:, a, c], ALU.mult, ALU.add)
                ins.then_inc(s_gself, 1)

            def gs_write(i):
                dve.wait_ge(s_gself, 4 * i + 3)
                nc.vector.tensor_scalar(column(i), qneg[:], -1.0, None, ALU.mult).then_inc(s_gself, 1)

            def response_matrix():
                dve.wait_ge(s_rm, 1)
                nc.vector.tensor_copy(gram[:], bank[0][0:R, 0:R])
                nc.vector.tensor_copy(t1[:], bank[1][0:R, 0:D])
                nc.vector.tensor_copy(uoT[:], bank[2][0:R, 0:D]).then_inc(s_rmc, 1)
                dve.wait_ge(s_rm, 2)
                nc.vector.tensor_copy(t2[:], bank[3][0:R, 0:D]).then_inc(s_rmc, 1)
                dve.wait_ge(s_rm, 3)
                nc.vector.tensor_copy(resp_m[:], tiles2(7)).then_inc(s_rmc, 1)

            stats(Batch(1))
            stats_end(Batch(1))

            def reduce_head(b, h):
                slot = 2 * b.par + h // CH
                dve.wait_ge(s_qk, H * b.n + h + 1)
                for qt in range(QT):
                    v = ring[:, slot, qt, h % CH]
                    if h % HG == 0:
                        dve.wait_ge(s_masked, 2 * NG * b.n + 2 * (h // HG) + qt + 1)
                    dve.nop(nofuse=True)
                    nc.vector.tensor_tensor_reduce(out=v, in0=qk_ps[h % 2][:, qt], in1=v, scale=-1.0, scalar=ROW_MAX_NEG,
                                                   op0=ALU.add, op1=ALU.min, accum_out=nmax[:, b.par, h, qt:qt + 1]).then_inc(s_reduced, 1)

            def copy_pT(b, h):
                dve.wait_ge(s_tp, H * b.n + h + 1)
                free_pT(dve, b, h)
                nc.vector.tensor_copy(pT[:, h % (2 * HG)], tp_ps[h % 2]).then_inc(s_ptd, 1)

            def xT_out(b):
                dve.wait_ge(s_xtp, b.n + 1)
                for c in range(DC):
                    ins = nc.vector.tensor_scalar(xT[:, c], prep_b[:, c], adaS[:, c, bass.ds(b.n, 1)], adaB[:, c, bass.ds(b.n, 1)], ALU.mult, ALU.add)
                ins.then_inc(s_xT, 1)

            def rest1(b, t):
                ps = prep_b if t == 0 else prep_a
                dve.wait_ge(s_p1, 2 * b.n + t + 1)
                for c in range(DC):
                    ins = nc.vector.scalar_tensor_tensor(ps[:, c], ps[:, c], bqk[:, t, c:c + 1], parts[:, t, 0, c], ALU.add, ALU.subtract)
                ins.then_inc(s_r1, 1)

            def rest2(b, t):
                ps = prep_b if t == 0 else prep_a
                dve.wait_ge(s_p2, 2 * b.n + t + 1)
                nc.vector.tensor_tensor(parts[:, t, 2], ps, parts[:, t, 1], ALU.subtract).then_inc(s_p3, 1)

            def v_out(b):
                dve.wait_ge(s_vp, b.n + 1)
                for t in range(QT):
                    ins = nc.vector.tensor_tensor(vt[:, b.par, t, :, 0:HD], prep_b[:, t].rearrange("p (h d) -> p h d", d=HD),
                                                  bvb[:].rearrange("p (h d) -> p h d", d=HD), ALU.add)
                ins.then_inc(s_v, 1)

            def xres_out(b):
                dve.wait_ge(s_xb, b.n + 1)
                if b.i is not None or b.off >= 2:
                    dve.wait_ge(s_x2, b.n - 1)
                nc.vector.tensor_tensor(xres[:, b.par], prep_a, bob[:].unsqueeze(1).to_broadcast([P, QT, D]), ALU.add).then_inc(s_xres, 1)

            def normalise_ctx(b, qt):
                dve.wait_ge(s_cn, 2 * b.n + qt + 1)
                heads = bank[7][:].rearrange("p (h w) -> p h w", w=VW)
                nc.vector.reciprocal(rec[:, qt].unsqueeze(2), heads[:, :, HD:HD + 1]).then_inc(s_rec, 1)
                dve.wait_ge(s_rec, 2 * b.n + qt + 1)
                nc.vector.tensor_tensor(ctxn[:, qt].rearrange("p (h d) -> p h d", d=HD), heads[:, :, 0:HD],
                                        rec[:, qt].unsqueeze(2).to_broadcast([P, H, HD]), ALU.mult).then_inc(s_ctxn, 1)

            def x2_out(b):
                dve.wait_ge(s_o, b.n + 1)
                if b.i is not None or b.off >= 2:
                    dve.wait_ge(s_x2st[b.par], 16 * b.half)
                dve.wait_ge(s_xres, b.n + 1)
                nc.vector.tensor_tensor(x2s[:, b.par], tail_ps, xres[:, b.par], ALU.add).then_inc(s_x2, 1)

            def prep_all(b):
                xT_out(b)
                rest1(b, 0)
                rest2(b, 0)
                rest1(b, 1)
                rest2(b, 1)
                v_out(b)
                xres_out(b)

            prep_all(Batch(0))
            xT_out(Batch(1))

            def body(b, n):
                main = n is None or n < B
                prep = n is None or n + 1 < B
                tail = n is None or n >= 1
                for h in range(H):
                    if main:
                        reduce_head(b, h)
                    at = behind(b, n, h, 3)
                    if at and at[1] in DVE_HEADS:
                        copy_pT(*at)
                    if prep:
                        if h == 3:
                            rest1(b.plus(1), 0)
                        if h == 5:
                            rest1(b.plus(1), 1)
                            rest2(b.plus(1), 0)
                        if h == 7:
                            rest2(b.plus(1), 1)
                        if h == 9:
                            v_out(b.plus(1))
                    if n is None or n + 2 < B:
                        if h == 1:
                            stats(b.plus(2))
                        if h == 2:
                            stats_end(b.plus(2))
                        if h == 11:
                            xT_out(b.plus(2))
                    if tail:
                        if h == 6:
                            normalise_ctx(b.plus(-1), 0)
                        if h == 8:
                            normalise_ctx(b.plus(-1), 1)
                        if h == 14:
                            x2_out(b.plus(-1))
                    if prep and h == 15:
                        xres_out(b.plus(1))
                    if main:
                        if h == 0:
                            gs_column(b.n, n == 0)
                        if h == 2:
                            gs_products(b.n)
                        if h == 10:
                            gs_reciprocal(b.n)
                        if h == 11:
                            gs_coefficients(b.n)
                        if h == 12:
                            gs_update(b.n)
                        if h == 13:
                            gs_write(b.n)

            run_batches(dve, 0, 3, B - 3, B + 1, body)
            last = Batch(B - 1)
            response_matrix()

            def stats2(b):
                dve.wait_ge(s_y[b.par], 16 * b.half + 16)
                if b.i is not None or b.off >= 1:
                    dve.wait_ge(s2_stats, b.n)
                for t in range(QT):
                    ins = nc.vector.bn_stats(st6b[:, t], y2[:, b.par, t])
                ins.then_inc(s2_six, 1)
                dve.wait_ge(s2_six, b.n + 1)
                if b.i is not None or b.off >= 2:
                    dve.wait_ge(s2_rstd, b.n - 1)
                dve.nop(nofuse=True)
                dve.nop(nofuse=True)
                for t in range(QT):
                    ins = nc.vector.bn_aggr(mvb[:, b.par, t], st6b[:, t])
                ins.then_inc(s2_stats, 1)

            def split_weights():
                for k, (w, (high, rest)) in enumerate(((w1, w1s), (w2, w2s))):
                    dve.wait_ge(s2_w, k + 1)
                    nc.vector.tensor_tensor(rest, w[:], f32(high), ALU.subtract).then_inc(s2_wl, 1)

            def hT_rest(b):
                dve.wait_ge(s2_hT, b.n + 1)
                if b.i is not None or b.off >= 2:
                    dve.wait_ge(s2_up, 4 * (b.n - 1))
                nc.vector.tensor_tensor(hTs[1][:, b.par], hT, f32(hTs[0][:, b.par]), ALU.subtract).then_inc(s2_hl, 1)

            def gate_pair(b, j):
                dve.wait_ge(s2_th, 4 * b.n + j + 1)
                if j in U_ACT:
                    dve.wait_ge(s2_ua, u_done(True, b, j))
                else:
                    if b.i is not None or b.off >= 1:
                        dve.wait_ge(s2_g, 4 * (b.n - 1) + j + 1)
                    for f in range(2):
                        ins = nc.vector.tensor_scalar(up[:, j, f], tiles2(j)[:, f], b1c[:, 2 * j + f:2 * j + f + 1], None, ALU.add)
                    ins.then_inc(s2_u, 1)
                    dve.wait_ge(s2_u, u_done(False, b, j))
                if b.i is not None or b.off >= 1:
                    dve.wait_ge(s2_gl, 4 * (b.n - 1) + j + 1)
                nc.vector.scalar_tensor_tensor(gT[:, 2 * j:2 * j + 2], th[:, j], 1.0, up[:, j], ALU.add, ALU.mult).then_inc(s2_g, 1)

            def gT_rest(b, j):
                dve.wait_ge(s2_gh, 4 * b.n + j + 1)
                if b.i is not None or b.off >= 2:
                    dve.wait_ge(s2_dn, b.n - 1)
                pair = slice(2 * j, 2 * j + 2)
                nc.vector.tensor_tensor(gTs[1][:, b.par, pair], gT[:, pair], f32(gTs[0][:, b.par, pair]), ALU.subtract).then_inc(s2_gl, 1)

            def hid_out(b):
                dve.wait_ge(s2_dn, b.n + 1)
                dve.wait_ge(s2_yb, b.n + 1)
                if b.i is not None or b.off >= 2:
                    dve.wait_ge(s2_fin, b.n - 1)
                nc.vector.tensor_tensor(hid[:, b.par], tiles2(4), yb[:, b.par], ALU.add).then_inc(s2_hid, 1)

            def strength(b):
                dve.wait_ge(s2_z, b.n + 1)
                if b.i is not None or b.off >= 1:
                    dve.wait_ge(s2_fin, b.n)
                nc.vector.tensor_scalar(strg[:, b.par:b.par + 1], gth[:], 1.0, modh[:, bass.ds(b.n, 1)], ALU.add, ALU.mult).then_inc(s2_str, 1)

            def rsp_out(b):
                dve.wait_ge(s2_r, b.n + 1)
                if b.i is not None or b.off >= 1:
                    dve.wait_ge(s2_fin, b.n)
                nc.vector.tensor_tensor(rsp[:], tiles2(7), cb[:].unsqueeze(1).to_broadcast([P, QT, D]), ALU.add).then_inc(s2_rs, 1)

            def fin_out(b):
                dve.wait_ge(s2_hid, b.n + 1)
                dve.wait_ge(s2_rs, b.n + 1)
                dve.wait_ge(s2_str, b.n + 1)
                if b.i is not None or b.off >= 2:
                    dve.wait_ge(s_out[b.par], 16 * b.half)
                nc.vector.scalar_tensor_tensor(fin[:, b.par], rsp[:], strg[:, b.par:b.par + 1], hid[:, b.par], ALU.mult, ALU.add).then_inc(s2_fin, 1)

            dve.wait_ge(s_tp, H * B)
            stats2(Batch(0))
            stats2(Batch(1))
            split_weights()
            hT_rest(Batch(0))

            def body2(b, n):
                main = n is None or n < B
                tail = n is None or 1 <= n <= B
                tail2 = n is None or n >= 2
                if main:
                    gate_pair(b, 0)
                if tail:
                    gT_rest(b.plus(-1), 3)
                if main:
                    gate_pair(b, 1)
                    gT_rest(b, 0)
                    if n is None or n + 1 < B:
                        hT_rest(b.plus(1))
                    if n is None or n + 2 < B:
                        stats2(b.plus(2))
                if tail2:
                    rsp_out(b.plus(-2))
                if tail:
                    hid_out(b.plus(-1))
                if tail2:
                    strength(b.plus(-2))
                    fin_out(b.plus(-2))
                if main:
                    gate_pair(b, 2)
                    gT_rest(b, 1)
                    gate_pair(b, 3)
                    gT_rest(b, 2)

            run_batches(dve, 0, 3, B - 3, B + 2, body2)

        @block.scalar
        def _(act):
            act.wait_ge(s_red, 1)
            nc.scalar.activation(sc[:], red[:], ACT.Sin).then_inc(s_act0, 1)
            act.wait_ge(s_act0, 1)
            nc.scalar.activation(modt[:], scr[:], ACT.Tanh, scale=0.5)
            nc.scalar.activation(sct[:], sc[:], ACT.Tanh, scale=0.5).then_inc(s_sin, 1)

            def xn_out(b):
                act.wait_ge(s_rstd, b.n + 1)
                act.wait_ge(s_x[b.par], 16 * b.half + 16)
                if b.i is not None or b.off >= 1:
                    act.wait_ge(s_xtp, b.n)
                for t in range(QT):
                    ins = nc.scalar.activation(xn[:, t], xt[:, b.par, t], ACT.Identity, bias=nmr[:, t:t + 1], scale=rstd[:, t:t + 1])
                ins.then_inc(s_xn, 1)

            def exp_head(b, h):
                slot = 2 * b.par + h // CH
                for qt in range(QT):
                    v = ring[:, slot, qt, h % CH]
                    act.wait_ge(s_reduced, 2 * H * b.n + 2 * h + qt + 1)
                    nc.scalar.activation(v, v, ACT.Exp, bias=nmax[:, b.par, h, qt:qt + 1], scale=-1.0).then_inc(s_exp, 1)

            def copy_pT(b, h):
                act.wait_ge(s_tp, H * b.n + h + 1)
                free_pT(act, b, h)
                nc.scalar.activation(pT[:, h % (2 * HG)], tp_ps[h % 2], ACT.Copy).then_inc(s_pta, 1)

            def part1(b, t):
                ps = prep_b if t == 0 else prep_a
                act.wait_ge(s_qp if t == 0 else s_kp, b.n + 1)
                if b.i is not None or b.off >= 1:
                    act.wait_ge(s_wq_d if t == 0 else s_wk_d, 16 * b.n)
                for c in range(DC):
                    ins = nc.scalar.activation(parts[:, t, 0, c], ps[:, c], ACT.Identity, bias=bqk[:, t, c:c + 1])
                ins.then_inc(s_p1, 1)

            def part2(b, t):
                ps = prep_b if t == 0 else prep_a
                act.wait_ge(s_r1, 2 * b.n + t + 1)
                nc.scalar.activation(parts[:, t, 1], ps, ACT.Copy).then_inc(s_p2, 1)

            def pv_out(b, g):
                act.wait_ge(s_pv, NG * b.n + g + 1)
                if g == 0 and (b.i is not None or b.off >= 1):
                    act.wait_ge(s_cn, 2 * b.n)
                nc.scalar.activation(pv_sb[:, g], pv_ps, ACT.Copy).then_inc(s_pvc, 1)

            def ctxT_out(b):
                act.wait_ge(s_cT, b.n + 1)
                nc.scalar.activation(ctxT[:], tail_ps, ACT.Copy).then_inc(s_ctxT, 1)

            def prep_parts(b):
                for t in range(2):
                    part1(b, t)
                    part2(b, t)

            act.wait_ge(s_setup, 1)
            xn_out(Batch(0))
            prep_parts(Batch(0))
            xn_out(Batch(1))

            def body(b, n):
                prep = n is None or n + 1 < B
                tail = n is None or n >= 1
                for h in range(H):
                    at = behind(b, n, h, 1)
                    if at:
                        exp_head(*at)
                    at = behind(b, n, h, 3)
                    if at and at[1] in ACT_HEADS:
                        copy_pT(*at)
                    at = behind(b, n, h, 8)
                    if at and at[1] % HG == 0:
                        pv_out(at[0], at[1] // HG)
                    if prep:
                        if h == 1:
                            part1(b.plus(1), 0)
                        if h == 3:
                            part1(b.plus(1), 1)
                        if h == 4:
                            part2(b.plus(1), 0)
                        if h == 6:
                            part2(b.plus(1), 1)
                    if tail and h == 10:
                        ctxT_out(b.plus(-1))
                    if h == 8 and (n is None or n + 2 < B):
                        xn_out(b.plus(2))

            run_batches(act, 0, 3, B - 3, B + 1, body)
            last = Batch(B - 1)

            def yn_out(b):
                act.wait_ge(s2_rstd, b.n + 1)
                act.wait_ge(s_y[b.par], 16 * b.half + 16)
                if b.i is not None or b.off >= 1:
                    act.wait_ge(s2_yt, b.n)
                for t in range(QT):
                    ins = nc.scalar.activation(yn[:, t], y2[:, b.par, t], ACT.Identity, bias=nmrb[:, t:t + 1], scale=rstdb[:, t:t + 1])
                ins.then_inc(s2_yn, 1)

            def split_weights():
                act.wait_ge(s_tp, H * B)
                act.wait_ge(s_pv, NG * B)
                for w, (high, rest) in ((w1, w1s), (w2, w2s)):
                    nc.scalar.activation(high, w[:], ACT.Copy).then_inc(s2_w, 1)

            def hT_out(b):
                act.wait_ge(s2_yt, b.n + 1)
                if b.i is not None or b.off >= 1:
                    act.wait_ge(s2_hl, b.n)
                for c in range(DC):
                    ins = nc.scalar.activation(hT[:, c], tiles2(5)[:, c], ACT.Identity, bias=be2c[:, c:c + 1], scale=g2c[:, c:c + 1])
                ins.then_inc(s2_hf, 1)
                act.wait_ge(s2_hf, b.n + 1)
                if b.i is not None or b.off >= 2:
                    act.wait_ge(s2_up, 4 * (b.n - 1))
                nc.scalar.activation(hTs[0][:, b.par], hT, ACT.Copy).then_inc(s2_hT, 1)

            def tanh_pair(b, j):
                act.wait_ge(s2_up, 4 * b.n + j + 1)
                if b.i is not None or b.off >= 1:
                    act.wait_ge(s2_g, 4 * (b.n - 1) + j + 1)
                for f in range(2):
                    ins = nc.scalar.activation(th[:, j, f], tiles2(j)[:, f], ACT.Tanh, bias=b1t[:, 2 * j + f:2 * j + f + 1], scale=0.5 * GELU_A)
                ins.then_inc(s2_th, 1)
                if j in U_ACT:
                    for f in range(2):
                        ins = nc.scalar.activation(up[:, j, f], tiles2(j)[:, f], ACT.Identity, bias=b1c[:, 2 * j + f:2 * j + f + 1])
                    ins.then_inc(s2_ua, 1)

            def gT_high(b, j):
                act.wait_ge(s2_g, 4 * b.n + j + 1)
                if b.i is not None or b.off >= 2:
                    act.wait_ge(s2_dn, b.n - 1)
                pair = slice(2 * j, 2 * j + 2)
                nc.scalar.activation(gTs[0][:, b.par, pair], gT[:, pair], ACT.Copy).then_inc(s2_gh, 1)

            def hidT_out(b):
                act.wait_ge(s2_hidp, b.n + 1)
                if b.i is not None or b.off >= 1:
                    act.wait_ge(s2_r, b.n)
                    act.wait_ge(s2_h1p, b.n)
                for c in range(DC):
                    ins = nc.scalar.activation(hidT[:, c], tiles2(6)[:, c], ACT.Copy, accum_out=pooled[:, c:c + 1])
                ins.then_inc(s2_hidT, 1)

            def gate1(b):
                act.wait_ge(s2_h1p, b.n + 1)
                nc.scalar.activation(h1[:], bank[6][0:GW, 0:1], ACT.Relu, bias=gb1[:], scale=1.0 / S).then_inc(s2_h1, 1)

            def gate2(b):
                act.wait_ge(s2_zp, b.n + 1)
                if b.i is not None or b.off >= 1:
                    act.wait_ge(s2_str, b.n)
                nc.scalar.activation(gth[:], bank[6][:, 8:9], ACT.Tanh, bias=gb2h[:], scale=0.5).then_inc(s2_z, 1)

            split_weights()
            yn_out(Batch(0))
            hT_out(Batch(0))
            yn_out(Batch(1))

            def body2(b, n):
                main = n is None or n < B
                tail = n is None or 1 <= n <= B
                tail2 = n is None or n >= 2
                if main:
                    tanh_pair(b, 0)
                if tail:
                    gT_high(b.plus(-1), 3)
                if tail2:
                    gate1(b.plus(-2))
                if main:
                    tanh_pair(b, 1)
                    gT_high(b, 0)
                    if n is None or n + 1 < B:
                        hT_out(b.plus(1))
                if tail2:
                    gate2(b.plus(-2))
                if main:
                    tanh_pair(b, 2)
                    gT_high(b, 1)
                    tanh_pair(b, 3)
                    gT_high(b, 2)
                if n is None or n + 2 < B:
                    yn_out(b.plus(2))
                if tail:
                    hidT_out(b.plus(-1))

            run_batches(act, 0, 3, B - 3, B + 2, body2)

        @block.tensor
        def _(pe):
            mm = nc.tensor.matmul
            pe.wait_ge(s_emb, 1)
            for n in range(2 * DC):
                for c in range(2):
                    ins = mm(bank[7][:, n * B:(n + 1) * B], wada[:, c, n * P:(n + 1) * P], emb[:, c], start=(c == 0), stop=(c == 1))
            ins.then_inc(s_adaps, 1)

            def gs_gram(i, i_prev, i_prev2):
                pe.wait_ge(s_gcol, i + 1)
                if i_prev:
                    pe.wait_ge(s_gself, 4 * i)
                if i_prev2:
                    pe.wait_ge(s_x2, i - 1)
                for a in range(2):
                    for c in range(DC):
                        ins = mm(gs_ps[:, a * R:(a + 1) * R], ucol[:, a, c:c + 1].to_broadcast([P, P]), uv[:, a, c], start=(c == 0), stop=(c == DC - 1))
                ins.then_inc(s_gram, 1)

            def response_matrix():
                pe.wait_ge(s_gself, 4 * R)
                for c in range(DC):
                    mm(bank[0][0:R, 0:R], uv[:, 1, c], uv[:, 1, c], start=(c == 0), stop=(c == DC - 1))
                mm(bank[1][0:R, 0:D], uv[0:R, 0, 0], respT[:], start=True, stop=True)
                for c in range(DC):
                    ins = nc.tensor.transpose(bank[2][0:R, c * P:(c + 1) * P], uv[:, 0, c], ident[:])
                ins.then_inc(s_rm, 1)
                pe.wait_ge(s_rmc, 1)
                mm(bank[3][0:R, 0:D], gram[:], t1[:], start=True, stop=True).then_inc(s_rm, 1)
                pe.wait_ge(s_rmc, 2)
                for c in range(DC):
                    ins = mm(bank[7][:, c * D:(c + 1) * D], uoT[:, c * P:(c + 1) * P], t2[:], start=True, stop=True)
                ins.then_inc(s_rm, 1)
                pe.wait_ge(s_rmc, 3)
            pe.wait_ge(s_setup, 1)

            def scores(b, h):
                if b.i is not None or H * b.off + h >= 2:
                    pe.wait_ge(s_reduced, 2 * (H * b.n + h - 1))
                if h == 0:
                    pe.wait_ge(s_stq[b.par], 16 * len(RUNS[0]) * (b.half + 1))
                    pe.wait_ge(s_stk[b.par], 16 * len(RUNS[0]) * (b.half + 1))
                at = h % (H // DC) * DC + h // (H // DC)
                for qt in range(QT):
                    ins = mm(qk_ps[h % 2][:, qt], stack[:, b.par, 0, at, qt * P:(qt + 1) * P], stack[:, b.par, 1, at, :], start=True, stop=True)
                ins.then_inc(s_qk, 1)

            def transposes(b, h):
                slot = 2 * b.par + h // CH
                if b.i is not None or H * b.off + h >= 2:
                    last, bb = (h - 2, b) if h >= 2 else (h - 2 + H, b.plus(-1))
                    if last in ACT_HEADS:
                        pe.wait_ge(s_pta, copied(ACT_HEADS, bb, last))
                    else:
                        pe.wait_ge(s_ptd, copied(DVE_HEADS, bb, last))
                for qt in range(QT):
                    pe.wait_ge(s_exp, 2 * H * b.n + 2 * h + qt + 1)
                    for kt in range(QT):
                        ins = nc.tensor.transpose(tp_ps[h % 2][:, kt, qt * P:(qt + 1) * P], ring[:, slot, qt, h % CH, kt * P:(kt + 1) * P], ident[:])
                ins.then_inc(s_tp, 1)

            def pv(b, g):
                pe.wait_ge(s_pta, copied(ACT_HEADS, b, HG * g + HG - 1))
                pe.wait_ge(s_ptd, copied(DVE_HEADS, b, HG * g + HG - 1))
                if g == 0:
                    pe.wait_ge(s_v, b.n + 1)
                if b.i is not None or NG * b.off + g >= 1:
                    pe.wait_ge(s_pvc, NG * b.n + g)
                for kt in range(QT):
                    for j in range(HG):
                        h = HG * g + j
                        ins = mm(pv_ps[VW * j:VW * (j + 1), :], vt[:, b.par, kt, h], pT[:, h % (2 * HG), kt], start=(kt == 0), stop=(kt == QT - 1))
                ins.then_inc(s_pv, 1)

            def x_transpose(b):
                pe.wait_ge(s_xn, b.n + 1)
                if b.i is not None or b.off >= 1:
                    pe.wait_ge(s_v, b.n)
                for c in range(DC):
                    for t in range(QT):
                        ins = nc.tensor.transpose(prep_b[:, c, t * P:(t + 1) * P], xn[:, t, c * P:(c + 1) * P], ident[:])
                ins.then_inc(s_xtp, 1)

            def project_qk(b, t):
                w, ps = (wq, prep_b) if t == 0 else (wk, prep_a)
                pe.wait_ge(s_xT, b.n + 1)
                if t == 1 and (b.i is not None or b.off >= 1):
                    pe.wait_ge(s_xres, b.n)
                for n in range(DC):
                    for c in range(DC):
                        ins = mm(ps[:, n], w[:, c, n * P:(n + 1) * P], xT[:, c], start=(c == 0), stop=(c == DC - 1))
                ins.then_inc(s_qp if t == 0 else s_kp, 1)

            def project_v(b):
                pe.wait_ge(s_p3, 2 * b.n + 1)
                for t in range(QT):
                    for c in range(DC):
                        ins = mm(prep_b[:, t], xT[:, c, t * P:(t + 1) * P], wv[:, c], start=(c == 0), stop=(c == DC - 1))
                ins.then_inc(s_vp, 1)

            def x_back(b):
                pe.wait_ge(s_p3, 2 * b.n + 2)
                for t in range(QT):
                    for c in range(DC):
                        ins = nc.tensor.transpose(prep_a[:, t, c * P:(c + 1) * P], xT[:, c, t * P:(t + 1) * P], ident[:])
                ins.then_inc(s_xb, 1)

            def ctx_natural(b, qt):
                pe.wait_ge(s_pvc, NG * b.n + NG)
                if qt == 0:
                    if b.i is not None or b.off >= 1:
                        pe.wait_ge(s_x2, b.n)
                    if b.i is not None or b.off + 1 < B:
                        pe.wait_ge(s_gii, b.n + 2)
                else:
                    pe.wait_ge(s_ctxn, 2 * b.n + 1)
                for g in range(NG):
                    ins = nc.tensor.transpose(bank[7][:, g * P:(g + 1) * P], pv_sb[:, g, qt * P:(qt + 1) * P], ident[:])
                ins.then_inc(s_cn, 1)

            def ctx_transpose(b):
                pe.wait_ge(s_ctxn, 2 * b.n + 2)
                for c in range(DC):
                    for t in range(QT):
                        ins = nc.tensor.transpose(tail_ps[:, c, t * P:(t + 1) * P], ctxn[:, t, c * P:(c + 1) * P], ident[:])
                ins.then_inc(s_cT, 1)

            def project_o(b):
                pe.wait_ge(s_ctxT, b.n + 1)
                for t in range(QT):
                    for c in range(DC):
                        ins = mm(tail_ps[:, t], ctxT[:, c, t * P:(t + 1) * P], wo[:, c], start=(c == 0), stop=(c == DC - 1))
                ins.then_inc(s_o, 1)

            first = Batch(0)
            x_transpose(first)
            project_qk(first, 0)
            project_qk(first, 1)
            project_v(first)
            x_back(first)
            x_transpose(Batch(1))
            scores(first, 0)

            def body(b, n):
                main = n is None or n < B
                prep = n is None or n + 1 < B
                tail = n is None or n >= 1
                for h in range(H):
                    if main and h + 1 < H:
                        scores(b, h + 1)
                    elif prep:
                        scores(b.plus(1), 0)
                    at = behind(b, n, h, 2)
                    if at:
                        transposes(*at)
                    at = behind(b, n, h, 7)
                    if at and at[1] % HG == 0:
                        pv(at[0], at[1] // HG)
                    if prep:
                        if h == 0:
                            project_qk(b.plus(1), 0)
                        if h == 2:
                            project_qk(b.plus(1), 1)
                        if h == 6:
                            project_v(b.plus(1))
                        if h == 8:
                            x_back(b.plus(1))
                    if h == 10 and (n is None or n + 2 < B):
                        x_transpose(b.plus(2))
                    if main and h == 1:
                        gs_gram(b.n, n is None or n >= 1, n is None or n >= 2)
                    if tail:
                        if h == 5:
                            ctx_natural(b.plus(-1), 0)
                        if h == 7:
                            ctx_natural(b.plus(-1), 1)
                        if h == 9:
                            ctx_transpose(b.plus(-1))
                        if h == 12:
                            project_o(b.plus(-1))

            run_batches(pe, 0, 3, B - 3, B + 1, body)
            last = Batch(B - 1)

            pe.wait_ge(s_x2, B)
            response_matrix()

            def y_transpose(b):
                pe.wait_ge(s2_yn, b.n + 1)
                if b.i is not None or b.off >= 1:
                    pe.wait_ge(s2_hf, b.n)
                for c in range(DC):
                    for t in range(QT):
                        ins = nc.tensor.transpose(tiles2(5)[:, c, t * P:(t + 1) * P], yn[:, t, c * P:(c + 1) * P], ident[:])
                ins.then_inc(s2_yt, 1)

            def up_pair(b, j):
                if j == 0:
                    pe.wait_ge(s2_hl, b.n + 1)
                    if b.i is None and b.off == 0:
                        pe.wait_ge(s2_wl, 2)
                if b.i is not None or b.off >= 1:
                    if j in U_ACT:
                        pe.wait_ge(s2_ua, u_done(True, b.plus(-1), j))
                    else:
                        pe.wait_ge(s2_u, u_done(False, b.plus(-1), j))
                for f in range(2):
                    n = 2 * j + f
                    for c in range(DC):
                        for k, (kw, kx) in enumerate(HI_LO):
                            ins = mm(tiles2(j)[:, f], w1s[kw][:, c, n * P:(n + 1) * P], hTs[kx][:, b.par, c],
                                     start=(c == 0 and k == 0), stop=(c == DC - 1 and k == len(HI_LO) - 1))
                ins.then_inc(s2_up, 1)

            def down(b):
                if b.i is not None or b.off >= 1:
                    pe.wait_ge(s2_hid, b.n)
                for t in range(QT):
                    for f in range(FC):
                        if t == 0 and f % 2 == 0:
                            pe.wait_ge(s2_gl, 4 * b.n + f // 2 + 1)
                        for k, (kx, kw) in enumerate(HI_LO):
                            ins = mm(tiles2(4)[:, t], gTs[kx][:, b.par, f, t * P:(t + 1) * P], w2s[kw][:, f],
                                     start=(f == 0 and k == 0), stop=(f == FC - 1 and k == len(HI_LO) - 1))
                ins.then_inc(s2_dn, 1)

            def hid_transpose(b):
                pe.wait_ge(s2_hid, b.n + 1)
                if b.i is not None or b.off >= 1:
                    pe.wait_ge(s2_z, b.n)
                for c in range(DC):
                    for t in range(QT):
                        ins = nc.tensor.transpose(tiles2(6)[:, c, t * P:(t + 1) * P], hid[:, b.par, t, c * P:(c + 1) * P], ident[:])
                ins.then_inc(s2_hidp, 1)

            def gate_h1(b):
                pe.wait_ge(s2_hidT, b.n + 1)
                for c in range(DC):
                    ins = mm(bank[6][0:GW, 0:1], gw1[:, c], pooled[:, c:c + 1], start=(c == 0), stop=(c == DC - 1))
                ins.then_inc(s2_h1p, 1)

            def gate_z(b):
                pe.wait_ge(s2_h1, b.n + 1)
                mm(bank[6][:, 8:9], h1[:].to_broadcast([GW, P]), gw2[:], start=True, stop=True).then_inc(s2_zp, 1)

            def response(b):
                pe.wait_ge(s2_hidT, b.n + 1)
                if b.i is not None or b.off >= 1:
                    pe.wait_ge(s2_rs, b.n)
                for t in range(QT):
                    for c in range(DC):
                        ins = mm(tiles2(7)[:, t], hidT[:, c, t * P:(t + 1) * P], resp_m[:, c], start=(c == 0), stop=(c == DC - 1))
                ins.then_inc(s2_r, 1)

            y_transpose(first)

            def body2(b, n):
                main = n is None or n < B
                tail = n is None or 1 <= n <= B
                tail2 = n is None or n >= 2
                if main:
                    up_pair(b, 0)
                    if n is None or n + 1 < B:
                        y_transpose(b.plus(1))
                if tail2:
                    gate_h1(b.plus(-2))
                if main:
                    up_pair(b, 1)
                if tail2:
                    response(b.plus(-2))
                if tail:
                    down(b.plus(-1))
                if tail2:
                    gate_z(b.plus(-2))
                if main:
                    up_pair(b, 2)
                    up_pair(b, 3)
                if tail:
                    hid_transpose(b.plus(-1))

            run_batches(pe, 0, 3, B - 3, B + 2, body2)


_NAMES = ['W_ada', 'b_ada', 'Wq', 'bq', 'Wk', 'bk', 'Wv', 'bv', 'Wo', 'bo', 'W1', 'b1', 'W2', 'b2', 'g2', 'beta2']


def kernel(**inputs):
    import concourse.bacc as _bacc
    from concourse.bass_utils import run_bass_kernel_spmd as _run

    a = {k: np.asarray(v) for k, v in inputs.items()}
    feeds = {
        "x": a["x"], "itok": a["itok_B_34_63"], "fside": a["fside_Bx16xSxS_0"], "score": a["condB_safetyscore"],
        "mask": a["mask_Bx1xSxS_bk0"],
    }
    feeds.update({n: a["L0_cond_" + n] for n in _NAMES})
    for n in ('Wq', 'bq', 'Wk', 'bk'):
        w = feeds[n]
        feeds[n] = w.reshape(-1, DC, P // HD, HD).transpose(0, 1, 3, 2).reshape(w.shape)
    feeds.update({n: feeds[n].reshape(-1, P).T for n in ('b_ada', 'bq', 'bk', 'b1', 'g2', 'beta2')})
    feeds.update({
        "U": a["L1_cond_U"], "V": a["L1_cond_V"], "safety_bias": a["L1_cond_safety_bias"],
        "gate_w1T": a["L1_cond_gate_w1"].T, "gate_b1": a["L1_cond_gate_b1"], "gate_w2T": a["L1_cond_gate_w2"].T,
        "gate_b2": a["L1_cond_gate_b2"], "resp_wT": a["L1_cond_resp_w"].T, "resp_b": a["L1_cond_resp_b"],
        "freqs": np.exp(np.arange(D // 2, dtype=np.float32) * np.float32(-np.log(10000.0) / (D // 2 - 1))).astype(np.float32),
    })
    nc = _bacc.Bacc("TRN2", target_bir_lowering=False, num_devices=1)
    arrays, aps = {}, {}
    for name, v in feeds.items():
        v = np.ascontiguousarray(v)
        arrays["in_" + name] = v
        aps[name] = nc.dram_tensor("in_" + name, v.shape, mybir.dt.from_np(v.dtype), kind="ExternalInput").ap()
    aps["out"] = nc.dram_tensor("out_0", (B, S, D), F32, kind="ExternalOutput").ap()
    attention_block_kernel(nc, **aps)
    r = _run(nc, [arrays], core_ids=[0])
    return r.results[0]["out_0"]
```

```python
from contextlib import ExitStack

import numpy as np

import concourse.bass as bass
from concourse import mybir

F32 = mybir.dt.float32
F32R = mybir.dt.float32r
BF16 = mybir.dt.bfloat16
I32 = mybir.dt.int32
U8 = mybir.dt.uint8
ALU = mybir.AluOpType
ACT = mybir.ActivationFunctionType

P = 128
B, S, D = 32, 256, 256
H, HD = 16, 16
F = 1024
R = 32
GW = 64
QT = S // P
DC = D // P
FC = F // P
HG = 4
NG = H // HG
CH = 8
RING = 4
VW = 32
LN_EPS = 1e-5
GS_EPS = 1e-8
SPLIT = [(0, 0), (0, 1), (0, 2), (1, 0), (1, 1), (2, 0)]
RUNS = [[(0, 3, 0, 0), (3, 2, 1, 0), (5, 1, 2, 0)], [(0, 3, 0, 1), (3, 2, 0, 1), (5, 1, 0, 0)]]
NS = len(SPLIT)
KQ = NS * HD
GELU_A = 1.702
TWO_PI = 2.0 * np.pi
C1 = 6.28125
C2 = float(np.float32(np.round((TWO_PI - C1) * 2.0**21) / 2.0**21))
C3 = float(np.float32(TWO_PI - C1 - C2))
MASKED = -1.0e30
ROW_MAX_NEG = 1.0e29
MAGIC = 1.5 * 2.0**23
PI_IN = 3.1415925


HI_LO = [(0, 0), (0, 1), (1, 0)]
U_ACT = [0, 2]


def u_done(owner_has, b, j):
    return 2 * b.n + sum(1 for k in range(j + 1) if (k in U_ACT) == owner_has)


def f32(a):
    return a.bitcast(F32)


class Batch:

    def __init__(self, off, i=None):
        self.par = off % 2
        self.half = off // 2 if i is None else i + off // 2
        self.n = off if i is None else 2 * i + off
        self.off, self.i = off, i

    def plus(self, k):
        return Batch(self.off + k, self.i)


DVE_HEADS = [1, 5, 9, 13, 15]
ACT_HEADS = [h for h in range(H) if h not in DVE_HEADS]


def copied(heads, b, h):
    return len(heads) * b.n + sum(1 for k in heads if k <= h)


def behind(b, n, h, k):
    if h >= k:
        return (b, h - k) if n is None or n < B else None
    return (b.plus(-1), h - k + H) if n is None or n >= 1 else None


def run_batches(eng, first, loop_from, loop_to, last, body):
    for b in range(first, loop_from):
        body(Batch(b), b)
    with eng.Fori(0, (loop_to - loop_from) // 2) as i:
        for off in range(2):
            body(Batch(loop_from + off, i), None)
    for b in range(loop_to, last):
        body(Batch(b), b)


def attention_block_kernel(nc, x, itok, fside, score, mask, W_ada, b_ada, Wq, bq, Wk, bk, Wv, bv, Wo, bo,
                           W1, b1, W2, b2, g2, beta2, U, V, safety_bias, gate_w1T, gate_b1, gate_w2T, gate_b2,
                           resp_wT, resp_b, freqs, out):
    with ExitStack() as ctx:
        def sb(name, shape, dt=F32):
            return ctx.enter_context(nc.sbuf_tensor(name, shape, dt))

        def sem(name):
            return ctx.enter_context(nc.semaphore(name))

        parts_d = nc.dram_tensor("parts_d", (2, 2, 3, P, DC * S), BF16, kind="Internal").ap()
        x2_d = nc.dram_tensor("x2_d", (B, S, D), F32, kind="Internal").ap()

        wq = sb("wq", [P, DC, D]); wk = sb("wk", [P, DC, D]); wv = sb("wv", [P, DC, D]); wo = sb("wo", [P, DC, D])
        w1 = sb("w1", [P, DC, F]); w2 = sb("w2", [P, FC, D]); wada = sb("wada", [P, 2, 2 * D])
        bqk = sb("bqk", [P, 2, DC]); bada = sb("bada", [P, 2 * DC]); b1c = sb("b1c", [P, FC]); b1t = sb("b1t", [P, FC])
        g2c = sb("g2c", [P, DC]); be2c = sb("be2c", [P, DC])
        bvb = sb("bvb", [P, D]); bob = sb("bob", [P, D]); b2b = sb("b2b", [P, D]); cb = sb("cb", [P, D]); cb2 = sb("cb2", [P, D])
        ident = sb("ident", [P, P]); later = sb("later", [P, R, R]); expo = sb("expo", [P, 2, 2])
        frq = sb("frq", [P, 1]); tti = sb("tti", [P, B], I32); ttf = sb("ttf", [P, B]); ang = sb("ang", [P, B])
        turns = sb("turns", [P, 2, B]); red = sb("red", [P, 2, B]); red2 = sb("red2", [P, 2, B])
        sc = sb("sc", [P, 2, B]); sct = sb("sct", [P, 2, B]); emb = sb("emb", [P, 2, B])
        adaS = sb("adaS", [P, DC, B]); adaB = sb("adaB", [P, DC, B])
        scr = sb("scr", [P, B]); modh = sb("modh", [P, B]); modt = sb("modt", [P, B])
        gw1 = sb("gw1", [P, DC, GW]); gb1 = sb("gb1", [GW, 1]); gw2 = sb("gw2", [GW, 1]); gb2 = sb("gb2", [P, 1]); gb2h = sb("gb2h", [P, 1])
        uv = sb("uv", [P, 2, DC, R]); ucol = sb("ucol", [P, 2, DC]); gsb = sb("gsb", [P, 2, R]); gii = sb("gii", [P, 2])
        nrm = sb("nrm", [P, 2]); nrme = sb("nrme", [P, 2]); rnrm = sb("rnrm", [P, 2]); qneg = sb("qneg", [P, 2, DC]); coef = sb("coef", [P, 2, R])
        respT = sb("respT", [R, D]); gram = sb("gram", [R, R]); t1 = sb("t1", [R, D]); t2 = sb("t2", [R, D]); uoT = sb("uoT", [R, D]); resp_m = sb("resp_m", [P, DC, D])

        ring = sb("ring", [P, RING, QT, CH, S])
        ring_at = nc.sbuf_base - 4 * RING * QT * CH * S
        pT = sb("pT", [P, 2 * HG, QT, S])
        stack_all = sb("stack", [P, 2, 2, H, S], BF16)
        stack = stack_all[0:KQ]
        parts = sb("parts", [P, 2, 3, DC, S], BF16)
        xt = sb("xt", [P, 2, QT, D])
        xt_at = nc.sbuf_base - 4 * 2 * QT * D
        st6 = sb("st6", [P, QT, 6]); mv = sb("mv", [P, QT, 2])
        vpe = sb("vpe", [P, QT]); rstd = sb("rstd", [P, QT]); mneg = sb("mneg", [P, QT]); nmr = sb("nmr", [P, QT])
        xn = sb("xn", [P, QT, D]); xT = sb("xT", [P, DC, S]); xres = sb("xres", [P, 2, QT, D])
        xres_at = nc.sbuf_base - 4 * 2 * QT * D
        vt = sb("vt", [P, 2, QT, H, VW])
        vt_at = nc.sbuf_base - 4 * 2 * QT * H * VW
        mk = sb("mk", [P, 2, QT, S], U8); maskv = sb("maskv", [P, QT, S])
        nmax = sb("nmax", [P, 2, H, QT])
        pv_sb = sb("pv_sb", [P, NG, S]); rec = sb("rec", [P, QT, H]); ctxn = sb("ctxn", [P, QT, D]); ctxT = sb("ctxT", [P, DC, S]); x2s = sb("x2s", [P, 2, QT, D])

        def lay(name, shape, at):
            return nc.alloc_sbuf_tensor_at(name, shape, F32R, offset=at)[:]

        w1s = [lay("w1_high", [P, DC, F], ring_at), lay("w1_rest", [P, DC, F], ring_at + 4 * DC * F)]
        w2s_at = ring_at + 4 * 2 * DC * F
        w2s = [lay("w2_high", [P, FC, D], w2s_at), lay("w2_rest", [P, FC, D], w2s_at + 4 * FC * D)]
        gTs_at = w2s_at + 4 * 2 * FC * D
        gTs = [lay("gT_high", [P, 2, FC, S], gTs_at), lay("gT_rest", [P, 2, FC, S], gTs_at + 4 * 2 * FC * S)]
        hTs = [lay("hT_high", [P, 2, DC, S], vt_at), lay("hT_rest", [P, 2, DC, S], vt_at + 4 * 2 * DC * S)]
        hidTs = [lay("hidT_high", [P, DC, S], xt_at), lay("hidT_rest", [P, DC, S], xt_at + 4 * DC * S)]
        resp_ms = [lay("resp_m_high", [P, DC, D], xres_at), lay("resp_m_rest", [P, DC, D], xres_at + 4 * DC * D)]
        regions = [stack_all[:].rearrange("p a t h s -> p (a t h s)").bitcast(F32), pT[:].rearrange("p h t s -> p (h t s)")]
        place = [0, 0]

        def carve(*shape):
            n = int(np.prod(shape))
            i = 0 if place[0] + n <= regions[0].shape[1] else 1
            a = regions[i][:, place[i]:place[i] + n]
            place[i] += n
            if len(shape) == 2:
                return a.rearrange("p (a b) -> p a b", a=shape[0])
            return a.rearrange("p (a b c) -> p a b c", a=shape[0], b=shape[1])

        y2 = carve(2, QT, D)
        yb = carve(2, QT, D)
        yn = carve(QT, D)
        hT = carve(DC, S)
        th = carve(4, 2, S)
        up = carve(4, 2, S)
        gT = carve(FC, S)
        hid = carve(2, QT, D)
        hidT = carve(DC, S)
        rsp = carve(QT, D)
        fin = carve(2, QT, D)
        pooled = sb("pooled", [P, DC]); h1 = sb("h1", [GW, 1]); gth = sb("gth", [P, 1]); strg = sb("strg", [P, 2])
        st6b = sb("st6b", [P, QT, 6]); mvb = sb("mvb", [P, 2, QT, 2]); vpeb = sb("vpeb", [P, QT]); rstdb = sb("rstdb", [P, QT]); mnegb = sb("mnegb", [P, QT]); nmrb = sb("nmrb", [P, QT])

        bank = [ctx.enter_context(nc.psum_tensor(f"bank{i}", [P, 512], F32)) for i in range(8)]

        def tiles2(i):
            return bank[i][:].rearrange("p (a s) -> p a s", a=2)

        qk_ps = [tiles2(0), tiles2(1)]
        tp_ps = [tiles2(2), tiles2(3)]
        pv_ps = bank[4][:, 0:S]
        gs_ps = bank[7][:, 0:2 * R]
        prep_a, prep_b, tail_ps = tiles2(5), tiles2(6), tiles2(7)

        s_load = sem("s_load"); s_load_ada = sem("s_load_ada"); s_load_att = sem("s_load_att"); s_const = sem("s_const"); s_dve0 = sem("s_dve0"); s_red = sem("s_red"); s_sin = sem("s_sin"); s_emb = sem("s_emb")
        s_act0 = sem("s_act0"); s_adaps = sem("s_adaps"); s_setup = sem("s_setup")
        s_gcol = sem("s_gcol"); s_gram = sem("s_gram"); s_gii = sem("s_gii"); s_gnrm = sem("s_gnrm"); s_gp = sem("s_gp"); s_gself = sem("s_gself")
        s_rm = sem("s_rm"); s_rmc = sem("s_rmc")
        s_x = [sem("s_x0"), sem("s_x1")]; s_mk = [sem("s_mk0"), sem("s_mk1")]; s_bias = [sem(f"s_bias{i}") for i in range(RING)]
        s_wq_d = sem("s_partq_out"); s_wk_d = sem("s_partk_out"); s_stq = [sem("s_stackq0"), sem("s_stackq1")]; s_stk = [sem("s_stackk0"), sem("s_stackk1")]
        s_x2st = [sem("s_x2st0"), sem("s_x2st1")]
        s_maskv = sem("s_maskv"); s_masked = sem("s_masked"); s_pool = sem("s_pool"); s_rstd = sem("s_rstd")
        s_stats6 = sem("s_stats6"); s_stats = sem("s_stats"); s_reduced = sem("s_reduced"); s_ptd = sem("s_ptd"); s_xT = sem("s_xT")
        s_r1 = sem("s_r1"); s_p3 = sem("s_p3"); s_v = sem("s_v"); s_xres = sem("s_xres"); s_rec = sem("s_rec"); s_ctxn = sem("s_ctxn"); s_x2 = sem("s_x2")
        s_xn = sem("s_xn"); s_exp = sem("s_exp"); s_pta = sem("s_pta"); s_p1 = sem("s_p1"); s_p2 = sem("s_p2"); s_pvc = sem("s_pvc"); s_ctxT = sem("s_ctxT")
        s_qk = sem("s_qk"); s_tp = sem("s_tp"); s_pv = sem("s_pv"); s_xtp = sem("s_xtp"); s_qp = sem("s_qp"); s_kp = sem("s_kp"); s_vp = sem("s_vp"); s_xb = sem("s_xb")
        s_cn = sem("s_cn"); s_cT = sem("s_cT"); s_o = sem("s_o")
        s_y = [sem("s_y0"), sem("s_y1")]; s_out = [sem("s_out0"), sem("s_out1")]
        s2_six = sem("s2_six"); s2_stats = sem("s2_stats"); s2_pool = sem("s2_pool"); s2_rstd = sem("s2_rstd"); s2_yb = sem("s2_yb"); s2_yn = sem("s2_yn")
        s2_yt = sem("s2_yt"); s2_hT = sem("s2_hT"); s2_up = sem("s2_up"); s2_th = sem("s2_th"); s2_u = sem("s2_u"); s2_ua = sem("s2_ua"); s2_w = sem("s2_w"); s2_wl = sem("s2_wl"); s2_hf = sem("s2_hf"); s2_hl = sem("s2_hl"); s2_gh = sem("s2_gh"); s2_gl = sem("s2_gl"); s2_hidf = sem("s2_hidf"); s2_hidl = sem("s2_hidl"); s2_m = sem("s2_m"); s2_ml = sem("s2_ml"); s2_g = sem("s2_g"); s2_dn = sem("s2_dn")
        s2_hid = sem("s2_hid"); s2_hidp = sem("s2_hidp"); s2_hidT = sem("s2_hidT"); s2_r = sem("s2_r"); s2_h1p = sem("s2_h1p"); s2_h1 = sem("s2_h1"); s2_zp = sem("s2_zp")
        s2_z = sem("s2_z"); s2_str = sem("s2_str"); s2_rs = sem("s2_rs"); s2_fin = sem("s2_fin")

        loads_x = [(xt[:, i], x[i].rearrange("(t p) d -> p t d", p=P), s_x[i]) for i in range(2)]
        loads_ada = [(dst, src, s_load_ada) for dst, src in [
            (tti[:], itok.partition_broadcast(P)), (frq[:], freqs.rearrange("(p a) -> p a", a=1)),
            (wada[:], W_ada.rearrange("(c p) n -> p c n", p=P)), (bada[:], b_ada), (scr[:], score.partition_broadcast(P)),
            (wq[:], Wq.rearrange("(c p) n -> p c n", p=P)), (bqk[:, 0], bq),
        ]]
        loads_att = [(dst, src, s_load_att) for dst, src in [
            (wk[:], Wk.rearrange("(c p) n -> p c n", p=P)), (wv[:], Wv.rearrange("(c p) n -> p c n", p=P)), (bqk[:, 1], bk),
            (bvb[:], bv.partition_broadcast(P)), (bob[:], bo.partition_broadcast(P)), (wo[:], Wo.rearrange("(c p) n -> p c n", p=P)),
            (uv[:, 0], U.rearrange("(c p) r -> p c r", p=P)), (uv[:, 1], V.rearrange("(c p) r -> p c r", p=P)),
        ]]
        loads_rest = [(dst, src, s_load) for dst, src in [
            (w1[:], W1.rearrange("(c p) n -> p c n", p=P)), (w2[:], W2.rearrange("(c p) n -> p c n", p=P)),
            (b1c[:], b1), (g2c[:], g2), (be2c[:], beta2), (b2b[:], b2.partition_broadcast(P)),
            (cb[:], resp_b.partition_broadcast(P)), (cb2[:], safety_bias.partition_broadcast(P)),
            (gw1[:], gate_w1T.rearrange("(c p) n -> p c n", p=P)),
            (gb1[:], gate_b1.rearrange("(p a) -> p a", a=1)), (gw2[:], gate_w2T), (gb2[:], gate_b2.partition_broadcast(P)),
            (respT[:], resp_wT),
        ]]

        def x_view(b):
            return x[bass.ds(b.n, 1)].rearrange("a (t p) d -> p (a t) d", p=P)

        def bias_chunk(b, c, qt):
            return fside[bass.ds(b.n, 1), c * CH:(c + 1) * CH, qt * P:(qt + 1) * P, :].rearrange("a h p k -> p (a h) k")

        def free_pT(eng, b, h):
            g = h // HG
            if b.i is not None or NG * b.off + g >= 2:
                eng.wait_ge(s_pv, NG * b.n + g - 1)

        block = ctx.enter_context(nc.Block())

        @block.sync
        def _(sp):
            for dst, src, loaded in loads_x + loads_ada + loads_att:
                sp.dma_start(dst, src).then_inc(loaded, 16)

            def load_mask(b):
                sp.dma_start(mk[:, b.par], mask[bass.ds(b.n, 1)].rearrange("a c (t p) k -> p (a c t) k", p=P)).then_inc(s_mk[b.par], 16)

            def load_bias(b, c):
                slot = 2 * b.par + c
                for qt in range(QT):
                    sp.dma_start(ring[:, slot, qt], bias_chunk(b, c, qt)).then_inc(s_bias[slot], 16)

            def restack(b):
                for t, (s_written, s_back) in enumerate(((s_wq_d, s_stq), (s_wk_d, s_stk))):
                    sp.wait_ge(s_p3, 2 * b.n + t + 1)
                    sp.dma_start(parts_d[b.par, t].rearrange("a p n -> p a n"),
                                 parts[:, t].rearrange("p a c s -> p a (c s)")).then_inc(s_written, 16)
                    sp.wait_ge(s_written, 16 * b.n + 16)
                    for row, n, part, step in RUNS[t]:
                        src = parts_d[b.par, t].rearrange("a (d j) n -> a d (j n)", d=HD)
                        src = src[part:part + n] if step else src[part:part + 1].to_broadcast([n, HD, H * S])
                        sp.dma_start(stack[HD * row:HD * (row + n), b.par, t].rearrange("p h s -> p (h s)"), src).then_inc(s_back[b.par], 16)

            def load_x(b):
                sp.wait_ge(s_xn, b.n - 1)
                sp.dma_start(xt[:, b.par], x_view(b)).then_inc(s_x[b.par], 16)

            load_mask(Batch(0))
            load_mask(Batch(1))
            load_bias(Batch(0), 0)
            load_x(Batch(2))
            restack(Batch(0))
            load_bias(Batch(0), 1)
            load_bias(Batch(1), 0)
            def store_x2(b):
                sp.wait_ge(s_x2, b.n + 1)
                sp.dma_start(x2_d[bass.ds(b.n, 1)].rearrange("a (t p) d -> p (a t) d", p=P), x2s[:, b.par]).then_inc(s_x2st[b.par], 16)

            def body(b, n):
                if n is None or n + 3 < B:
                    load_x(b.plus(3))
                if n == B - 3:
                    for dst, src, loaded in loads_rest:
                        sp.dma_start(dst, src).then_inc(loaded, 16)
                if n is None or 1 <= n < B - 1:
                    sp.wait_ge(s_tp, H * b.n)
                    load_bias(b.plus(1), 1)
                if n is None or n + 2 < B:
                    sp.wait_ge(s_maskv, b.n + 1)
                    sp.nop(nofuse=True)
                    load_mask(b.plus(2))
                if n is None or n + 1 < B:
                    restack(b.plus(1))
                if n == 0:
                    load_bias(b.plus(1), 1)
                if n is None or n + 2 < B:
                    sp.wait_ge(s_tp, H * b.n + CH)
                    load_bias(b.plus(2), 0)
                if n is None or n >= 1:
                    store_x2(b.plus(-1))

            run_batches(sp, 0, 3, B - 3, B, body)

            def load_y(b):
                sp.wait_ge(s_x2st[b.par], 16 * b.half + 16)
                sp.dma_start(y2[:, b.par], x2_d[bass.ds(b.n, 1)].rearrange("a (t p) d -> p (a t) d", p=P)).then_inc(s_y[b.par], 16)

            def store_out(b):
                sp.wait_ge(s2_fin, b.n + 1)
                sp.dma_start(out[bass.ds(b.n, 1)].rearrange("a (t p) d -> p (a t) d", p=P), fin[:, b.par]).then_inc(s_out[b.par], 16)

            sp.wait_ge(s_qk, H * B)
            load_y(Batch(0))
            load_y(Batch(1))
            store_x2(Batch(B - 1))
            sp.wait_ge(s_pv, NG * B)

            def body2(b, n):
                if n is None or n + 2 < B:
                    sp.wait_ge(s2_yn, b.n + 1)
                    sp.wait_ge(s2_yb, b.n + 1)
                    load_y(b.plus(2))
                if n is None or n >= 2:
                    store_out(b.plus(-2))

            run_batches(sp, 0, 3, B - 3, B + 2, body2)
            for par in range(2):
                sp.wait_ge(s_out[par], 16 * B // 2)

        @block.gpsimd
        def _(pool):
            nc.gpsimd.memset(ident[:], 0.0)
            nc.gpsimd.memset(later[:], 1.0)
            nc.gpsimd.memset(expo[:, 0], -0.5)
            nc.gpsimd.memset(expo[:, 1], 0.5).then_inc(s_gp, 1)
            pool.wait_ge(s_gp, 1)
            nc.gpsimd.affine_select(out=ident[:], in_=ident[:], compare_op=ALU.not_equal, fill=1.0, base=0,
                                    pattern=[[-1, P]], channel_multiplier=1)
            nc.gpsimd.affine_select(out=later[:], in_=later[:], compare_op=ALU.is_gt, fill=0.0, base=0,
                                    pattern=[[-1, R], [1, R]], channel_multiplier=0).then_inc(s_const, 1)
            pool.wait_ge(s_const, 1)

            def gs_norm(i):
                pool.wait_ge(s_gii, i + 1)
                nc.gpsimd.tensor_tensor(nrm[:], gii[:], expo[:, 1], ALU.pow).then_inc(s_gp, 1)
                pool.wait_ge(s_gp, i + 2)
                pool.nop(nofuse=True)
                nc.gpsimd.tensor_scalar(nrme[:], nrm[:], GS_EPS, 1.0, ALU.add, ALU.mult).then_inc(s_gnrm, 1)

            def inv_std(b):
                pool.wait_ge(s_stats, b.n + 1)
                if b.i is not None or b.off >= 1:
                    pool.wait_ge(s_xn, b.n)
                pool.nop(nofuse=True)
                nc.gpsimd.tensor_scalar(vpe[:], mv[:, :, 1], LN_EPS, 1.0, ALU.add, ALU.mult)
                nc.gpsimd.tensor_scalar(mneg[:], mv[:, :, 0], -1.0, 1.0, ALU.mult, ALU.mult).then_inc(s_pool, 1)
                pool.wait_ge(s_pool, 2 * b.n + 1)
                nc.gpsimd.tensor_tensor(rstd[:], vpe[:], expo[:, 0], ALU.pow).then_inc(s_pool, 1)
                pool.wait_ge(s_pool, 2 * b.n + 2)
                nc.gpsimd.tensor_tensor(nmr[:], mneg[:], rstd[:], ALU.mult).then_inc(s_rstd, 1)

            def normalise_x(b):
                pool.wait_ge(s_rstd, b.n + 1)
                if b.i is not None or b.off >= 1:
                    pool.wait_ge(s_xtp, b.n)
                pool.nop(nofuse=True)
                for t in range(QT):
                    ins = nc.gpsimd.tensor_scalar(xn[:, t], xt[:, b.par, t], rstd[:, t:t + 1], nmr[:, t:t + 1], ALU.mult, ALU.add)
                ins.then_inc(s_xn, 1)

            def mask_values(b):
                pool.wait_ge(s_mk[b.par], 16 * b.half + 16)
                if b.i is not None or b.off >= 1:
                    pool.wait_ge(s_masked, 2 * NG * b.n)
                pool.nop(nofuse=True)
                nc.gpsimd.tensor_scalar(maskv[:], mk[:, b.par], MASKED, 1.0, ALU.mult, ALU.mult).then_inc(s_maskv, 1)
                pool.wait_ge(s_maskv, b.n + 1)

            def add_mask(b, g):
                slot, h0 = 2 * b.par + g // 2, (g % 2) * HG
                if g % 2 == 0:
                    pool.wait_ge(s_bias[slot], 32 * b.half + 32)
                for qt in range(QT):
                    v = ring[:, slot, qt, h0:h0 + HG]
                    m = maskv[:, qt:qt + 1].to_broadcast([P, HG, S])
                    nc.gpsimd.tensor_tensor(v, v, m, ALU.add).then_inc(s_masked, 1)

            inv_std(Batch(0))
            normalise_x(Batch(0))
            inv_std(Batch(1))
            normalise_x(Batch(1))

            def body(b, n):
                mask_values(b)
                add_mask(b, 0)
                add_mask(b, 1)
                if n is None or n + 2 < B:
                    inv_std(b.plus(2))
                    normalise_x(b.plus(2))
                add_mask(b, 2)
                gs_norm(b.n)
                add_mask(b, 3)

            run_batches(pool, 0, 3, B - 3, B, body)

            def inv_std2(b):
                pool.wait_ge(s2_stats, b.n + 1)
                if b.i is not None or b.off >= 1:
                    pool.wait_ge(s2_rstd, b.n)
                pool.nop(nofuse=True)
                nc.gpsimd.tensor_scalar(vpeb[:], mvb[:, b.par, :, 1], LN_EPS, 1.0, ALU.add, ALU.mult)
                nc.gpsimd.tensor_scalar(mnegb[:], mvb[:, b.par, :, 0], -1.0, 1.0, ALU.mult, ALU.mult).then_inc(s2_pool, 1)
                pool.wait_ge(s2_pool, 2 * b.n + 1)
                if b.i is not None or b.off >= 1:
                    pool.wait_ge(s2_yn, b.n)
                nc.gpsimd.tensor_tensor(rstdb[:], vpeb[:], expo[:, 0], ALU.pow).then_inc(s2_pool, 1)
                pool.wait_ge(s2_pool, 2 * b.n + 2)
                nc.gpsimd.tensor_tensor(nmrb[:], mnegb[:], rstdb[:], ALU.mult).then_inc(s2_rstd, 1)

            def add_b2(b):
                pool.wait_ge(s_y[b.par], 16 * b.half + 16)
                if b.i is not None or b.off >= 2:
                    pool.wait_ge(s2_hid, b.n - 1)
                nc.gpsimd.tensor_tensor(yb[:, b.par], y2[:, b.par], b2b[:].unsqueeze(1).to_broadcast([P, QT, D]), ALU.add).then_inc(s2_yb, 1)

            def body2(b, n):
                if n is None or n < B:
                    inv_std2(b)
                if n is None or n >= 1:
                    add_b2(b.plus(-1))

            run_batches(pool, 0, 4, B, B + 1, body2)

        @block.vector
        def _(dve):
            chain = [0]

            def link(ins):
                chain[0] += 1
                ins.then_inc(s_dve0, 1)
                dve.wait_ge(s_dve0, chain[0])

            nc.vector.memset(vt[:, :, :, :, HD:VW], 0.0)
            link(nc.vector.memset(strg[:], 0.0))
            nc.vector.memset(vt[:, :, :, :, HD:HD + 1], 1.0)

            def stats(b):
                dve.wait_ge(s_x[b.par], 16 * b.half + 16)
                if b.i is not None or b.off >= 1:
                    dve.wait_ge(s_rstd, b.n)
                for t in range(QT):
                    ins = nc.vector.bn_stats(st6[:, t], xt[:, b.par, t])
                ins.then_inc(s_stats6, 1)

            def stats_end(b):
                dve.wait_ge(s_stats6, b.n + 1)
                dve.nop(nofuse=True)
                for t in range(QT):
                    ins = nc.vector.bn_aggr(mv[:, t], st6[:, t])
                ins.then_inc(s_stats, 1)

            stats(Batch(0))
            stats_end(Batch(0))
            dve.wait_ge(s_load_ada, 16 * len(loads_ada))
            link(nc.vector.tensor_copy(ttf[:], tti[:]))
            link(nc.vector.tensor_scalar(ang[:], ttf[:], 40.0, frq[:, 0:1], ALU.mult, ALU.mult))
            nc.vector.tensor_scalar(turns[:, 0], ang[:], 1.0 / TWO_PI, None, ALU.mult)
            link(nc.vector.tensor_scalar(turns[:, 1], ang[:], 1.0 / TWO_PI, 0.25, ALU.mult, ALU.add))
            link(nc.vector.tensor_scalar(turns[:], turns[:], MAGIC, None, ALU.add))
            link(nc.vector.tensor_scalar(turns[:], turns[:], -MAGIC, None, ALU.add))
            link(nc.vector.scalar_tensor_tensor(red[:], turns[:], -C1, ang[:].unsqueeze(1).to_broadcast([P, 2, B]), ALU.mult, ALU.add))
            link(nc.vector.scalar_tensor_tensor(red2[:], turns[:], -C2, red[:], ALU.mult, ALU.add))
            link(nc.vector.scalar_tensor_tensor(red[:], turns[:], -C3, red2[:], ALU.mult, ALU.add))
            link(nc.vector.tensor_scalar(red[:, 1], red[:, 1], float(np.pi / 2), None, ALU.add))
            nc.vector.tensor_scalar(red[:], red[:], PI_IN, -PI_IN, ALU.min, ALU.max).then_inc(s_red, 1)
            nc.vector.tensor_scalar(wq[:], wq[:], HD ** -0.5, None, ALU.mult)
            nc.vector.tensor_scalar(bqk[:, 0], bqk[:, 0], HD ** -0.5, None, ALU.mult)
            dve.wait_ge(s_sin, 1)
            link(nc.vector.scalar_tensor_tensor(emb[:], sct[:], 1.0, sc[:], ALU.add, ALU.mult))
            nc.vector.tensor_scalar(emb[:], emb[:], 0.5, None, ALU.mult).then_inc(s_emb, 1)
            nc.vector.tensor_scalar(modh[:], modt[:], 0.25, 0.25, ALU.mult, ALU.add)
            dve.wait_ge(s_adaps, 1)
            for c in range(DC):
                nc.vector.tensor_scalar(adaS[:, c], bank[7][:, c * B:(c + 1) * B], bada[:, c:c + 1], 1.0, ALU.add, ALU.add)
            for c in range(DC):
                link(nc.vector.tensor_scalar(adaB[:, c], bank[7][:, (DC + c) * B:(DC + c + 1) * B], bada[:, DC + c:DC + c + 1], None, ALU.add))

            dve.wait_ge(s_load_att, 16 * len(loads_att))
            nc.vector.memset(pooled[:], 0.0).then_inc(s_setup, 1)

            def column(i):
                return uv[:, :, :, bass.ds(i, 1)].rearrange("p a c r -> p a (c r)")

            def gs_column(i, first):
                if not first:
                    dve.wait_ge(s_gself, 4 * i)
                nc.vector.tensor_copy(ucol[:], column(i)).then_inc(s_gcol, 1)

            def gs_products(i):
                dve.wait_ge(s_gram, i + 1)
                nc.vector.tensor_copy(gii[:], gs_ps.rearrange("p (a r) -> p a r", a=2)[:, :, bass.ds(i, 1)].rearrange("p a r -> p (a r)"))
                nc.vector.tensor_copy(gsb[:], gs_ps.rearrange("p (a r) -> p a r", a=2)).then_inc(s_gii, 1)

            def gs_reciprocal(i):
                dve.wait_ge(s_gnrm, i + 1)
                nc.vector.reciprocal(rnrm[:], nrme[:]).then_inc(s_gself, 1)

            def gs_coefficients(i):
                dve.wait_ge(s_gii, i + 1)
                dve.wait_ge(s_gself, 4 * i + 1)
                for a in range(2):
                    nc.vector.scalar_tensor_tensor(coef[:, a], gsb[:, a], rnrm[:, a:a + 1],
                                                   later[:, bass.ds(i, 1)].rearrange("p a r -> p (a r)"), ALU.mult, ALU.mult)
                    ins = nc.vector.tensor_scalar(qneg[:, a], ucol[:, a], rnrm[:, a:a + 1], -1.0, ALU.mult, ALU.mult)
                ins.then_inc(s_gself, 1)

            def gs_update(i):
                dve.wait_ge(s_gself, 4 * i + 2)
                for a in range(2):
                    for c in range(DC):
                        ins = nc.vector.scalar_tensor_tensor(uv[:, a, c], coef[:, a], qneg[:, a, c:c + 1], uv[:, a, c], ALU.mult, ALU.add)
                ins.then_inc(s_gself, 1)

            def gs_write(i):
                dve.wait_ge(s_gself, 4 * i + 3)
                nc.vector.tensor_scalar(column(i), qneg[:], -1.0, None, ALU.mult).then_inc(s_gself, 1)

            def response_matrix(step):
                dve.wait_ge(s_rm, step + 1)
                if step == 0:
                    nc.vector.tensor_copy(gram[:], bank[0][0:R, 0:R])
                    nc.vector.tensor_copy(t1[:], bank[1][0:R, 0:D])
                    nc.vector.tensor_copy(uoT[:], bank[5][0:R, 0:D]).then_inc(s_rmc, 1)
                if step == 1:
                    nc.vector.tensor_copy(t2[:], bank[6][0:R, 0:D]).then_inc(s_rmc, 1)
                if step == 2:
                    nc.vector.tensor_copy(resp_m[:], tiles2(1)).then_inc(s_rmc, 1)

            stats(Batch(1))
            stats_end(Batch(1))

            def reduce_head(b, h):
                slot = 2 * b.par + h // CH
                dve.wait_ge(s_qk, H * b.n + h + 1)
                for qt in range(QT):
                    v = ring[:, slot, qt, h % CH]
                    if h % HG == 0:
                        dve.wait_ge(s_masked, 2 * NG * b.n + 2 * (h // HG) + qt + 1)
                    dve.nop(nofuse=True)
                    nc.vector.tensor_tensor_reduce(out=v, in0=qk_ps[h % 2][:, qt], in1=v, scale=-1.0, scalar=ROW_MAX_NEG,
                                                   op0=ALU.add, op1=ALU.min, accum_out=nmax[:, b.par, h, qt:qt + 1]).then_inc(s_reduced, 1)

            def copy_pT(b, h):
                dve.wait_ge(s_tp, H * b.n + h + 1)
                free_pT(dve, b, h)
                nc.vector.tensor_copy(pT[:, h % (2 * HG)], tp_ps[h % 2]).then_inc(s_ptd, 1)

            def xT_out(b):
                dve.wait_ge(s_xtp, b.n + 1)
                for c in range(DC):
                    ins = nc.vector.tensor_scalar(xT[:, c], prep_b[:, c], adaS[:, c, bass.ds(b.n, 1)], adaB[:, c, bass.ds(b.n, 1)], ALU.mult, ALU.add)
                ins.then_inc(s_xT, 1)

            def rest1(b, t):
                ps = prep_b if t == 0 else prep_a
                dve.wait_ge(s_p1, 2 * b.n + t + 1)
                for c in range(DC):
                    ins = nc.vector.scalar_tensor_tensor(ps[:, c], ps[:, c], bqk[:, t, c:c + 1], parts[:, t, 0, c], ALU.add, ALU.subtract)
                ins.then_inc(s_r1, 1)

            def rest2(b, t):
                ps = prep_b if t == 0 else prep_a
                dve.wait_ge(s_p2, 2 * b.n + t + 1)
                nc.vector.tensor_tensor(parts[:, t, 2], ps, parts[:, t, 1], ALU.subtract).then_inc(s_p3, 1)

            def v_out(b):
                dve.wait_ge(s_vp, b.n + 1)
                for t in range(QT):
                    ins = nc.vector.tensor_tensor(vt[:, b.par, t, :, 0:HD], prep_b[:, t].rearrange("p (h d) -> p h d", d=HD),
                                                  bvb[:].rearrange("p (h d) -> p h d", d=HD), ALU.add)
                ins.then_inc(s_v, 1)

            def xres_out(b):
                dve.wait_ge(s_xb, b.n + 1)
                if b.i is not None or b.off >= 2:
                    dve.wait_ge(s_x2, b.n - 1)
                nc.vector.tensor_tensor(xres[:, b.par], prep_a, bob[:].unsqueeze(1).to_broadcast([P, QT, D]), ALU.add).then_inc(s_xres, 1)

            def normalise_ctx(b, qt):
                dve.wait_ge(s_cn, 2 * b.n + qt + 1)
                heads = bank[7][:].rearrange("p (h w) -> p h w", w=VW)
                nc.vector.reciprocal(rec[:, qt].unsqueeze(2), heads[:, :, HD:HD + 1]).then_inc(s_rec, 1)
                dve.wait_ge(s_rec, 2 * b.n + qt + 1)
                nc.vector.tensor_tensor(ctxn[:, qt].rearrange("p (h d) -> p h d", d=HD), heads[:, :, 0:HD],
                                        rec[:, qt].unsqueeze(2).to_broadcast([P, H, HD]), ALU.mult).then_inc(s_ctxn, 1)

            def x2_out(b):
                dve.wait_ge(s_o, b.n + 1)
                if b.i is not None or b.off >= 2:
                    dve.wait_ge(s_x2st[b.par], 16 * b.half)
                dve.wait_ge(s_xres, b.n + 1)
                nc.vector.tensor_tensor(x2s[:, b.par], tail_ps, xres[:, b.par], ALU.add).then_inc(s_x2, 1)

            def prep_all(b):
                xT_out(b)
                rest1(b, 0)
                rest2(b, 0)
                rest1(b, 1)
                rest2(b, 1)
                v_out(b)
                xres_out(b)

            prep_all(Batch(0))
            xT_out(Batch(1))
            dve.wait_ge(s_const, 1)

            def constants2():
                dve.wait_ge(s_load, 16 * len(loads_rest))
                nc.vector.tensor_scalar(w2[:], w2[:], 0.5, None, ALU.mult)
                nc.vector.tensor_scalar(b1t[:], b1c[:], 0.5 * GELU_A, None, ALU.mult)
                nc.vector.tensor_scalar(gb2h[:], gb2[:], 0.5, None, ALU.mult)
                nc.vector.tensor_tensor(cb[:], cb[:], cb2[:], ALU.add)

            def stats2(b):
                dve.wait_ge(s_y[b.par], 16 * b.half + 16)
                if b.i is not None or b.off >= 1:
                    dve.wait_ge(s2_stats, b.n)
                for t in range(QT):
                    ins = nc.vector.bn_stats(st6b[:, t], y2[:, b.par, t])
                ins.then_inc(s2_six, 1)
                dve.wait_ge(s2_six, b.n + 1)
                if b.i is not None or b.off >= 2:
                    dve.wait_ge(s2_rstd, b.n - 1)
                dve.nop(nofuse=True)
                dve.nop(nofuse=True)
                for t in range(QT):
                    ins = nc.vector.bn_aggr(mvb[:, b.par, t], st6b[:, t])
                ins.then_inc(s2_stats, 1)

            def split_weights(i):
                w, (high, rest) = ((w1, w1s), (w2, w2s))[i]
                dve.wait_ge(s2_w, i + 1)
                nc.vector.tensor_tensor(rest, w[:], f32(high), ALU.subtract).then_inc(s2_wl, 1)

            def body(b, n):
                main = n is None or n < B
                prep = n is None or n + 1 < B
                ahead = n is None or n + 2 < B
                tail = n is None or n >= 1
                for h in range(H):
                    if main:
                        reduce_head(b, h)
                    at = behind(b, n, h, 4)
                    if at and at[1] in DVE_HEADS:
                        copy_pT(*at)
                    if h == 0:
                        if main:
                            gs_column(b.n, n == 0)
                        if ahead:
                            stats(b.plus(2))
                    if h == 2 and ahead:
                        stats_end(b.plus(2))
                    if h == 4:
                        if prep:
                            rest1(b.plus(1), 0)
                        if main:
                            gs_products(b.n)
                    if h == 6 and prep:
                        rest2(b.plus(1), 0)
                    if h == 7 and prep:
                        rest1(b.plus(1), 1)
                    if h == 8:
                        if tail:
                            normalise_ctx(b.plus(-1), 0)
                        if prep:
                            rest2(b.plus(1), 1)
                    if h == 10:
                        if prep:
                            v_out(b.plus(1))
                        if tail:
                            normalise_ctx(b.plus(-1), 1)
                    if h == 11 and main:
                        gs_reciprocal(b.n)
                    if h == 11 and n == B - 2:
                        constants2()
                    if h == 12:
                        if ahead:
                            xT_out(b.plus(2))
                        if main:
                            gs_coefficients(b.n)
                    if h == 14 and main:
                        gs_update(b.n)
                    if h == 15:
                        if tail:
                            x2_out(b.plus(-1))
                        if prep:
                            xres_out(b.plus(1))
                        if main:
                            gs_write(b.n)
                    if n == B and h in (4, 6, 9):
                        response_matrix((4, 6, 9).index(h))
                    if n == B and h == 5:
                        stats2(Batch(1))
                    if n == B and h == 11:
                        split_weights(0)

            run_batches(dve, 0, 3, B - 3, B, body)
            stats2(Batch(0))
            body(Batch(B), B)

            def hT_rest(b):
                dve.wait_ge(s2_hT, b.n + 1)
                if b.i is not None or b.off >= 2:
                    dve.wait_ge(s2_up, 4 * (b.n - 1))
                nc.vector.tensor_tensor(hTs[1][:, b.par], hT, f32(hTs[0][:, b.par]), ALU.subtract).then_inc(s2_hl, 1)

            def gate_pair(b, j):
                dve.wait_ge(s2_th, 4 * b.n + j + 1)
                if j in U_ACT:
                    dve.wait_ge(s2_ua, u_done(True, b, j))
                else:
                    if b.i is not None or b.off >= 1:
                        dve.wait_ge(s2_g, 4 * (b.n - 1) + j + 1)
                    for f in range(2):
                        ins = nc.vector.tensor_scalar(up[:, j, f], tiles2(j)[:, f], b1c[:, 2 * j + f:2 * j + f + 1], None, ALU.add)
                    ins.then_inc(s2_u, 1)
                    dve.wait_ge(s2_u, u_done(False, b, j))
                if b.i is not None or b.off >= 1:
                    dve.wait_ge(s2_gl, 4 * (b.n - 1) + j + 1)
                nc.vector.scalar_tensor_tensor(gT[:, 2 * j:2 * j + 2], th[:, j], 1.0, up[:, j], ALU.add, ALU.mult).then_inc(s2_g, 1)

            def gT_rest(b, j):
                dve.wait_ge(s2_gh, 4 * b.n + j + 1)
                if b.i is not None or b.off >= 2:
                    dve.wait_ge(s2_dn, b.n - 1)
                pair = slice(2 * j, 2 * j + 2)
                nc.vector.tensor_tensor(gTs[1][:, b.par, pair], gT[:, pair], f32(gTs[0][:, b.par, pair]), ALU.subtract).then_inc(s2_gl, 1)

            def hid_out(b):
                dve.wait_ge(s2_dn, b.n + 1)
                dve.wait_ge(s2_yb, b.n + 1)
                if b.i is not None or b.off >= 2:
                    dve.wait_ge(s2_fin, b.n - 1)
                nc.vector.tensor_tensor(hid[:, b.par], tiles2(4), yb[:, b.par], ALU.add).then_inc(s2_hid, 1)

            def strength(b):
                dve.wait_ge(s2_z, b.n + 1)
                if b.i is not None or b.off >= 1:
                    dve.wait_ge(s2_fin, b.n)
                nc.vector.tensor_scalar(strg[:, b.par:b.par + 1], gth[:], 1.0, modh[:, bass.ds(b.n, 1)], ALU.add, ALU.mult).then_inc(s2_str, 1)

            def hidT_rest(b):
                dve.wait_ge(s2_hidT, b.n + 1)
                if b.i is not None or b.off >= 1:
                    dve.wait_ge(s2_r, b.n)
                nc.vector.tensor_tensor(hidTs[1], hidT, f32(hidTs[0]), ALU.subtract).then_inc(s2_hidl, 1)

            def rsp_out(b):
                dve.wait_ge(s2_r, b.n + 1)
                if b.i is not None or b.off >= 1:
                    dve.wait_ge(s2_fin, b.n)
                nc.vector.tensor_tensor(rsp[:], tiles2(7), cb[:].unsqueeze(1).to_broadcast([P, QT, D]), ALU.add).then_inc(s2_rs, 1)

            def fin_out(b):
                dve.wait_ge(s2_hid, b.n + 1)
                dve.wait_ge(s2_rs, b.n + 1)
                dve.wait_ge(s2_str, b.n + 1)
                if b.i is not None or b.off >= 2:
                    dve.wait_ge(s_out[b.par], 16 * b.half)
                nc.vector.scalar_tensor_tensor(fin[:, b.par], rsp[:], strg[:, b.par:b.par + 1], hid[:, b.par], ALU.mult, ALU.add).then_inc(s2_fin, 1)

            hT_rest(Batch(0))
            split_weights(1)
            dve.wait_ge(s2_m, 1)
            nc.vector.tensor_tensor(resp_ms[1], resp_m[:], f32(resp_ms[0]), ALU.subtract).then_inc(s2_ml, 1)

            def body2(b, n):
                main = n is None or n < B
                tail = n is None or 1 <= n <= B
                tail2 = n is None or n >= 2
                if main:
                    gate_pair(b, 0)
                if tail:
                    gT_rest(b.plus(-1), 3)
                if tail2:
                    hidT_rest(b.plus(-2))
                if n is None or n + 2 < B:
                    stats2(b.plus(2))
                if main:
                    gate_pair(b, 1)
                    gT_rest(b, 0)
                    if n is None or n + 1 < B:
                        hT_rest(b.plus(1))
                if tail2:
                    rsp_out(b.plus(-2))
                if main:
                    gate_pair(b, 2)
                    gT_rest(b, 1)
                if tail:
                    hid_out(b.plus(-1))
                if tail2:
                    strength(b.plus(-2))
                    fin_out(b.plus(-2))
                if main:
                    gate_pair(b, 3)
                    gT_rest(b, 2)

            run_batches(dve, 0, 3, B - 3, B + 2, body2)

        @block.scalar
        def _(act):
            act.wait_ge(s_red, 1)
            nc.scalar.activation(sc[:], red[:], ACT.Sin).then_inc(s_act0, 1)
            act.wait_ge(s_act0, 1)
            nc.scalar.activation(modt[:], scr[:], ACT.Tanh, scale=0.5)
            nc.scalar.activation(sct[:], sc[:], ACT.Tanh, scale=0.5).then_inc(s_sin, 1)

            def exp_head(b, h):
                slot = 2 * b.par + h // CH
                for qt in range(QT):
                    v = ring[:, slot, qt, h % CH]
                    act.wait_ge(s_reduced, 2 * H * b.n + 2 * h + qt + 1)
                    nc.scalar.activation(v, v, ACT.Exp, bias=nmax[:, b.par, h, qt:qt + 1], scale=-1.0).then_inc(s_exp, 1)

            def copy_pT(b, h):
                act.wait_ge(s_tp, H * b.n + h + 1)
                free_pT(act, b, h)
                nc.scalar.activation(pT[:, h % (2 * HG)], tp_ps[h % 2], ACT.Copy).then_inc(s_pta, 1)

            def part1(b, t):
                ps = prep_b if t == 0 else prep_a
                act.wait_ge(s_qp if t == 0 else s_kp, b.n + 1)
                if b.i is not None or b.off >= 1:
                    act.wait_ge(s_wq_d if t == 0 else s_wk_d, 16 * b.n)
                for c in range(DC):
                    ins = nc.scalar.activation(parts[:, t, 0, c], ps[:, c], ACT.Identity, bias=bqk[:, t, c:c + 1])
                ins.then_inc(s_p1, 1)

            def part2(b, t):
                ps = prep_b if t == 0 else prep_a
                act.wait_ge(s_r1, 2 * b.n + t + 1)
                nc.scalar.activation(parts[:, t, 1], ps, ACT.Copy).then_inc(s_p2, 1)

            def pv_out(b, g):
                act.wait_ge(s_pv, NG * b.n + g + 1)
                if g == 0 and (b.i is not None or b.off >= 1):
                    act.wait_ge(s_cn, 2 * b.n)
                nc.scalar.activation(pv_sb[:, g], pv_ps, ACT.Copy).then_inc(s_pvc, 1)

            def ctxT_out(b):
                act.wait_ge(s_cT, b.n + 1)
                nc.scalar.activation(ctxT[:], tail_ps, ACT.Copy).then_inc(s_ctxT, 1)

            def prep_parts(b):
                for t in range(2):
                    part1(b, t)
                    part2(b, t)

            act.wait_ge(s_setup, 1)
            prep_parts(Batch(0))

            def yn_out(b):
                act.wait_ge(s2_rstd, b.n + 1)
                act.wait_ge(s_y[b.par], 16 * b.half + 16)
                if b.i is not None or b.off >= 1:
                    act.wait_ge(s2_yt, b.n)
                for t in range(QT):
                    ins = nc.scalar.activation(yn[:, t], y2[:, b.par, t], ACT.Identity, bias=nmrb[:, t:t + 1], scale=rstdb[:, t:t + 1])
                ins.then_inc(s2_yn, 1)

            def split_weights(i):
                act.wait_ge(s_tp, H * B)
                act.wait_ge(s_pv, NG * B)
                w, high = ((w1, w1s[0]), (w2, w2s[0]))[i]
                nc.scalar.activation(high, w[:], ACT.Copy).then_inc(s2_w, 1)

            def body(b, n):
                prep = n is None or n + 1 < B
                tail = n is None or n >= 1
                for h in range(H):
                    at = behind(b, n, h, 1)
                    if at:
                        exp_head(*at)
                    at = behind(b, n, h, 4)
                    if at and at[1] in ACT_HEADS:
                        copy_pT(*at)
                    at = behind(b, n, h, 10)
                    if at and at[1] % HG == 0:
                        pv_out(at[0], at[1] // HG)
                    if prep:
                        if h == 2:
                            part1(b.plus(1), 0)
                        if h == 5:
                            part2(b.plus(1), 0)
                        if h == 6:
                            part1(b.plus(1), 1)
                        if h == 7:
                            part2(b.plus(1), 1)
                    if n == B and h == 7:
                        yn_out(Batch(0))
                    if n == B and h == 10:
                        split_weights(0)
                    if h == 12 and tail:
                        ctxT_out(b.plus(-1))

            run_batches(act, 0, 3, B - 3, B + 1, body)
            last = Batch(B - 1)

            def hT_out(b):
                act.wait_ge(s2_yt, b.n + 1)
                if b.i is not None or b.off >= 1:
                    act.wait_ge(s2_hl, b.n)
                for c in range(DC):
                    ins = nc.scalar.activation(hT[:, c], tiles2(5)[:, c], ACT.Identity, bias=be2c[:, c:c + 1], scale=g2c[:, c:c + 1])
                ins.then_inc(s2_hf, 1)
                act.wait_ge(s2_hf, b.n + 1)
                if b.i is not None or b.off >= 2:
                    act.wait_ge(s2_up, 4 * (b.n - 1))
                nc.scalar.activation(hTs[0][:, b.par], hT, ACT.Copy).then_inc(s2_hT, 1)

            def tanh_pair(b, j):
                act.wait_ge(s2_up, 4 * b.n + j + 1)
                if b.i is not None or b.off >= 1:
                    act.wait_ge(s2_g, 4 * (b.n - 1) + j + 1)
                for f in range(2):
                    ins = nc.scalar.activation(th[:, j, f], tiles2(j)[:, f], ACT.Tanh, bias=b1t[:, 2 * j + f:2 * j + f + 1], scale=0.5 * GELU_A)
                ins.then_inc(s2_th, 1)
                if j in U_ACT:
                    for f in range(2):
                        ins = nc.scalar.activation(up[:, j, f], tiles2(j)[:, f], ACT.Identity, bias=b1c[:, 2 * j + f:2 * j + f + 1])
                    ins.then_inc(s2_ua, 1)

            def gT_high(b, j):
                act.wait_ge(s2_g, 4 * b.n + j + 1)
                if b.i is not None or b.off >= 2:
                    act.wait_ge(s2_dn, b.n - 1)
                pair = slice(2 * j, 2 * j + 2)
                nc.scalar.activation(gTs[0][:, b.par, pair], gT[:, pair], ACT.Copy).then_inc(s2_gh, 1)

            def hidT_out(b):
                act.wait_ge(s2_hidp, b.n + 1)
                if b.i is not None or b.off >= 1:
                    act.wait_ge(s2_r, b.n)
                    act.wait_ge(s2_h1p, b.n)
                    act.wait_ge(s2_hidl, b.n)
                for c in range(DC):
                    ins = nc.scalar.activation(hidT[:, c], tiles2(6)[:, c], ACT.Copy, accum_out=pooled[:, c:c + 1])
                ins.then_inc(s2_hidf, 1)
                act.wait_ge(s2_hidf, b.n + 1)
                nc.scalar.activation(hidTs[0], hidT, ACT.Copy).then_inc(s2_hidT, 1)

            def gate1(b):
                act.wait_ge(s2_h1p, b.n + 1)
                nc.scalar.activation(h1[:], bank[6][0:GW, 0:1], ACT.Relu, bias=gb1[:], scale=1.0 / S).then_inc(s2_h1, 1)

            def gate2(b):
                act.wait_ge(s2_zp, b.n + 1)
                if b.i is not None or b.off >= 1:
                    act.wait_ge(s2_str, b.n)
                nc.scalar.activation(gth[:], bank[6][:, 8:9], ACT.Tanh, bias=gb2h[:], scale=0.5).then_inc(s2_z, 1)

            hT_out(Batch(0))
            split_weights(1)
            act.wait_ge(s_rmc, 3)
            act.wait_ge(s_x2, B)
            nc.scalar.activation(resp_ms[0], resp_m[:], ACT.Copy).then_inc(s2_m, 1)
            yn_out(Batch(1))

            def body2(b, n):
                main = n is None or n < B
                tail = n is None or 1 <= n <= B
                tail2 = n is None or n >= 2
                if main:
                    tanh_pair(b, 0)
                if tail:
                    gT_high(b.plus(-1), 3)
                if main:
                    tanh_pair(b, 1)
                    gT_high(b, 0)
                if tail2:
                    gate1(b.plus(-2))
                if main:
                    if n is None or n + 1 < B:
                        hT_out(b.plus(1))
                    tanh_pair(b, 2)
                    gT_high(b, 1)
                    if n is None or n + 2 < B:
                        yn_out(b.plus(2))
                if tail2:
                    gate2(b.plus(-2))
                if main:
                    tanh_pair(b, 3)
                    gT_high(b, 2)
                if tail:
                    hidT_out(b.plus(-1))

            run_batches(act, 0, 3, B - 3, B + 2, body2)

        @block.tensor
        def _(pe):
            mm = nc.tensor.matmul
            pe.wait_ge(s_emb, 1)
            for n in range(2 * DC):
                for c in range(2):
                    ins = mm(bank[7][:, n * B:(n + 1) * B], wada[:, c, n * P:(n + 1) * P], emb[:, c], start=(c == 0), stop=(c == 1))
            ins.then_inc(s_adaps, 1)

            def gs_gram(b, n):
                i = b.n
                pe.wait_ge(s_gcol, i + 1)
                if n is None or n >= 1:
                    pe.wait_ge(s_gself, 4 * i)
                if n is None or n >= 2:
                    pe.wait_ge(s_x2, i - 1)
                for a in range(2):
                    for c in range(DC):
                        ins = mm(gs_ps[:, a * R:(a + 1) * R], ucol[:, a, c:c + 1].to_broadcast([P, P]), uv[:, a, c], start=(c == 0), stop=(c == DC - 1))
                ins.then_inc(s_gram, 1)

            def response_matrix(step):
                if step == 0:
                    pe.wait_ge(s_gself, 4 * R)
                    pe.wait_ge(s_reduced, 2 * H * B)
                    pe.wait_ge(s_xres, B)
                    for c in range(DC):
                        mm(bank[0][0:R, 0:R], uv[:, 1, c], uv[:, 1, c], start=(c == 0), stop=(c == DC - 1))
                    mm(bank[1][0:R, 0:D], uv[0:R, 0, 0], respT[:], start=True, stop=True)
                    for c in range(DC):
                        ins = nc.tensor.transpose(bank[5][0:R, c * P:(c + 1) * P], uv[:, 0, c], ident[:])
                if step == 1:
                    pe.wait_ge(s_v, B)
                    pe.wait_ge(s_rmc, 1)
                    ins = mm(bank[6][0:R, 0:D], gram[:], t1[:], start=True, stop=True)
                if step == 2:
                    pe.wait_ge(s_rmc, 2)
                    for c in range(DC):
                        ins = mm(bank[1][:, c * D:(c + 1) * D], uoT[:, c * P:(c + 1) * P], t2[:], start=True, stop=True)
                ins.then_inc(s_rm, 1)

            pe.wait_ge(s_setup, 1)

            def scores(b, h):
                if b.i is not None or H * b.off + h >= 2:
                    pe.wait_ge(s_reduced, 2 * (H * b.n + h - 1))
                if h == 0:
                    pe.wait_ge(s_stq[b.par], 16 * len(RUNS[0]) * (b.half + 1))
                    pe.wait_ge(s_stk[b.par], 16 * len(RUNS[0]) * (b.half + 1))
                at = h % (H // DC) * DC + h // (H // DC)
                for qt in range(QT):
                    ins = mm(qk_ps[h % 2][:, qt], stack[:, b.par, 0, at, qt * P:(qt + 1) * P], stack[:, b.par, 1, at, :], start=True, stop=True)
                ins.then_inc(s_qk, 1)

            def transposes(b, h):
                slot = 2 * b.par + h // CH
                if b.i is not None or H * b.off + h >= 2:
                    last, bb = (h - 2, b) if h >= 2 else (h - 2 + H, b.plus(-1))
                    if last in ACT_HEADS:
                        pe.wait_ge(s_pta, copied(ACT_HEADS, bb, last))
                    else:
                        pe.wait_ge(s_ptd, copied(DVE_HEADS, bb, last))
                for qt in range(QT):
                    pe.wait_ge(s_exp, 2 * H * b.n + 2 * h + qt + 1)
                    for kt in range(QT):
                        ins = nc.tensor.transpose(tp_ps[h % 2][:, kt, qt * P:(qt + 1) * P], ring[:, slot, qt, h % CH, kt * P:(kt + 1) * P], ident[:])
                ins.then_inc(s_tp, 1)

            def pv(b, g, kt):
                if kt == 0:
                    pv_waits(b, g)
                for j in range(HG):
                    h = HG * g + j
                    ins = mm(pv_ps[VW * j:VW * (j + 1), :], vt[:, b.par, kt, h], pT[:, h % (2 * HG), kt], start=(kt == 0), stop=(kt == QT - 1))
                if kt == QT - 1:
                    ins.then_inc(s_pv, 1)

            def pv_waits(b, g):
                pe.wait_ge(s_pta, copied(ACT_HEADS, b, HG * g + HG - 1))
                pe.wait_ge(s_ptd, copied(DVE_HEADS, b, HG * g + HG - 1))
                if g == 0:
                    pe.wait_ge(s_v, b.n + 1)
                if b.i is not None or NG * b.off + g >= 1:
                    pe.wait_ge(s_pvc, NG * b.n + g)

            def x_transpose(b):
                pe.wait_ge(s_xn, b.n + 1)
                if b.i is not None or b.off >= 1:
                    pe.wait_ge(s_v, b.n)
                for c in range(DC):
                    for t in range(QT):
                        ins = nc.tensor.transpose(prep_b[:, c, t * P:(t + 1) * P], xn[:, t, c * P:(c + 1) * P], ident[:])
                ins.then_inc(s_xtp, 1)

            def project_qk(b, t, n):
                w, ps = (wq, prep_b) if t == 0 else (wk, prep_a)
                pe.wait_ge(s_xT, b.n + 1)
                if t == 1 and (b.i is not None or b.off >= 1):
                    pe.wait_ge(s_xres, b.n)
                for c in range(DC):
                    ins = mm(ps[:, n], w[:, c, n * P:(n + 1) * P], xT[:, c], start=(c == 0), stop=(c == DC - 1))
                if n == DC - 1:
                    ins.then_inc(s_qp if t == 0 else s_kp, 1)

            def project_v(b, t):
                pe.wait_ge(s_p3, 2 * b.n + 1)
                for c in range(DC):
                    ins = mm(prep_b[:, t], xT[:, c, t * P:(t + 1) * P], wv[:, c], start=(c == 0), stop=(c == DC - 1))
                if t == QT - 1:
                    ins.then_inc(s_vp, 1)

            def x_back(b):
                pe.wait_ge(s_p3, 2 * b.n + 2)
                for t in range(QT):
                    for c in range(DC):
                        ins = nc.tensor.transpose(prep_a[:, t, c * P:(c + 1) * P], xT[:, c, t * P:(t + 1) * P], ident[:])
                ins.then_inc(s_xb, 1)

            def ctx_natural(b, qt):
                pe.wait_ge(s_pvc, NG * b.n + NG)
                if qt == 0:
                    if b.i is not None or b.off >= 1:
                        pe.wait_ge(s_x2, b.n)
                    if b.i is not None or b.off + 1 < B:
                        pe.wait_ge(s_gii, b.n + 2)
                else:
                    pe.wait_ge(s_ctxn, 2 * b.n + 1)
                for g in range(NG):
                    ins = nc.tensor.transpose(bank[7][:, g * P:(g + 1) * P], pv_sb[:, g, qt * P:(qt + 1) * P], ident[:])
                ins.then_inc(s_cn, 1)

            def ctx_transpose(b):
                pe.wait_ge(s_ctxn, 2 * b.n + 2)
                for c in range(DC):
                    for t in range(QT):
                        ins = nc.tensor.transpose(tail_ps[:, c, t * P:(t + 1) * P], ctxn[:, t, c * P:(c + 1) * P], ident[:])
                ins.then_inc(s_cT, 1)

            def project_o(b, t):
                pe.wait_ge(s_ctxT, b.n + 1)
                for c in range(DC):
                    ins = mm(tail_ps[:, t], ctxT[:, c, t * P:(t + 1) * P], wo[:, c], start=(c == 0), stop=(c == DC - 1))
                if t == QT - 1:
                    ins.then_inc(s_o, 1)

            first = Batch(0)
            x_transpose(first)
            for t in range(2):
                for n in range(DC):
                    project_qk(first, t, n)
            for t in range(QT):
                project_v(first, t)
            x_back(first)
            x_transpose(Batch(1))
            scores(first, 0)

            def y_transpose(b):
                pe.wait_ge(s2_yn, b.n + 1)
                if b.i is None and b.off == 0:
                    pe.wait_ge(s_rmc, 1)
                if b.i is not None or b.off >= 1:
                    pe.wait_ge(s2_hf, b.n)
                for c in range(DC):
                    for t in range(QT):
                        ins = nc.tensor.transpose(tiles2(5)[:, c, t * P:(t + 1) * P], yn[:, t, c * P:(c + 1) * P], ident[:])
                ins.then_inc(s2_yt, 1)

            def body(b, n):
                main = n is None or n < B
                prep = n is None or n + 1 < B
                tail = n is None or n >= 1
                for h in range(H):
                    if main and h + 1 < H:
                        scores(b, h + 1)
                    elif prep:
                        scores(b.plus(1), 0)
                    at = behind(b, n, h, 3)
                    if at:
                        transposes(*at)
                    for kt, k in ((0, 8), (1, 9)):
                        at = behind(b, n, h, k)
                        if at and at[1] % HG == 0:
                            pv(at[0], at[1] // HG, kt)
                    if prep:
                        if h in (0, 1):
                            project_qk(b.plus(1), 0, h)
                        if h in (3, 4):
                            project_qk(b.plus(1), 1, h - 3)
                        if h == 10:
                            x_back(b.plus(1))
                    if h == 11 and (n is None or n + 2 < B):
                        x_transpose(b.plus(2))
                    if h == 2 and main:
                        gs_gram(b, n)
                    if tail:
                        if h == 7:
                            ctx_natural(b.plus(-1), 0)
                        if h == 9:
                            ctx_natural(b.plus(-1), 1)
                        if h == 11:
                            ctx_transpose(b.plus(-1))
                        if n == B and h == 12:
                            y_transpose(Batch(0))
                        if h in (13, 14):
                            project_o(b.plus(-1), h - 13)
                    if n == B and h in (3, 6, 8):
                        response_matrix((3, 6, 8).index(h))
                    if prep and h in (7, 8):
                        project_v(b.plus(1), h - 7)

            run_batches(pe, 0, 3, B - 3, B + 1, body)
            last = Batch(B - 1)

            pe.wait_ge(s_x2, B)
            pe.wait_ge(s_rmc, 3)

            def up_pair(b, j):
                if j == 0:
                    pe.wait_ge(s2_hl, b.n + 1)
                    if b.i is None and b.off == 0:
                        pe.wait_ge(s2_wl, 1)
                if b.i is not None or b.off >= 1:
                    if j in U_ACT:
                        pe.wait_ge(s2_ua, u_done(True, b.plus(-1), j))
                    else:
                        pe.wait_ge(s2_u, u_done(False, b.plus(-1), j))
                for f in range(2):
                    n = 2 * j + f
                    for c in range(DC):
                        for k, (kw, kx) in enumerate(HI_LO):
                            ins = mm(tiles2(j)[:, f], w1s[kw][:, c, n * P:(n + 1) * P], hTs[kx][:, b.par, c],
                                     start=(c == 0 and k == 0), stop=(c == DC - 1 and k == len(HI_LO) - 1))
                ins.then_inc(s2_up, 1)

            def down(b, t):
                if t == 0 and (b.i is not None or b.off >= 1):
                    pe.wait_ge(s2_hid, b.n)
                elif t == 0:
                    pe.wait_ge(s2_wl, 2)
                for f in range(FC):
                    if t == 0 and f % 2 == 0:
                        pe.wait_ge(s2_gl, 4 * b.n + f // 2 + 1)
                    for k, (kx, kw) in enumerate(HI_LO):
                        ins = mm(tiles2(4)[:, t], gTs[kx][:, b.par, f, t * P:(t + 1) * P], w2s[kw][:, f],
                                 start=(f == 0 and k == 0), stop=(f == FC - 1 and k == len(HI_LO) - 1))
                if t == QT - 1:
                    ins.then_inc(s2_dn, 1)

            def hid_transpose(b):
                pe.wait_ge(s2_hid, b.n + 1)
                if b.i is not None or b.off >= 1:
                    pe.wait_ge(s2_z, b.n)
                for c in range(DC):
                    for t in range(QT):
                        ins = nc.tensor.transpose(tiles2(6)[:, c, t * P:(t + 1) * P], hid[:, b.par, t, c * P:(c + 1) * P], ident[:])
                ins.then_inc(s2_hidp, 1)

            def gate_h1(b):
                pe.wait_ge(s2_hidf, b.n + 1)
                for c in range(DC):
                    ins = mm(bank[6][0:GW, 0:1], gw1[:, c], pooled[:, c:c + 1], start=(c == 0), stop=(c == DC - 1))
                ins.then_inc(s2_h1p, 1)

            def gate_z(b):
                pe.wait_ge(s2_h1, b.n + 1)
                mm(bank[6][:, 8:9], h1[:].to_broadcast([GW, P]), gw2[:], start=True, stop=True).then_inc(s2_zp, 1)

            def response(b):
                pe.wait_ge(s2_hidl, b.n + 1)
                if b.i is not None or b.off >= 1:
                    pe.wait_ge(s2_rs, b.n)
                else:
                    pe.wait_ge(s2_ml, 1)
                for t in range(QT):
                    for c in range(DC):
                        for k, (kx, kw) in enumerate(HI_LO):
                            ins = mm(tiles2(7)[:, t], hidTs[kx][:, c, t * P:(t + 1) * P], resp_ms[kw][:, c],
                                     start=(c == 0 and k == 0), stop=(c == DC - 1 and k == len(HI_LO) - 1))
                ins.then_inc(s2_r, 1)

            def body2(b, n):
                main = n is None or n < B
                tail = n is None or 1 <= n <= B
                tail2 = n is None or n >= 2
                if main:
                    up_pair(b, 0)
                    if n is None or n + 1 < B:
                        y_transpose(b.plus(1))
                if main:
                    up_pair(b, 1)
                if tail2:
                    gate_h1(b.plus(-2))
                if tail:
                    down(b.plus(-1), 0)
                if tail2:
                    response(b.plus(-2))
                if main:
                    up_pair(b, 2)
                if tail:
                    down(b.plus(-1), 1)
                if tail2:
                    gate_z(b.plus(-2))
                if main:
                    up_pair(b, 3)
                if tail:
                    hid_transpose(b.plus(-1))

            run_batches(pe, 0, 3, B - 3, B + 2, body2)


_NAMES = ['W_ada', 'b_ada', 'Wq', 'bq', 'Wk', 'bk', 'Wv', 'bv', 'Wo', 'bo', 'W1', 'b1', 'W2', 'b2', 'g2', 'beta2']


def kernel(**inputs):
    import concourse.bacc as _bacc
    from concourse.bass_utils import run_bass_kernel_spmd as _run

    a = {k: np.asarray(v) for k, v in inputs.items()}
    feeds = {
        "x": a["x"], "itok": a["itok_B_34_63"], "fside": a["fside_Bx16xSxS_0"], "score": a["condB_safetyscore"],
        "mask": a["mask_Bx1xSxS_bk0"],
    }
    feeds.update({n: a["L0_cond_" + n] for n in _NAMES})
    for n in ('Wq', 'bq', 'Wk', 'bk'):
        w = feeds[n]
        feeds[n] = w.reshape(-1, DC, P // HD, HD).transpose(0, 1, 3, 2).reshape(w.shape)
    feeds.update({n: feeds[n].reshape(-1, P).T for n in ('b_ada', 'bq', 'bk', 'b1', 'g2', 'beta2')})
    feeds.update({
        "U": a["L1_cond_U"], "V": a["L1_cond_V"], "safety_bias": a["L1_cond_safety_bias"],
        "gate_w1T": a["L1_cond_gate_w1"].T, "gate_b1": a["L1_cond_gate_b1"], "gate_w2T": a["L1_cond_gate_w2"].T,
        "gate_b2": a["L1_cond_gate_b2"], "resp_wT": a["L1_cond_resp_w"].T, "resp_b": a["L1_cond_resp_b"],
        "freqs": np.exp(np.arange(D // 2, dtype=np.float32) * np.float32(-np.log(10000.0) / (D // 2 - 1))).astype(np.float32),
    })
    nc = _bacc.Bacc("TRN2", target_bir_lowering=False, num_devices=1)
    arrays, aps = {}, {}
    for name, v in feeds.items():
        v = np.ascontiguousarray(v)
        arrays["in_" + name] = v
        aps[name] = nc.dram_tensor("in_" + name, v.shape, mybir.dt.from_np(v.dtype), kind="ExternalInput").ap()
    aps["out"] = nc.dram_tensor("out_0", (B, S, D), F32, kind="ExternalOutput").ap()
    attention_block_kernel(nc, **aps)
    r = _run(nc, [arrays], core_ids=[0])
    return r.results[0]["out_0"]
```
